# Optimizing a Trainium2 kernel written in Bass

```python
import numpy as np
import jax
import jax.numpy as jnp

def _softmax(x, axis=-1):
    return jax.nn.softmax(x, axis=axis)

def _gelu(x):
    return jax.nn.gelu(x, approximate=True)

def _silu(x):
    return jax.nn.silu(x)

def _sigmoid(x):
    return jax.nn.sigmoid(x)

def _layernorm(x, axis=-1, eps=1e-05):
    m = jnp.mean(x, axis=axis, keepdims=True)
    v = jnp.var(x, axis=axis, keepdims=True)
    return (x - m) / jnp.sqrt(v + eps)

def _scatter_add(tgt, idx, src, axis=0):
    return tgt.at[idx].add(src)

def _segment_sum(src, seg, n):
    return jax.ops.segment_sum(src, seg, n)
kernel_name = 'mk_adaln_ffn_d2_seqx_r4_0467bf'

def setup_inputs(seed: int=0):
    np.random.seed(seed)
    _w = jnp.asarray

    def _rec_inputs():
        import jax
        import jax.numpy as jnp
        _rk = jax.random.key(seed)
        x = -0.000125 + 0.9999 * jax.random.normal(jax.random.fold_in(_rk, 1), (16, 256, 256), jnp.float32)
        _lenS = 256 - jax.random.randint(jax.random.fold_in(_rk, 7), (16,), 0, max(1, 256 // 4) + 1, jnp.int32)
        _lenS2 = 256 - jax.random.randint(jax.random.fold_in(_rk, 8), (16,), 0, max(1, 256 // 4) + 1, jnp.int32)
        cond_1024 = -0.00495105 + 0.998799 * jax.random.normal(jax.random.fold_in(_rk, 11), (16, 256), jnp.float32)
        return (x, cond_1024)
    x, cond_1024 = _rec_inputs()

    def _L0_cond_setup():
        import jax, jax.numpy as jnp
        import numpy as np
        B, L, D_IN, D = (64, 128, 256, 256)
        key = jax.random.key(seed)
        k1, k2, k3, k4, k5 = jax.random.split(key, 5)
        x = jax.random.normal(k1, (B, L, D_IN), dtype=jnp.float32)
        Wk = jax.random.normal(k2, (D_IN, 3 * D), dtype=jnp.float32) * (1.0 / np.sqrt(D_IN))
        Wr = jax.random.normal(k3, (D, 3 * D), dtype=jnp.float32) * (1.0 / np.sqrt(D))
        c0 = jax.random.normal(k4, (B, D), dtype=jnp.float32)
        h0 = jax.random.normal(k5, (B, D), dtype=jnp.float32)
        return {'x': x, 'Wk': Wk, 'Wr': Wr, 'c0': c0, 'h0': h0}
    _L0_cond_all = _L0_cond_setup()
    _L0_cond_in = {k: v for k, v in _L0_cond_all.items() if k in ('Wk', 'Wr')}
    del _L0_cond_all

    def _L0_ffn_setup():
        import jax, jax.numpy as jnp
        import numpy as np
        E = 8
        K = 2
        CAP_RATIO = 1.05
        key = jax.random.key(seed)
        ks = jax.random.split(key, 4)
        B, S, D, H = (2, 512, 256, 1024)
        x = jax.random.normal(ks[0], (B, S, D), jnp.float32)
        Wg = jax.random.normal(ks[1], (E, D), jnp.float32) * 0.02
        W1 = jax.random.normal(ks[2], (E, D, H), jnp.float32) * 0.02
        b1 = jnp.zeros((E, H), jnp.float32)
        W2 = jax.random.normal(ks[3], (E, H, D), jnp.float32) * 0.02
        b2 = jnp.zeros((E, D), jnp.float32)
        return {'x': x, 'Wg': Wg, 'W1': W1, 'b1': b1, 'W2': W2, 'b2': b2}
    _L0_ffn_all = _L0_ffn_setup()
    _L0_ffn_in = {k: v for k, v in _L0_ffn_all.items() if k in ('Wg', 'W1', 'b1', 'W2', 'b2')}
    del _L0_ffn_all

    def _L1_cond_setup():
        import jax, jax.numpy as jnp
        import numpy as np
        key = jax.random.key(seed)
        ks = jax.random.split(key, 8)
        B, L, D, N, K = (4, 1024, 256, 64, 4)
        return {'x': jax.random.normal(ks[0], (B, L, D), dtype=jnp.float32), 'conv_w': jax.random.normal(ks[1], (K, 1, D), dtype=jnp.float32) * 0.1, 'conv_b': jnp.zeros((D,), dtype=jnp.float32), 'Wp': jax.random.normal(ks[2], (D, 2 * N), dtype=jnp.float32) * (1.0 / np.sqrt(D)), 'bp': jnp.zeros((2 * N,), dtype=jnp.float32), 'Ws': jax.random.normal(ks[3], (D, N), dtype=jnp.float32) * (1.0 / np.sqrt(D)), 'bs': jnp.zeros((N,), dtype=jnp.float32), 'A_log': jax.random.normal(ks[4], (N,), dtype=jnp.float32) * 0.02, 'dt_log': jax.random.normal(ks[5], (N,), dtype=jnp.float32) * 0.02, 'Wo': jax.random.normal(ks[6], (N, D), dtype=jnp.float32) * (1.0 / np.sqrt(N)), 'bo': jnp.zeros((D,), dtype=jnp.float32)}
    _L1_cond_all = _L1_cond_setup()
    _L1_cond_in = {k: v for k, v in _L1_cond_all.items() if k in ('conv_b', 'Wp', 'bp', 'Ws', 'bs', 'A_log', 'dt_log', 'Wo', 'bo')}
    del _L1_cond_all

    def _L1_ffn_setup():
        import jax, jax.numpy as jnp
        import numpy as np
        DIM = 256
        DEPTH = 2
        HEADS = 8
        DIM_HEAD = 64
        WINDOW = 128
        INNER = HEADS * DIM_HEAD
        HID = int(DIM * 4 * 2 / 3)
        B, N = (2, 2048)
        QK_SCALE = 8.0

        def shift_token(t):
            t1, t2 = jnp.split(t, 2, axis=-1)
            t2 = jnp.pad(t2, ((0, 0), (1, 0), (0, 0)))[:, :-1]
            return jnp.concatenate([t1, t2], axis=-1)

        def l2norm(t):
            return t / jnp.clip(jnp.linalg.norm(t, axis=-1, keepdims=True), 1e-12)

        def rotate_half(x):
            x1, x2 = jnp.split(x, 2, axis=-1)
            return jnp.concatenate([-x2, x1], axis=-1)

        def rotary_xpos(q, k):
            n = q.shape[-2]
            half_idx = jnp.arange(0, DIM_HEAD, 2, dtype=jnp.float32)
            inv_freq = 1.0 / 10000.0 ** (half_idx / DIM_HEAD)
            t = jnp.arange(n, dtype=jnp.float32)
            freqs = t[:, None] * inv_freq[None, :]
            freqs = jnp.concatenate([freqs, freqs], axis=-1)
            base = (half_idx + 0.4 * DIM_HEAD) / (1.4 * DIM_HEAD)
            power = (t - n // 2) / float(WINDOW // 2)
            scale = base[None, :] ** power[:, None]
            scale = jnp.concatenate([scale, scale], axis=-1)
            cos, sin = (jnp.cos(freqs), jnp.sin(freqs))
            q = q * cos * scale + rotate_half(q) * sin * scale
            k = k * cos / scale + rotate_half(k) * sin / scale
            return (q, k)

        def local_attention(q, k, v):
            b, h, n, d = q.shape
            w = n // WINDOW
            bq = q.reshape(b, h, w, WINDOW, d) * QK_SCALE
            bk = k.reshape(b, h, w, WINDOW, d)
            bv = v.reshape(b, h, w, WINDOW, d)

            def look_around(t):
                p = jnp.pad(t, ((0, 0), (0, 0), (1, 0), (0, 0), (0, 0)))
                return jnp.concatenate([p[:, :, :w], p[:, :, 1:]], axis=3)
            bk, bv = (look_around(bk), look_around(bv))
            bt = jnp.arange(n).reshape(w, WINDOW)
            btp = jnp.pad(bt, ((1, 0), (0, 0)), constant_values=-1)
            btk = jnp.concatenate([btp[:w], btp[1:]], axis=1)
            sim = jnp.einsum('bhwid,bhwjd->bhwij', bq, bk)
            i = bt[:, :, None]
            j = btk[:, None, :]
            mask = (i < j) | (i > j + WINDOW) | (j == -1)
            sim = jnp.where(mask, -jnp.finfo(sim.dtype).max, sim)
            attn = jax.nn.softmax(sim, axis=-1)
            out = jnp.einsum('bhwij,bhwjd->bhwid', attn, bv)
            return out.reshape(b, h, n, d)

        def _layer(x, wqkv, qs, ksc, wo, lg, lb, w1, b1, w2, b2):
            b, n, _ = x.shape
            h = shift_token(x)
            qkv = h @ wqkv
            q, k, v = jnp.split(qkv, 3, axis=-1)
            to_heads = lambda t: t.reshape(b, n, HEADS, DIM_HEAD).transpose(0, 2, 1, 3)
            q, k, v = (to_heads(q), to_heads(k), to_heads(v))
            q = l2norm(q) * qs
            k = l2norm(k) * ksc
            q, k = rotary_xpos(q, k)
            o = local_attention(q, k, v)
            o = o.transpose(0, 2, 1, 3).reshape(b, n, INNER)
            x = x + o @ wo
            h = shift_token(x)
            mu = h.mean(-1, keepdims=True)
            var = h.var(-1, keepdims=True)
            h = (h - mu) / jnp.sqrt(var + 1e-05) * lg + lb
            h = h @ w1 + b1
            a, g = jnp.split(h, 2, axis=-1)
            h = a * jax.nn.gelu(g, approximate=False)
            x = x + h @ w2 + b2
            return x
        key = jax.random.key(seed)
        ks = jax.random.split(key, 6)
        return {'x': jax.random.normal(ks[0], (B, N, DIM), jnp.float32), 'wqkv': jax.random.normal(ks[1], (DEPTH, DIM, 3 * INNER), jnp.float32) * 0.02, 'q_scale': jnp.ones((DEPTH, DIM_HEAD), jnp.float32), 'k_scale': jnp.ones((DEPTH, DIM_HEAD), jnp.float32), 'wo': jax.random.normal(ks[2], (DEPTH, INNER, DIM), jnp.float32) * 0.02, 'ln_g': jnp.ones((DEPTH, DIM), jnp.float32), 'ln_b': jnp.zeros((DEPTH, DIM), jnp.float32), 'w1': jax.random.normal(ks[3], (DEPTH, DIM, 2 * HID), jnp.float32) * 0.02, 'b1': jnp.zeros((DEPTH, 2 * HID), jnp.float32), 'w2': jax.random.normal(ks[4], (DEPTH, HID, DIM), jnp.float32) * 0.02, 'b2': jnp.zeros((DEPTH, DIM), jnp.float32)}
    _L1_ffn_all = _L1_ffn_setup()
    _L1_ffn_in = {k: v for k, v in _L1_ffn_all.items() if k in ('wqkv', 'q_scale', 'k_scale', 'wo', 'ln_g', 'ln_b', 'w1', 'b1', 'w2', 'b2')}
    del _L1_ffn_all
    return {'x': x, 'cond_1024': cond_1024, 'L0_cond_Wk': _L0_cond_in['Wk'], 'L0_cond_Wr': _L0_cond_in['Wr'], 'L0_ffn_Wg': _L0_ffn_in['Wg'], 'L0_ffn_W1': _L0_ffn_in['W1'], 'L0_ffn_b1': _L0_ffn_in['b1'], 'L0_ffn_W2': _L0_ffn_in['W2'], 'L0_ffn_b2': _L0_ffn_in['b2'], 'L1_cond_conv_b': _L1_cond_in['conv_b'], 'L1_cond_Wp': _L1_cond_in['Wp'], 'L1_cond_bp': _L1_cond_in['bp'], 'L1_cond_Ws': _L1_cond_in['Ws'], 'L1_cond_bs': _L1_cond_in['bs'], 'L1_cond_A_log': _L1_cond_in['A_log'], 'L1_cond_dt_log': _L1_cond_in['dt_log'], 'L1_cond_Wo': _L1_cond_in['Wo'], 'L1_cond_bo': _L1_cond_in['bo'], 'L1_ffn_wqkv': _L1_ffn_in['wqkv'], 'L1_ffn_q_scale': _L1_ffn_in['q_scale'], 'L1_ffn_k_scale': _L1_ffn_in['k_scale'], 'L1_ffn_wo': _L1_ffn_in['wo'], 'L1_ffn_ln_g': _L1_ffn_in['ln_g'], 'L1_ffn_ln_b': _L1_ffn_in['ln_b'], 'L1_ffn_w1': _L1_ffn_in['w1'], 'L1_ffn_b1': _L1_ffn_in['b1'], 'L1_ffn_w2': _L1_ffn_in['w2'], 'L1_ffn_b2': _L1_ffn_in['b2']}

def reference(x, cond_1024, L0_cond_Wk, L0_cond_Wr, L0_ffn_Wg, L0_ffn_W1, L0_ffn_b1, L0_ffn_W2, L0_ffn_b2, L1_cond_conv_b, L1_cond_Wp, L1_cond_bp, L1_cond_Ws, L1_cond_bs, L1_cond_A_log, L1_cond_dt_log, L1_cond_Wo, L1_cond_bo, L1_ffn_wqkv, L1_ffn_q_scale, L1_ffn_k_scale, L1_ffn_wo, L1_ffn_ln_g, L1_ffn_ln_b, L1_ffn_w1, L1_ffn_b1, L1_ffn_w2, L1_ffn_b2):
    import jax
    import jax.numpy as jnp

    def _L0_cond_ref(x, Wk, Wr, c0, h0):
        import jax, jax.numpy as jnp
        import numpy as np
        B, L, D_IN, D = (64, 128, 256, 256)
        x_proj = jnp.einsum('bli,ig->blg', x, Wk)

        def step(carry, xp_t):
            c, h = carry
            gates = xp_t + h @ Wr
            f, o, g = jnp.split(gates, 3, axis=-1)
            sf = jax.nn.sigmoid(f)
            c_new = c * sf + (1.0 - sf) * jnp.tanh(g)
            h_new = jax.nn.sigmoid(o) * jnp.tanh(c_new)
            return ((c_new, h_new), h_new)
        _, hs = jax.lax.scan(step, (c0, h0), jnp.swapaxes(x_proj, 0, 1))
        return jnp.swapaxes(hs, 0, 1)

    def _L0_ffn_ref(x, Wg, W1, b1, W2, b2):
        import jax, jax.numpy as jnp
        import numpy as np
        E = 8
        K = 2
        CAP_RATIO = 1.05
        B, S, D = x.shape
        T = B * S
        xf = x.reshape(T, D)
        gates = jax.nn.softmax(xf @ Wg.T, axis=-1)
        topw, topi = jax.lax.top_k(gates, K)
        C = int(round(K * T * CAP_RATIO / E))
        e_ord = topi.T.reshape(-1)
        tok_ord = jnp.tile(jnp.arange(T), K)
        oh = jax.nn.one_hot(e_ord, E, dtype=jnp.int32)
        cnt = jnp.take_along_axis(jnp.cumsum(oh, 0) - oh, e_ord[:, None], 1)[:, 0]
        within = cnt < C
        pos = jnp.where(within, cnt, C)
        x_disp = xf[tok_ord]
        buf = jnp.zeros((E, C + 1, D), xf.dtype).at[e_ord, pos].add(x_disp)[:, :C]
        h = jax.nn.gelu(jnp.einsum('ecd,edh->ech', buf, W1) + b1[:, None, :], approximate=False)
        y = jnp.einsum('ech,ehd->ecd', h, W2) + b2[:, None, :]
        y_ord = y[e_ord, jnp.minimum(pos, C - 1)] * within[:, None].astype(y.dtype)
        y_tk = y_ord.reshape(K, T, D).transpose(1, 0, 2)
        cw = topw * within.reshape(K, T).T.astype(topw.dtype)
        out = jnp.einsum('tk,tkd->td', cw, y_tk)
        return out.reshape(B, S, D)

    def _L1_cond_ref(x, conv_w, conv_b, Wp, bp, Ws, bs, A_log, dt_log, Wo, bo):
        import jax, jax.numpy as jnp
        import numpy as np
        B, L, D = x.shape
        K = conv_w.shape[0]
        N = Ws.shape[1]
        x_pad = jnp.pad(x, ((0, 0), (K - 1, 0), (0, 0)))
        conv = conv_b + sum((x_pad[:, k:k + L, :] * conv_w[k, 0] for k in range(K)))
        proj = conv @ Wp + bp
        B_t = jax.nn.softplus(proj[..., :N])
        C_t = jnp.tanh(proj[..., N:])
        u = x @ Ws + bs
        A = -jax.nn.softplus(A_log)
        dt = jax.nn.softplus(dt_log)
        decay = 1.0 + dt * A

        def step(state, inputs):
            u_t, b_t, c_t = inputs
            state = decay * state + dt * b_t * u_t
            return (state, c_t * state)
        init = jnp.zeros((B, N), dtype=x.dtype)
        xs = tuple((jnp.swapaxes(a, 0, 1) for a in (u, B_t, C_t)))
        _, ys = jax.lax.scan(step, init, xs, unroll=4)
        y = jnp.swapaxes(ys, 0, 1)
        return y @ Wo + bo

    def _L1_ffn_ref(x, wqkv, q_scale, k_scale, wo, ln_g, ln_b, w1, b1, w2, b2):
        import jax, jax.numpy as jnp
        import numpy as np
        DIM = 256
        DEPTH = 2
        HEADS = 8
        DIM_HEAD = 64
        WINDOW = 128
        INNER = HEADS * DIM_HEAD
        HID = int(DIM * 4 * 2 / 3)
        B, N = (2, 2048)
        QK_SCALE = 8.0

        def shift_token(t):
            t1, t2 = jnp.split(t, 2, axis=-1)
            t2 = jnp.pad(t2, ((0, 0), (1, 0), (0, 0)))[:, :-1]
            return jnp.concatenate([t1, t2], axis=-1)

        def l2norm(t):
            return t / jnp.clip(jnp.linalg.norm(t, axis=-1, keepdims=True), 1e-12)

        def rotate_half(x):
            x1, x2 = jnp.split(x, 2, axis=-1)
            return jnp.concatenate([-x2, x1], axis=-1)

        def rotary_xpos(q, k):
            n = q.shape[-2]
            half_idx = jnp.arange(0, DIM_HEAD, 2, dtype=jnp.float32)
            inv_freq = 1.0 / 10000.0 ** (half_idx / DIM_HEAD)
            t = jnp.arange(n, dtype=jnp.float32)
            freqs = t[:, None] * inv_freq[None, :]
            freqs = jnp.concatenate([freqs, freqs], axis=-1)
            base = (half_idx + 0.4 * DIM_HEAD) / (1.4 * DIM_HEAD)
            power = (t - n // 2) / float(WINDOW // 2)
            scale = base[None, :] ** power[:, None]
            scale = jnp.concatenate([scale, scale], axis=-1)
            cos, sin = (jnp.cos(freqs), jnp.sin(freqs))
            q = q * cos * scale + rotate_half(q) * sin * scale
            k = k * cos / scale + rotate_half(k) * sin / scale
            return (q, k)

        def local_attention(q, k, v):
            b, h, n, d = q.shape
            w = n // WINDOW
            bq = q.reshape(b, h, w, WINDOW, d) * QK_SCALE
            bk = k.reshape(b, h, w, WINDOW, d)
            bv = v.reshape(b, h, w, WINDOW, d)

            def look_around(t):
                p = jnp.pad(t, ((0, 0), (0, 0), (1, 0), (0, 0), (0, 0)))
                return jnp.concatenate([p[:, :, :w], p[:, :, 1:]], axis=3)
            bk, bv = (look_around(bk), look_around(bv))
            bt = jnp.arange(n).reshape(w, WINDOW)
            btp = jnp.pad(bt, ((1, 0), (0, 0)), constant_values=-1)
            btk = jnp.concatenate([btp[:w], btp[1:]], axis=1)
            sim = jnp.einsum('bhwid,bhwjd->bhwij', bq, bk)
            i = bt[:, :, None]
            j = btk[:, None, :]
            mask = (i < j) | (i > j + WINDOW) | (j == -1)
            sim = jnp.where(mask, -jnp.finfo(sim.dtype).max, sim)
            attn = jax.nn.softmax(sim, axis=-1)
            out = jnp.einsum('bhwij,bhwjd->bhwid', attn, bv)
            return out.reshape(b, h, n, d)

        def _layer(x, wqkv, qs, ksc, wo, lg, lb, w1, b1, w2, b2):
            b, n, _ = x.shape
            h = shift_token(x)
            qkv = h @ wqkv
            q, k, v = jnp.split(qkv, 3, axis=-1)
            to_heads = lambda t: t.reshape(b, n, HEADS, DIM_HEAD).transpose(0, 2, 1, 3)
            q, k, v = (to_heads(q), to_heads(k), to_heads(v))
            q = l2norm(q) * qs
            k = l2norm(k) * ksc
            q, k = rotary_xpos(q, k)
            o = local_attention(q, k, v)
            o = o.transpose(0, 2, 1, 3).reshape(b, n, INNER)
            x = x + o @ wo
            h = shift_token(x)
            mu = h.mean(-1, keepdims=True)
            var = h.var(-1, keepdims=True)
            h = (h - mu) / jnp.sqrt(var + 1e-05) * lg + lb
            h = h @ w1 + b1
            a, g = jnp.split(h, 2, axis=-1)
            h = a * jax.nn.gelu(g, approximate=False)
            x = x + h @ w2 + b2
            return x
        for l in range(DEPTH):
            x = _layer(x, wqkv[l], q_scale[l], k_scale[l], wo[l], ln_g[l], ln_b[l], w1[l], b1[l], w2[l], b2[l])
        return x
    x = x + _L0_ffn_ref(_L0_cond_ref(x, L0_cond_Wk, L0_cond_Wr, cond_1024, cond_1024), L0_ffn_Wg, L0_ffn_W1, L0_ffn_b1, L0_ffn_W2, L0_ffn_b2)
    x = x + _L1_ffn_ref(_L1_cond_ref(x, cond_1024[:, None, :], L1_cond_conv_b, L1_cond_Wp, L1_cond_bp, L1_cond_Ws, L1_cond_bs, L1_cond_A_log, L1_cond_dt_log, L1_cond_Wo, L1_cond_bo), L1_ffn_wqkv, L1_ffn_q_scale, L1_ffn_k_scale, L1_ffn_wo, L1_ffn_ln_g, L1_ffn_ln_b, L1_ffn_w1, L1_ffn_b1, L1_ffn_w2, L1_ffn_b2)
    return x

_drawn_inputs = setup_inputs


def setup_inputs(seed=0):
    import zlib

    import numpy as np

    out = dict(_drawn_inputs(seed))
    spreads = {'L0_ffn_b1': (0.0, 0.618),
     'L0_ffn_b2': (0.0, 0.1),
     'L1_cond_conv_b': (0.0, 0.1),
     'L1_cond_bp': (0.0, 0.1),
     'L1_cond_bs': (0.0, 0.1),
     'L1_cond_bo': (0.0, 0.1),
     'L1_ffn_q_scale': (1.0, 0.6),
     'L1_ffn_k_scale': (1.0, 0.6),
     'L1_ffn_ln_g': (1.0, 0.6),
     'L1_ffn_ln_b': (0.0, 0.8),
     'L1_ffn_b1': (0.0, 0.8),
     'L1_ffn_b2': (0.0, 0.1)}
    factors = {'L0_cond_Wr': 3.142,
     'L0_ffn_W1': 7.457,
     'L0_ffn_W2': 3.753,
     'L1_cond_A_log': 6.061,
     'L1_cond_dt_log': 4.313,
     'L1_ffn_w1': 2.698,
     'L1_ffn_w2': 2.673}
    for name, (base, spread) in spreads.items():
        noise = np.random.default_rng([zlib.crc32(name.encode()), seed]).standard_normal(out[name].shape)
        drawn = base * np.exp(spread * noise) if base else spread * noise
        out[name] = jnp.asarray(drawn.astype(out[name].dtype))
    for name, factor in factors.items():
        out[name] = (out[name] * factor).astype(out[name].dtype)
    return out
```

```python
import numpy as np
import concourse.bass as bass
from concourse import mybir
from concourse.alu_op_type import AluOpType as ALU
from contextlib import ExitStack

ACT = mybir.ActivationFunctionType
AX = mybir.AxisListType
F32 = mybir.dt.float32
F16 = mybir.dt.float16
F32R = mybir.dt.float32r
U32 = mybir.dt.uint32
I32 = mybir.dt.int32

B = 16
L = 256
D = 256
T = B * L
P = 128
KD = D // P


def gated_recurrence(nc, ctx, mem, A):
    G = 3 * D
    W_SCALE = 256.0
    xt, hst = mem["xt"], mem["hst"]
    sb = lambda n, s, d: ctx.enter_context(nc.sbuf_tensor(n, s, d))
    pb = lambda n, s: ctx.enter_context(nc.psum_tensor(n, s, F32))
    sem = lambda n: ctx.enter_context(nc.semaphore(n))
    wk32 = sb("wk32", [P, KD, G], F32)
    wr32 = sb("wr32", [P, KD, G], F32)
    wk = [sb("wk_hi", [P, KD, G], F16), sb("wk_lo", [P, KD, G], F16)]
    wr = [sb("wr_hi", [P, KD, G], F16), sb("wr_lo", [P, KD, G], F16)]
    xs = [[sb(f"xs_{h}{p}", [P, KD, B], F16) for h in ("hi", "lo")] for p in range(2)]
    x_now = [sb(f"x_now{p}", [P, KD, B], F32) for p in range(2)]
    hh = [[sb(f"h_{h}{p}", [P, KD, B], F16) for h in ("hi", "lo")] for p in range(2)]
    hf = [sb(f"h_full{p}", [P, KD, B], F32) for p in range(2)]
    t_fg = sb("t_fg", [P, 4, B], F32)
    t_o = sb("t_o", [P, KD, B], F32)
    t_c = sb("t_c", [P, KD, B], F32)
    cell = sb("cell", [P, KD, B], F32)
    keep = sb("keep", [P, KD, B], F32)
    fresh = sb("fresh", [P, KD, B], F32)
    cnd = sb("cnd", [P, KD, B], F32)
    zero = mem["zero"]
    zero_kb = zero[:, 0:KD * B].rearrange("p (k b) -> p k b", k=KD)
    p_fg = [pb(f"p_fg{p}", [P, 4, B]) for p in range(2)]
    p_o = [pb(f"p_o{p}", [P, KD, B]) for p in range(2)]

    w_loaded, x_loaded, c_loaded = sem("w_loaded"), [sem(f"x_loaded{c}") for c in range(4)], sem("c_loaded")
    w_scaled, w_hi, w_split = sem("w_scaled"), sem("w_hi"), sem("w_split")
    x_taken, x_hi_ready, x_split = sem("x_taken"), sem("x_hi_ready"), sem("x_split")
    x_used = sem("x_used")
    fg_sums, o_sums = sem("fg_sums"), sem("o_sums")
    fg_ready, o_ready, tc_ready = sem("fg_ready"), sem("o_ready"), sem("tc_ready")
    kept, cell_ready = sem("kept"), sem("cell_ready")
    h_hi_ready, h_full_ready, h_split = sem("h_hi_ready"), sem("h_full_ready"), sem("h_split")
    h_stored = sem("h_stored")
    zero_ready, zeroed = mem["zero_ready"], mem["zeroed"]
    QT = T // 4
    slots = mem["slots"]
    NSLOT = mem["n_slots"]

    STEPS = L
    U = 8
    blk = ctx.enter_context(nc.Block())

    @blk.sync
    def _(sp):
        sp.dma_start(wr32[:, :, :], A["L0_cond_Wr"].rearrange("(k p) n -> p k n", p=P)).then_inc(w_loaded, 16)
        sp.dma_start(wk32[:, :, :], A["L0_cond_Wk"].rearrange("(k p) n -> p k n", p=P)).then_inc(w_loaded, 16)
        sp.dma_start(cnd[:, :, :], A["condT"].rearrange("(k p) b -> p k b", p=P)).then_inc(c_loaded, 16)
        xv = A["xT_tb"].rearrange("(k p) n -> p k n", p=P)
        for c in range(4):
            sp.dma_start(xt[:, :, c * QT:(c + 1) * QT], xv[:, :, c * QT:(c + 1) * QT]).then_inc(x_loaded[c], 16)
        sp.wait_ge(zero_ready, 1)
        rows = 8
        sv = slots.rearrange("(a p r) d -> a p (r d)", p=120, r=rows)
        for a in range(NSLOT // (120 * rows)):
            sp.dma_start(sv[a], zero[0:120, :]).then_inc(zeroed, 16)
        sp.wait_ge(zeroed, 16 * (NSLOT // (120 * rows)))

    @blk.gpsimd
    def _(pool):
        pool.memset(zero[:, :], 0.0).then_inc(zero_ready, 1)
        pool.wait_ge(zero_ready, 1)

        def split_x(i, t_off, first=False):
            par = t_off % 2
            if not first:
                pool.wait_ge(x_used, U * i + t_off - 1)
            col = bass.ds(i * (U * B) + t_off * B, B)
            nc.gpsimd.tensor_copy(x_now[par][:, :, :], xt[:, :, col]).then_inc(x_taken, 1)
            pool.wait_ge(x_taken, U * i + t_off + 1)
            nc.gpsimd.tensor_tensor(xs[par][0][:, :, :], x_now[par][:, :, :], zero_kb, ALU.add).then_inc(x_hi_ready, 1)
            pool.wait_ge(x_hi_ready, U * i + t_off + 1)
            nc.gpsimd.tensor_tensor(xs[par][1][:, :, :], x_now[par][:, :, :], xs[par][0][:, :, :],
                                    ALU.subtract).then_inc(x_split, 1)

        def store_h(i, t):
            pool.wait_ge(h_full_ready, U * i + t + 1)
            nc.gpsimd.tensor_copy(hst[:, :, bass.ds(i * (U * B) + t * B, B)], hf[t % 2][:, :, :]).then_inc(h_stored, 1)

        pool.wait_ge(x_loaded[0], 16)
        split_x(0, 0, True)
        split_x(0, 1, True)
        for c in range(1, 4):
            pool.wait_ge(x_loaded[c], 16)
        with pool.Fori(0, STEPS // U - 1) as i:
            for t in range(U):
                split_x(i, t + 2)
                store_h(i, t)
        for t in range(U):
            if t + 2 < U:
                split_x(STEPS // U - 1, t + 2)
            store_h(STEPS // U - 1, t)

    @blk.tensor
    def _(pe):
        FG = [0, 1, 4, 5]
        O = [2, 3]

        def part(psum, chunks, w, a, start, order):
            for n, (wh, ah) in enumerate(order):
                for j, c in enumerate(chunks):
                    for k in range(KD):
                        last = nc.tensor.matmul(psum[:, j, :], w[wh][:, k, c * P:(c + 1) * P], a[ah][:, k, :],
                                                start=(start and n == 0 and j == 0 and k == 0), stop=False,
                                                skip_group_check=True)
            return last

        def x_products(i, t_off):
            par = t_off % 2
            pe.wait_ge(x_split, U * i + t_off + 1)
            part(p_fg[par], FG, wk, xs[par], True, [(0, 0), (1, 0), (0, 1)])
            part(p_o[par], O, wk, xs[par], True, [(0, 0), (1, 0), (0, 1)]).then_inc(x_used, 1)

        def h_products(i, t):
            par = t % 2
            pe.wait_ge(h_hi_ready, U * i + t + 1)
            part(p_fg[par], FG, wr, hh[1 - par], False, [(0, 0), (1, 0)])
            pe.wait_ge(h_split, U * i + t + 1)
            part(p_fg[par], FG, wr, hh[1 - par], False, [(0, 1)]).then_inc(fg_sums, 1)
            part(p_o[par], O, wr, hh[1 - par], False, [(0, 0), (1, 0), (0, 1)]).then_inc(o_sums, 1)

        pe.wait_ge(w_split, 2)
        x_products(0, 0)
        with pe.Fori(0, STEPS // U - 1) as i:
            for t in range(U):
                h_products(i, t)
                x_products(i, t + 1)
        for t in range(U):
            h_products(STEPS // U - 1, t)
            if t + 1 < U:
                x_products(STEPS // U - 1, t + 1)

    @blk.scalar
    def _(act):
        def step(i, t):
            par = t % 2
            act.wait_ge(fg_sums, U * i + t + 1)
            nc.scalar.activation(t_fg[:, :, :], p_fg[par][:, :, :], ACT.Tanh, scale=1.0 / W_SCALE).then_inc(fg_ready, 1)
            act.wait_ge(o_sums, U * i + t + 1)
            nc.scalar.activation(t_o[:, :, :], p_o[par][:, :, :], ACT.Tanh, scale=1.0 / W_SCALE).then_inc(o_ready, 1)
            act.wait_ge(cell_ready, U * i + t + 2)
            nc.scalar.activation(t_c[:, :, :], cell[:, :, :], ACT.Tanh, scale=0.5).then_inc(tc_ready, 1)

        with act.Fori(0, STEPS // U) as i:
            for t in range(U):
                step(i, t)

    @blk.vector
    def _(dve):
        dve.wait_ge(w_loaded, 32)
        for n, (w, sc) in enumerate([(wr32, 0.25), (wk32, 0.5)]):
            nc.vector.tensor_scalar(w[:, :, 0:2 * D], w[:, :, 0:2 * D], sc * W_SCALE, None, ALU.mult).then_inc(w_scaled, 1)
            nc.vector.tensor_scalar(w[:, :, 2 * D:G], w[:, :, 2 * D:G], 2 * sc * W_SCALE, None, ALU.mult).then_inc(w_scaled, 1)
            dve.wait_ge(w_scaled, 2 * n + 2)
            wp = (wr, wk)[n]
            nc.vector.tensor_copy(wp[0][:, :, :], w[:, :, :]).then_inc(w_hi, 1)
            dve.wait_ge(w_hi, n + 1)
            nc.vector.tensor_tensor(wp[1][:, :, :], w[:, :, :], wp[0][:, :, :], ALU.subtract).then_inc(w_split, 1)
        dve.wait_ge(c_loaded, 16)
        nc.vector.tensor_scalar(cell[:, :, :], cnd[:, :, :], 2.0, None, ALU.mult).then_inc(cell_ready, 1)
        dve.wait_ge(cell_ready, 1)
        nc.vector.tensor_copy(hh[1][0][:, :, :], cell[:, :, :]).then_inc(h_hi_ready, 1)
        dve.wait_ge(h_hi_ready, 1)
        nc.vector.tensor_tensor(hh[1][1][:, :, :], cell[:, :, :], hh[1][0][:, :, :], ALU.subtract).then_inc(h_split, 1)

        def step(i, t):
            par, t1 = t % 2, U * i + t + 1
            dve.wait_ge(fg_ready, t1)
            nc.vector.scalar_tensor_tensor(keep[:, :, :], t_fg[:, 0:2, :], 1.0, cell[:, :, :], ALU.add, ALU.mult)
            nc.vector.scalar_tensor_tensor(fresh[:, :, :], t_fg[:, 0:2, :], 1.0, t_fg[:, 2:4, :],
                                           ALU.subtract, ALU.mult).then_inc(kept, 1)
            dve.wait_ge(kept, t1)
            nc.vector.scalar_tensor_tensor(cell[:, :, :], keep[:, :, :], 0.5, fresh[:, :, :],
                                           ALU.mult, ALU.subtract).then_inc(cell_ready, 1)
            dve.wait_ge(tc_ready, t1)
            nc.vector.scalar_tensor_tensor(hh[par][0][:, :, :], t_o[:, :, :], 1.0, t_c[:, :, :],
                                           ALU.add, ALU.mult).then_inc(h_hi_ready, 1)
            dve.wait_ge(h_stored, t1)
            nc.vector.scalar_tensor_tensor(hf[par][:, :, :], t_o[:, :, :], 1.0, t_c[:, :, :],
                                           ALU.add, ALU.mult).then_inc(h_full_ready, 1)
            dve.wait_ge(h_full_ready, t1)
            nc.vector.tensor_tensor(hh[par][1][:, :, :], hf[par][:, :, :], hh[par][0][:, :, :],
                                    ALU.subtract).then_inc(h_split, 1)

        dve.sem_inc(h_stored, 2)
        with dve.Fori(0, STEPS // U) as i:
            for t in range(U):
                step(i, t)


E = 8
TOP = 2
HID = 1024
KH = HID // P
CAP = int(round(TOP * T * 1.05 / E))
CHUNK = 360
SUB = CHUNK // 3
CPE = -(-CAP // CHUNK)
STRIDE = CPE * CHUNK
NSLOTS = E * STRIDE
NT = T // P
TT = P // B
DROPPED = 4.0 * NSLOTS


def route(nc, ctx, mem, A):
    sb = lambda n, s, d=F32: ctx.enter_context(nc.sbuf_tensor(n, s, d))
    pb = lambda n, s: ctx.enter_context(nc.psum_tensor(n, s, F32))
    sem = lambda n: ctx.enter_context(nc.semaphore(n))
    hst, rows = mem["hst"], mem["rows"]
    ident = mem["ident"]
    wg = sb("wg", [P, KD, E])
    cst = sb("route_masks", [P, 4, P])
    iota = sb("iota", [P, NT, E])
    keepcol = sb("keepcol", [P, E * TOP, NT])
    ebase = sb("ebase", [P, E])
    lg = sb("lg", [P, NT, E])
    m1 = sb("m1", [P, NT]); dl = sb("dl", [P, NT, E]); ex = sb("ex", [P, NT, E]); sm = sb("sm", [P, NT]); rs = sb("rs", [P, NT])
    g = sb("g", [P, NT, E]); gk = sb("gk", [P, TOP, NT]); eq = sb("eq", [P, NT, E]); cand = sb("cand", [P, NT, E])
    idx = sb("idx", [P, TOP, NT]); hot = sb("hot", [P, E, TOP, NT])
    rest = sb("rest", [P, NT, E])
    tot = sb("tot", [P, E * TOP]); base = sb("base", [P, E, TOP])
    scan = sb("scan", [P, E * TOP, NT]); cnt = sb("cnt", [P, E, TOP, NT])
    pos = sb("pos", [P, TOP, NT]); fits = sb("fits", [P, TOP, NT]); off = sb("off", [P, TOP, NT])
    sl = sb("sl", [P, TOP, NT]); miss = sb("miss", [P, TOP, NT])
    put, get, cw = mem["put"], mem["get"], mem["cw"]
    p_rows = [pb(f"p_rows{p}", [P, D]) for p in range(3)]
    p_lg = pb("p_lg", [P, NT, E])
    p_same = pb("p_same", [P, E * TOP, NT])
    p_cor = pb("p_cor", [P, E * TOP, NT])
    p_base = pb("p_base", [P, 2, E * TOP])

    loaded = sem("route_loaded")
    tile_turned, rows_ready, lg_done = sem("tile_turned"), sem("rows_ready"), sem("lg_done")
    v = sem("route_step")
    logit_sub, exps = sem("logit_sub"), sem("exps")
    hot_ready, counted, tot_ready, tot_summed = sem("hot_ready"), sem("counted"), sem("tot_ready"), sem("tot_summed")
    put_ready, scattered = sem("put_ready"), sem("scattered")
    slots = mem["slots"]
    blk = ctx.enter_context(nc.Block())

    @blk.sync
    def _(sp):
        sp.dma_start(wg[:, :, :], A["WgT"].rearrange("(k p) e -> p k e", p=P)).then_inc(loaded, 16)
        sp.dma_start(ident[:, :], A["ident"]).then_inc(loaded, 16)
        sp.dma_start(cst[:, :, :], A["route_masks"]).then_inc(loaded, 16)
        sp.dma_start(iota[:, :, :], A["iota"].rearrange("p (n e) -> p n e", e=E)).then_inc(loaded, 16)
        sp.dma_start(keepcol[:, :, :], A["keepcol"].rearrange("p (a n) -> p a n", n=NT)).then_inc(loaded, 16)

    @blk.tensor
    def _(pe):
        pe.wait_ge(loaded, 80)
        for n in range(NT):
            if n >= 3:
                pe.wait_ge(rows_ready, n - 2)
            for k in range(KD):
                last = nc.tensor.transpose(p_rows[n % 3][:, k * P:(k + 1) * P], hst[:, k, n * P:(n + 1) * P], ident[:, :])
            last.then_inc(tile_turned, 1)
            for k in range(KD):
                last = nc.tensor.matmul(p_lg[:, n, :], hst[:, k, n * P:(n + 1) * P], wg[:, k, :], start=(k == 0), stop=(k == KD - 1))
        last.then_inc(lg_done, 1)
        hv = hot[:, :, :, :].rearrange("p e k n -> p (e k n)")
        pe.wait_ge(hot_ready, 2)
        nc.tensor.matmul(p_same[:, :, :], cst[:, 2, :], hv, start=True, stop=True).then_inc(counted, 1)
        nc.tensor.matmul(p_cor[:, :, :], cst[:, 3, :], hv, start=True, stop=True).then_inc(counted, 1)
        pe.wait_ge(tot_ready, 1)
        nc.tensor.matmul(p_base[:, 0, :], cst[:, 0, :], tot[:, :], start=True, stop=True)
        nc.tensor.matmul(p_base[:, 1, :], cst[:, 1, :], tot[:, :], start=True, stop=True).then_inc(tot_summed, 1)

    @blk.scalar
    def _(act):
        for n in range(NT):
            act.wait_ge(tile_turned, n + 1)
            nc.scalar.activation(rows[:, n, :], p_rows[n % 3][:, :], ACT.Copy, scale=0.5).then_inc(rows_ready, 1)
        act.wait_ge(logit_sub, 1)
        nc.scalar.activation(ex[:, :, :], dl[:, :, :], ACT.Exp).then_inc(exps, 1)

    @blk.vector
    def _(dve):
        count = [0]

        def then(ins):
            count[0] += 1
            ins.then_inc(v, 1)
            dve.wait_ge(v, count[0])

        V = nc.vector
        over = lambda a: a.broadcast_to([P, NT, E]) if False else a.unsqueeze(2).broadcast_to([P, NT, E])
        dve.wait_ge(lg_done, 1)
        then(V.tensor_scalar(lg[:, :, :], p_lg[:, :, :], 0.5, None, ALU.mult))
        then(V.tensor_reduce(m1[:, :], lg[:, :, :], AX.X, ALU.max))
        V.tensor_tensor(dl[:, :, :], lg[:, :, :], over(m1[:, :]), ALU.subtract).then_inc(logit_sub, 1)
        dve.wait_ge(exps, 1)
        then(V.tensor_reduce(sm[:, :], ex[:, :, :], AX.X, ALU.add))
        then(V.reciprocal(rs[:, :], sm[:, :]))
        then(V.tensor_tensor(g[:, :, :], ex[:, :, :], over(rs[:, :]), ALU.mult))
        cur = g
        for k in range(TOP):
            then(V.tensor_reduce(gk[:, k, :], cur[:, :, :], AX.X, ALU.max))
            then(V.tensor_tensor(eq[:, :, :], cur[:, :, :], over(gk[:, k, :]), ALU.is_equal))
            then(V.scalar_tensor_tensor(cand[:, :, :], eq[:, :, :], -float(E), iota[:, :, :], ALU.mult, ALU.add))
            then(V.tensor_reduce(idx[:, k, :], cand[:, :, :], AX.X, ALU.min))
            then(V.tensor_scalar(idx[:, k, :], idx[:, k, :], float(E), None, ALU.add))
            then(V.tensor_tensor(eq[:, :, :], iota[:, :, :], over(idx[:, k, :]), ALU.is_equal))
            V.tensor_copy(hot[:, :, k, :].rearrange("p e n -> p n e"), eq[:, :, :]).then_inc(hot_ready, 1)
            if k == 0:
                then(V.scalar_tensor_tensor(rest[:, :, :], eq[:, :, :], -2.0, g[:, :, :], ALU.mult, ALU.add))
                cur = rest
        dve.wait_ge(hot_ready, 2)
        hv = hot[:, :, :, :].rearrange("p e k n -> p (e k) n")
        V.tensor_reduce(tot[:, :], hv, AX.X, ALU.add).then_inc(tot_ready, 1)
        dve.wait_ge(counted, 2)
        flat = lambda a: a.rearrange("p a n -> p (a n)")
        then(V.tensor_tensor_scan(flat(scan[:, :, :]), flat(keepcol[:, :, :]), flat(p_same[:, :, :]), 0.0, ALU.mult, ALU.add))
        cv = cnt[:, :, :, :].rearrange("p e k n -> p (e k) n")
        then(V.tensor_tensor(cv, scan[:, :, :], p_cor[:, :, :], ALU.add))
        dve.wait_ge(tot_summed, 1)
        bv = base[:, :, :].rearrange("p e k -> p (e k)")
        then(V.tensor_copy(bv, p_base[:, 0, :]))
        then(V.tensor_tensor(base[:, :, 1], base[:, :, 1], p_base[:, 1, 0:2 * E:2], ALU.add))
        then(V.tensor_tensor(cv, cv, bv.unsqueeze(2).broadcast_to([P, E * TOP, NT]), ALU.add))
        then(V.tensor_tensor(cv, cv, hv, ALU.mult))
        for k in range(TOP):
            then(V.tensor_reduce(pos[:, k, :], cnt[:, :, k, :].rearrange("p e n -> p n e"), AX.X, ALU.add))
        then(V.tensor_scalar(fits[:, :, :], pos[:, :, :], float(CAP), None, ALU.is_lt))
        then(V.tensor_tensor(cw[:, :, :], gk[:, :, :], fits[:, :, :], ALU.mult))
        then(V.tensor_scalar(off[:, :, :], pos[:, :, :], float(CAP - 1), None, ALU.min))
        then(V.scalar_tensor_tensor(sl[:, :, :], idx[:, :, :], float(STRIDE), off[:, :, :], ALU.mult, ALU.add))
        then(V.tensor_scalar(miss[:, :, :], fits[:, :, :], -DROPPED, DROPPED, ALU.mult, ALU.add))
        then(V.tensor_tensor(miss[:, :, :], miss[:, :, :], sl[:, :, :], ALU.add))
        V.tensor_copy(get[:, :, :], sl[:, :, :]).then_inc(put_ready, 1)
        V.tensor_copy(put[:, :, :], miss[:, :, :]).then_inc(put_ready, 1)

    @blk.gpsimd
    def _(pool):
        pool.wait_ge(put_ready, 2)
        pool.wait_ge(rows_ready, NT)
        for n in range(NT):
            for k in range(TOP):
                nc.gpsimd.indirect_dma_start(slots, bass.IndirectOffsetOnAxis(put[:, k, n:n + 1], 0), rows[:, n, :], None,
                                             bounds_check=NSLOTS - 1, oob_is_err=False).then_inc(scattered, 16)
        pool.wait_ge(scattered, 16 * NT * TOP)


def experts(nc, ctx, mem, A):
    sb = lambda n, s, d=F32: ctx.enter_context(nc.sbuf_tensor(n, s, d))
    pb = lambda n, s: ctx.enter_context(nc.psum_tensor(n, s, F32))
    sem = lambda n: ctx.enter_context(nc.semaphore(n))
    ident, slots, ydram = mem["ident"], mem["slots"], mem["ydram"]
    w1_raw, w2_raw = sb("w1_raw", [P, KD, HID]), sb("w2_raw", [P, KH, D])
    w1 = [[sb(f"w1_{h}{q}", [P, KD, HID], F32R) for h in ("hi", "lo")] for q in range(2)]
    w2 = [[sb(f"w2_{h}{q}", [P, KH, D], F32R) for h in ("hi", "lo")] for q in range(2)]
    b1 = [sb(f"b1_{q}", [P, KH]) for q in range(2)]
    b2 = [sb(f"b2_{q}", [P, D]) for q in range(2)]
    rin = [sb(f"rin{q}", [SUB, 3, D]) for q in range(3)]
    xin = [[sb(f"xin_{h}{q}", [P, KD, CHUNK], F32R) for h in ("hi", "lo")] for q in range(2)]
    gelu = [sb(f"gelu{q}", [P, CHUNK]) for q in range(3)]
    hid = [[sb(f"hid_{h}{q}", [P, KH, CHUNK], F32R) for h in ("hi", "lo")] for q in range(2)]
    yout = [sb(f"yout{q}", [SUB, 3, D]) for q in range(2)]
    p_t = pb("p_t", [P, KD, 512])
    p_h = [pb(f"p_h{q}", [P, CHUNK]) for q in range(3)]
    p_y = [pb(f"p_y{q}", [SUB, D]) for q in range(3)]
    w_in, b_in, w_hi, w_split = [sem("w1_in"), sem("w2_in")], [sem(f"b_in{q}") for q in range(2)], sem("w_hi"), sem("w_split")
    r_in = [sem(f"r_in{q}") for q in range(3)]
    turned, xin_hi, xin_ready, h_sum, gelu_ready, h_hi, h_ready, y_sum, y_ready = (
        sem(n) for n in ("turned", "xin_hi", "xin_ready", "h_sum", "gelu_ready", "hid_hi", "h_ready", "y_sum", "y_ready"))
    y_stored = [sem(f"y_stored{q}") for q in range(2)]
    CB = 2 * CPE
    NI = E // 2
    blk = ctx.enter_context(nc.Block())
    sv = slots.rearrange("(a s p) d -> a p s d", p=SUB, s=3)
    yv = ydram.rearrange("(a s p) d -> a p s d", p=SUB, s=3)
    HALVES = ((0, 0), (0, 1), (1, 0))

    @blk.sync
    def _(sp):
        sp.sem_inc(turned, CB)
        sp.sem_inc(w_split, 2)

        def weights(i, q):
            e = i * 2 + q
            sp.wait_ge(w_split, 2 * e + 2)
            sp.dma_start(w1_raw[:, :, :], A["L0_ffn_W1"].rearrange("e (k p) n -> e p k n", p=P)[bass.ds(e, 1)].rearrange("o p k n -> (o p) k n")).then_inc(w_in[0], 16)
            sp.dma_start(w2_raw[:, :, :], A["L0_ffn_W2"].rearrange("e (k p) n -> e p k n", p=P)[bass.ds(e, 1)].rearrange("o p k n -> (o p) k n")).then_inc(w_in[1], 16)

        def biases(i, q):
            e = i * 2 + q
            sp.wait_ge(y_ready, 3 * CB * i + 3 * CPE * (q + 1))
            sp.dma_start(b1[q][:, :], A["b1T"][:, bass.ds(e * KH, KH)]).then_inc(b_in[q], 16)
            sp.dma_start(b2[q][:, :], A["L0_ffn_b2"][bass.ds(e, 1), :].broadcast_to([P, D])).then_inc(b_in[q], 16)

        def slot_rows(i, c):
            sp.wait_ge(turned, CB + CB * i + c - 2)
            sp.dma_start(rin[c % 3][:, :, :], sv[bass.ds(i * CB + c, 1)].rearrange("o p s d -> (o p) s d")).then_inc(r_in[c % 3], 16)

        with sp.Fori(0, NI) as i:
            for q in range(2):
                weights(i, q)
                for c in range(CPE):
                    slot_rows(i, q * CPE + c)
                    if c == 0:
                        biases(i, q)

    @blk.tensor
    def _(pe):
        def turn(i, c):
            pe.wait_ge(r_in[c % 3], 16 * ((CB // 3) * i + c // 3 + 1))
            for s in range(3):
                for k in range(KD):
                    last = nc.tensor.transpose(p_t[:, k, s * SUB:(s + 1) * SUB], rin[c % 3][:, s, k * P:(k + 1) * P], ident[0:SUB, 0:SUB])
            last.then_inc(turned, 1)

        def up(i, c):
            q = c // CPE
            if c % CPE == 0:
                pe.wait_ge(w_split, 2 * (2 * i + q) + 3)
            pe.wait_ge(xin_ready, CB * i + c + 1)
            for j in range(KH):
                pe.wait_ge(gelu_ready, KH * (CB * i + c) + j + 1)
                out = p_h[(c * KH + j) % 3][:, :]
                for k in range(KD):
                    for a, b in HALVES:
                        last = nc.tensor.matmul(out, w1[q][a][:, k, j * P:(j + 1) * P], xin[c % 2][b][:, k, :],
                                                start=(k == 0 and a + b == 0), stop=(k == KD - 1 and a == 1))
                last.then_inc(h_sum, 1)

        def down(i, c):
            q = c // CPE
            if c % CPE == 0:
                pe.wait_ge(w_split, 2 * (2 * i + q) + 4)
            pe.wait_ge(h_ready, KH * (CB * i + c + 1) + 3)
            for s in range(3):
                pe.wait_ge(y_ready, 3 * (CB * i + c) + s + 3 * CB - 2)
                for j in range(KH):
                    for a, b in HALVES:
                        last = nc.tensor.matmul(p_y[s][:, :], hid[c % 2][a][:, j, s * SUB:(s + 1) * SUB], w2[q][b][:, j, :],
                                                start=(j == 0 and a + b == 0), stop=(j == KH - 1 and a == 1))
                last.then_inc(y_sum, 1)

        def body(i, first=False, tail=False):
            for c in range(CB):
                up(i, c)
                if not (tail and c == CB - 1):
                    turn(i, c + 1)
                if c:
                    down(i, c - 1)
                elif not first:
                    down(i - 1, CB - 1)

        turn(0, 0)
        body(0, first=True)
        with pe.Fori(1, NI - 1) as i:
            body(i)
        body(NI - 1, tail=True)
        down(NI - 1, CB - 1)

    @blk.scalar
    def _(act):
        act.sem_inc(gelu_ready, 3)
        act.sem_inc(h_ready, 3)
        with act.Fori(0, NI) as i:
            for c in range(CB):
                if c % CPE == 0:
                    act.wait_ge(b_in[c // CPE], 32 * i + 32)
                for j in range(KH):
                    u = c * KH + j
                    act.wait_ge(h_sum, KH * CB * i + u + 1)
                    act.wait_ge(h_ready, KH * CB * i + u + 1)
                    nc.scalar.activation(gelu[u % 3][:, :], p_h[u % 3][:, :], ACT.Gelu,
                                         bias=b1[c // CPE][:, j:j + 1]).then_inc(gelu_ready, 1)

    @blk.vector
    def _(dve):
        dve.sem_inc(y_ready, 3 * CB)

        def take(i, c):
            hi, lo = xin[c % 2]
            dve.wait_ge(turned, CB * i + CB + c + 1)
            nc.vector.tensor_copy(hi[:, :, :], p_t[:, :, 0:CHUNK]).then_inc(xin_hi, 1)
            dve.wait_ge(xin_hi, CB * i + c + 1)
            nc.vector.tensor_tensor(lo[:, :, :], p_t[:, :, 0:CHUNK], hi[:, :, :].bitcast(F32), ALU.subtract).then_inc(xin_ready, 1)

        def weights_hi(i, q):
            e = i * 2 + q
            for n, (raw, (hi, lo)) in enumerate(((w1_raw, w1[q]), (w2_raw, w2[q]))):
                dve.wait_ge(w_in[n], 16 * e + 16)
                nc.vector.tensor_copy(hi[:, :, :], raw[:, :, :]).then_inc(w_hi, 1)

        def split_hidden(i, c):
            hi, lo = hid[c % 2]
            for j in range(KH):
                u = c * KH + j
                dve.wait_ge(gelu_ready, KH * CB * i + u + 4)
                nc.vector.tensor_copy(hi[:, j, :], gelu[u % 3][:, :]).then_inc(h_hi, 1)
                dve.wait_ge(h_hi, KH * CB * i + u + 1)
                nc.vector.tensor_tensor(lo[:, j, :], gelu[u % 3][:, :], hi[:, j, :].bitcast(F32), ALU.subtract).then_inc(h_ready, 1)

        def bias(i, c):
            if not (isinstance(i, int) and i == 0 and c < 2):
                dve.wait_ge(y_stored[c % 2], 16 * (CB // 2 * i + c // 2))
            for s in range(3):
                dve.wait_ge(y_sum, 3 * (CB * i + c) + s + 1)
                nc.vector.tensor_tensor(yout[c % 2][:, s, :], p_y[s][:, :], b2[c // CPE][0:SUB, :], ALU.add).then_inc(y_ready, 1)

        def body(i, first=False, tail=False):
            for c in range(CB):
                split_hidden(i, c)
                if not (tail and c == CB - 1):
                    take(i, c + 1)
                if c:
                    bias(i, c - 1)
                elif not first:
                    bias(i - 1, CB - 1)
                if c == 0:
                    weights_hi(i, 1)
                elif c == CPE and not tail:
                    weights_hi(i + 1, 0)

        take(0, 0)
        weights_hi(0, 0)
        body(0, first=True)
        with dve.Fori(1, NI - 1) as i:
            body(i)
        body(NI - 1, tail=True)
        bias(NI - 1, CB - 1)

    @blk.gpsimd
    def _(pool):
        def weights_lo(i, q):
            e = i * 2 + q
            for n, (raw, (hi, lo)) in enumerate(((w1_raw, w1[q]), (w2_raw, w2[q]))):
                pool.wait_ge(w_hi, 2 * e + n + 1)
                pool.tensor_tensor(lo[:, :, :], raw[:, :, :], hi[:, :, :].bitcast(F32), ALU.subtract).then_inc(w_split, 1)

        def store(i, q):
            for c in range(q * CPE, (q + 1) * CPE):
                pool.wait_ge(y_ready, 3 * (CB * i + c + 1) + 3 * CB)
                pool.dma_start(yv[bass.ds(i * CB + c, 1)].rearrange("o p s d -> (o p) s d"), yout[c % 2][:, :, :]).then_inc(y_stored[c % 2], 16)

        weights_lo(0, 0)
        with pool.Fori(0, NI - 1) as i:
            weights_lo(i, 1)
            store(i, 0)
            weights_lo(i + 1, 0)
            store(i, 1)
        weights_lo(NI - 1, 1)
        store(NI - 1, 0)
        store(NI - 1, 1)
        for q in range(2):
            pool.wait_ge(y_stored[q], 16 * (CB // 2) * NI)


PAD = 15
LP = L + PAD


def combine(nc, ctx, mem, A):
    sb = lambda n, s, d=F32: ctx.enter_context(nc.sbuf_tensor(n, s, d))
    sem = lambda n: ctx.enter_context(nc.semaphore(n))
    ident, ydram, x1, get, cw = mem["ident"], mem["ydram"], mem["x1"], mem["get"], mem["cw"]
    NB = 4
    yk = [[sb(f"yk{k}_{q}", [P, D]) for q in range(NB)] for k in range(TOP)]
    xr = [sb(f"xr{q}", [P, D]) for q in range(NB)]
    half = [sb(f"half{q}", [P, D]) for q in range(2)]
    whole = [sb(f"whole{q}", [P, D]) for q in range(2)]
    p_x = [ctx.enter_context(nc.psum_tensor(f"p_x{q}", [P, KD, P], F32)) for q in range(4)]
    gathered = [sem(f"gathered{q}") for q in range(NB)]
    x_rows = [sem(f"x_rows{q}") for q in range(NB)]
    half_ready, whole_ready, x1_turned, x1_out, padded = (sem(n) for n in ("half_ready", "whole_ready", "x1_turned", "x1_out", "padded"))
    blk = ctx.enter_context(nc.Block())

    @blk.gpsimd
    def _(pool):
        for k in range(KD):
            pool.memset(x1[:, k, :, 0:PAD], 0.0).then_inc(padded, 1)
        for n in range(NT):
            if n >= NB:
                pool.wait_ge(whole_ready, n - NB + 1)
            for k in range(TOP):
                nc.gpsimd.indirect_dma_start(yk[k][n % NB][:, :], None, ydram, bass.IndirectOffsetOnAxis(get[:, k, n:n + 1], 0),
                                             bounds_check=NSLOTS - 1, oob_is_err=False).then_inc(gathered[n % NB], 16)

    @blk.sync
    def _(sp):
        for n in range(NT):
            if n >= NB:
                sp.wait_ge(whole_ready, n - NB + 1)
            sp.dma_start(xr[n % NB][:, :], A["x_rows"][n * P:(n + 1) * P, :]).then_inc(x_rows[n % NB], 16)

    @blk.vector
    def _(dve):
        for n in range(NT):
            q = n % NB
            dve.wait_ge(x_rows[q], 16 * (n // NB + 1))
            dve.wait_ge(gathered[q], 32 * (n // NB + 1))
            nc.vector.scalar_tensor_tensor(half[n % 2][:, :], yk[0][q][:, :], cw[:, 0, n:n + 1], xr[q][:, :],
                                           ALU.mult, ALU.add).then_inc(half_ready, 1)
            dve.wait_ge(half_ready, n + 1)
            if n >= 2:
                dve.wait_ge(x1_turned, n - 1)
            nc.vector.scalar_tensor_tensor(whole[n % 2][:, :], yk[1][q][:, :], cw[:, 1, n:n + 1], half[n % 2][:, :],
                                           ALU.mult, ALU.add).then_inc(whole_ready, 1)

    @blk.tensor
    def _(pe):
        for n in range(NT):
            pe.wait_ge(whole_ready, n + 1)
            if n >= 4:
                pe.wait_ge(x1_out, n - 3)
            for k in range(KD):
                last = nc.tensor.transpose(p_x[n % 4][:, k, :], whole[n % 2][:, k * P:(k + 1) * P], ident[:, :])
            last.then_inc(x1_turned, 1)

    @blk.scalar
    def _(act):
        for n in range(NT):
            act.wait_ge(x1_turned, n + 1)
            for k in range(KD):
                dst = x1[:, k, :, PAD + n * TT:PAD + (n + 1) * TT]
                last = nc.scalar.activation(dst, p_x[n % 4][:, k, :].rearrange("p (t b) -> p b t", b=B), ACT.Copy)
            last.then_inc(x1_out, 1)


NS = 64
TAPS = B
PAIR = 2
NP_ = B // PAIR
C2 = PAIR * L
LX = L + 1


def state_scan(nc, ctx, mem, A):
    sb = lambda n, s, d=F32: ctx.enter_context(nc.sbuf_tensor(n, s, d))
    pb = lambda n, s: ctx.enter_context(nc.psum_tensor(n, s, F32))
    sem = lambda n: ctx.enter_context(nc.semaphore(n))
    x1, x2 = mem["x1"], mem["x2"]
    wp = sb("wp", [P, KD, 2 * NS]); wpk = sb("wpk", [P, TAPS, 2 * NS])
    ws = sb("ws", [P, KD, NS]); wo_s = sb("wo_s", [NS, D])
    cnd = sb("cnd2", [P, KD, TAPS]); cb = sb("cb", [P, KD]); bp = sb("bp", [P, 1]); bs = sb("bs", [NS, 1]); bo = sb("bo", [P, KD])
    logs = sb("logs", [NS, 2]); sp_a = sb("sp_a", [NS, 2]); sp_e = sb("sp_e", [NS, 2]); sp_l = sb("sp_l", [NS, 2]); sp_v = sb("sp_v", [NS, 2])
    prod = sb("prod", [NS, 1]); decay = sb("decay", [NS, L]); bias = sb("bias_bc", [P, 1])
    acc = [[sb(f"acc{q}_{r}", [P, PAIR, L]) for r in range(2)] for q in range(2)]
    conv = [sb(f"conv{q}", [P, PAIR, L]) for q in range(2)]
    zz = [sb(f"zz{q}", [NS, C2]) for q in range(2)]; az = sb("az", [NS, C2]); ez = sb("ez", [NS, C2]); lz = [sb(f"lz{q}", [NS, C2]) for q in range(2)]
    ct = [sb(f"ct{q}", [NS, C2]) for q in range(2)]; uu = [sb(f"uu{q}", [NS, C2]) for q in range(2)]
    rz = sb("rz", [NS, C2]); bt = sb("bt", [NS, C2]); d1 = sb("d1", [NS, C2]); st = sb("st", [NS, C2])
    yy = [sb(f"yy{q}", [NS, C2]) for q in range(2)]
    p_bc = [pb(f"p_bc{q}", [P, C2]) for q in range(2)]
    p_u = [pb(f"p_u{q}", [NS, C2]) for q in range(2)]
    p_2 = [pb(f"p_2{q}", [P, PAIR, L]) for q in range(3)]
    p_b = pb("p_b", [P, 1])
    loaded, setup, bias_sum, bias_ready = sem("scan_loaded"), sem("scan_setup"), sem("bias_sum"), sem("bias_ready")
    sp_step = sem("sp_step")
    part, conv_ready, bc_sum, u_sum = sem("part"), sem("conv_ready"), sem("bc_sum"), sem("u_sum")
    z_ready, abs_ready, exp_ready, ln_ready, ct_ready, u_ready = sem("z_ready"), sem("abs_ready"), sem("exp_ready"), sem("ln_ready"), sem("ct_ready"), sem("u_ready")
    relu_ready, b_ready, d_ready, st_ready, yy_ready = sem("relu_ready"), sem("b_ready"), sem("d_ready"), sem("st_ready"), sem("yy_ready")
    x2_sum, x2_ready, zeroed, saved = sem("x2_sum"), sem("x2_ready"), sem("x2_zeroed"), sem("x1_saved")
    blk = ctx.enter_context(nc.Block())
    col = lambda a: a.rearrange("(k p) -> p k", p=P)
    LOADS = 10

    def tap(k, i, t):
        return x1[:, k, bass.ds(i * PAIR, PAIR), t:t + L]

    @blk.sync
    def _(sp):
        for d, s in ((wp[:, :, :], A["L1_cond_Wp"].rearrange("(k p) n -> p k n", p=P)),
                     (ws[:, :, :], A["L1_cond_Ws"].rearrange("(k p) n -> p k n", p=P)),
                     (wo_s[:, :], A["L1_cond_Wo"]),
                     (cnd[:, :, :], A["condT"].rearrange("(k p) b -> p k b", p=P)),
                     (cb[:, :], A["conv_bT"]), (bp[:, :], A["bpT"]), (bs[:, :], A["bsT"]), (bo[:, :], A["boT"]),
                     (logs[:, 0:1], A["A_logT"]), (logs[:, 1:2], A["dt_logT"])):
            sp.dma_start(d, s).then_inc(loaded, 16)
        for k in range(KD):
            sp.dma_start(mem["x1_dram"][k], x1[:, k, :, PAD:LP]).then_inc(saved, 16)
        sp.wait_ge(saved, 32)

    @blk.gpsimd
    def _(pool):
        pool.memset(x2[:, :, :, 0:1], 0.0).then_inc(zeroed, 1)

    @blk.scalar
    def _(act):
        act.wait_ge(loaded, 16 * LOADS)
        act.activation(sp_a[:, :], logs[:, :], ACT.Abs).then_inc(sp_step, 1)
        act.wait_ge(sp_step, 1)
        act.activation(sp_e[:, :], sp_a[:, :], ACT.Exp, scale=-1.0).then_inc(sp_step, 1)
        act.wait_ge(sp_step, 2)
        act.activation(sp_l[:, :], sp_e[:, :], ACT.Ln, bias=1.0).then_inc(sp_step, 1)
        act.wait_ge(bias_ready, 1)

        def body(i, q):
            n = 2 * i + q
            act.wait_ge(bc_sum, n + 1)
            act.wait_ge(yy_ready, n + 1)
            nc.scalar.activation(zz[q][:, :], p_bc[q][0:NS, :], ACT.Identity, bias=bias[0:NS, :]).then_inc(z_ready, 1)
            nc.scalar.activation(ct[q][:, :], p_bc[q][NS:P, :], ACT.Tanh, bias=bias[NS:P, :]).then_inc(ct_ready, 1)
            act.wait_ge(z_ready, n + 1)
            nc.scalar.activation(az[:, :], zz[q][:, :], ACT.Abs).then_inc(abs_ready, 1)
            act.wait_ge(abs_ready, n + 1)
            nc.scalar.activation(ez[:, :], az[:, :], ACT.Exp, scale=-1.0).then_inc(exp_ready, 1)
            act.wait_ge(exp_ready, n + 1)
            nc.scalar.activation(lz[q][:, :], ez[:, :], ACT.Ln, bias=1.0).then_inc(ln_ready, 1)
            act.wait_ge(u_sum, n + 1)
            nc.scalar.activation(uu[q][:, :], p_u[q][:, :], ACT.Identity, bias=bs[:, :]).then_inc(u_ready, 1)

        def out(i, q):
            n = 2 * i + q
            for m in range(KD):
                act.wait_ge(x2_sum, 2 * n + m + 2)
                nc.scalar.activation(x2[:, m, bass.ds(n * PAIR, PAIR), 1:LX], p_2[m][:, :, :],
                                     ACT.Identity, bias=bo[:, m:m + 1]).then_inc(x2_ready, 1)

        with act.Fori(0, NP_ // 2) as i:
            for q in range(2):
                body(i, q)
                out(i, q)

    @blk.vector
    def _(dve):
        V = nc.vector
        dve.wait_ge(loaded, 16 * LOADS)
        for k in range(TAPS):
            V.tensor_scalar(wpk[:, k, :], wp[:, 1, :], cnd[:, 1, k:k + 1], None, ALU.mult).then_inc(setup, 1)
        V.memset(decay[:, :], 1.0).then_inc(setup, 1)
        V.tensor_scalar(sp_v[:, :], logs[:, :], 0.0, None, ALU.max).then_inc(setup, 1)
        dve.wait_ge(sp_step, 3)
        dve.wait_ge(setup, TAPS + 2)
        V.tensor_tensor(sp_v[:, :], sp_v[:, :], sp_l[:, :], ALU.add).then_inc(setup, 1)
        dve.wait_ge(setup, TAPS + 3)
        V.tensor_scalar(prod[:, :], sp_v[:, 0:1], sp_v[:, 1:2], -1.0, ALU.mult, ALU.mult).then_inc(setup, 1)
        dve.wait_ge(setup, TAPS + 4)
        V.tensor_scalar(prod[:, :], prod[:, :], 1.0, None, ALU.add).then_inc(setup, 1)
        dve.wait_ge(setup, TAPS + 5)
        V.tensor_scalar(decay[:, :], decay[:, :], prod[:, 0:1], None, ALU.mult).then_inc(setup, 1)
        dve.wait_ge(bias_sum, 1)
        V.tensor_tensor(bias[:, :], p_b[:, :], bp[:, :], ALU.add).then_inc(bias_ready, 1)

        def convolve(i, q):
            n = 2 * i + q
            for k in range(TAPS):
                a = acc[k % 2]
                if k < 2:
                    if k == 0:
                        V.tensor_scalar(a[0][:, :, :], tap(0, i * 2 + q, k), cnd[:, 0, k:k + 1], cb[:, 0:1], ALU.mult, ALU.add).then_inc(part, 1)
                    else:
                        V.tensor_scalar(a[0][:, :, :], tap(0, i * 2 + q, k), cnd[:, 0, k:k + 1], None, ALU.mult).then_inc(part, 1)
                else:
                    dve.wait_ge(part, TAPS * n + k - 1)
                    V.scalar_tensor_tensor(a[(k // 2) % 2][:, :, :], tap(0, i * 2 + q, k), cnd[:, 0, k:k + 1],
                                           a[1 - (k // 2) % 2][:, :, :], ALU.mult, ALU.add).then_inc(part, 1)
            dve.wait_ge(part, TAPS * n + TAPS)
            r = (TAPS // 2 - 1) % 2
            V.tensor_tensor(conv[q][:, :, :], acc[0][r][:, :, :], acc[1][r][:, :, :], ALU.add).then_inc(conv_ready, 1)

        def step(i, q):
            n = 2 * i + q
            dve.wait_ge(z_ready, n + 1)
            V.tensor_scalar(rz[:, :], zz[q][:, :], 0.0, None, ALU.max).then_inc(relu_ready, 1)
            dve.wait_ge(relu_ready, n + 1)
            dve.wait_ge(ln_ready, n + 1)
            V.tensor_tensor(bt[:, :], rz[:, :], lz[q][:, :], ALU.add).then_inc(b_ready, 1)
            dve.wait_ge(b_ready, n + 1)
            dve.wait_ge(u_ready, n + 1)
            V.scalar_tensor_tensor(d1[:, :], bt[:, :], sp_v[:, 1:2], uu[q][:, :], ALU.mult, ALU.mult).then_inc(d_ready, 1)
            dve.wait_ge(d_ready, n + 1)
            for s in range(PAIR):
                w = slice(s * L, (s + 1) * L)
                last = V.tensor_tensor_scan(st[:, w], decay[:, :], d1[:, w], 0.0, ALU.mult, ALU.add)
            last.then_inc(st_ready, 1)
            dve.wait_ge(st_ready, n + 1)
            dve.wait_ge(ct_ready, n + 1)
            dve.wait_ge(x2_sum, 2 * n + 1)
            V.tensor_tensor(yy[q][:, :], st[:, :], ct[q][:, :], ALU.mult).then_inc(yy_ready, 1)

        V.sem_inc(yy_ready, 2)
        V.sem_inc(x2_sum, 1)
        convolve(0, 0)
        with dve.Fori(0, NP_ // 2 - 1) as i:
            convolve(i, 1)
            step(i, 0)
            convolve(i + 1, 0)
            step(i, 1)
        i = NP_ // 2 - 1
        convolve(i, 1)
        step(i, 0)
        step(i, 1)

    @blk.tensor
    def _(pe):
        pe.wait_ge(loaded, 16 * LOADS)
        nc.tensor.matmul(p_b[:, :], wp[:, 1, :], cb[:, 1:2], start=True, stop=True).then_inc(bias_sum, 1)
        pe.wait_ge(setup, TAPS)

        def project(i, q):
            n = 2 * i + q
            pe.wait_ge(yy_ready, n + 1)
            for k in range(TAPS):
                nc.tensor.matmul(p_bc[q][:, :], wpk[:, k, :], tap(1, n, k), start=(k == 0), stop=False)
            pe.wait_ge(conv_ready, n + 1)
            nc.tensor.matmul(p_bc[q][:, :], wp[:, 0, :], conv[q][:, :, :], start=False, stop=True).then_inc(bc_sum, 1)
            for k in range(KD):
                last = nc.tensor.matmul(p_u[q][:, :], ws[:, k, :], tap(k, n, PAD), start=(k == 0), stop=(k == KD - 1))
            last.then_inc(u_sum, 1)

        def out(i, q):
            n = 2 * i + q
            pe.wait_ge(yy_ready, n + 3)
            pe.wait_ge(x2_ready, 2 * n + 1)
            for m in range(KD):
                nc.tensor.matmul(p_2[m][:, :, :], wo_s[:, m * P:(m + 1) * P], yy[q][:, :], start=True, stop=True).then_inc(x2_sum, 1)

        pe.sem_inc(x2_ready, 1)
        project(0, 0)
        with pe.Fori(0, NP_ // 2 - 1) as i:
            project(i, 1)
            out(i, 0)
            project(i + 1, 0)
            out(i, 1)
        i = NP_ // 2 - 1
        project(i, 1)
        out(i, 0)
        out(i, 1)


DEPTH = 2
HEADS = 8
DH = 64
INNER = HEADS * DH
WIN = 128
HC = INNER // P
FF = int(D * 4 * 2 / 3)
FK = -(-FF // P)
FSZ = [min(P, FF - c * P) for c in range(FK)]
WINS = L // WIN
NQ = PAIR * WINS
UNITS = PAIR * HEADS
SC = 3 * WIN
QK_SCALE = 8.0
NEVER = -1e30


def transformer(nc, ctx, mem, A):
    sem = lambda n: ctx.enter_context(nc.semaphore(n))
    x2, ident = mem["x2"], mem["ident"]
    place = {}

    def sb(n, s, d=F32):
        t = ctx.enter_context(nc.sbuf_tensor(n, s, d))
        place[n] = nc.sbuf_base - 4 * int(np.prod(s[1:]))
        return t

    def over(n, below, s, d=F32):
        return nc.alloc_sbuf_tensor_at(n, s, d, offset=place[below])

    def split(n, s):
        hi, lo = sb(n + "_hi", s, F32R), sb(n + "_lo", s, F32R)
        return [hi, lo, over(n + "_raw", n + "_lo", s)]

    wqkv = split("wqkv", [P, KD, 3 * INNER]); wo = split("wo_a", [P, HC, D])
    w1 = split("w1f", [P, KD, 2 * FF]); w2 = split("w2f", [P, FK, D])
    b1 = sb("b1f", [P, DEPTH, 2 * FK]); b2 = sb("b2f", [P, DEPTH, KD]); lgb = sb("lgb", [P, DEPTH, 2, KD])
    b1e = sb("b1e", [P, 2 * FK])
    tabs = sb("rot_tabs", [P, 2, 2, WINS, DH])
    qks = sb("qk_scales", [P, DEPTH, 2, DH])
    tab = sb("tab", [P, 2, 2, WINS, DH])
    mask = sb("mask", [P, SC]); mean_w = sb("mean_w", [P, P]); eps = sb("eps", [P, 1])
    hs = split("hs", [P, KD, PAIR, LX])
    qk_rows = [sb(f"qk_rows{w}", [P, NQ, INNER]) for w in range(2)]
    qk = [[qk_rows[w][:, t, :] for w in range(2)] for t in range(NQ)]
    oT = [over(f"oT_{h}", f"qk_rows{w}", [P, HC, C2], F32R) for w, h in enumerate(("hi", "lo"))]
    rs = [sb(f"rs{q}", [P, INNER]) for q in range(2)]
    sq = [sb(f"sq{q}", [P, INNER]) for q in range(2)]
    ss = sb("ss", [P, NQ, 2, HEADS]); nrm = sb("nrm", [P, NQ, 2, HEADS]); rn = sb("rn", [P, NQ, 2, HEADS])
    vv = [sb(f"vv{t}", [P, INNER]) for t in range(NQ)]
    qkT = [sb(f"qkT{w}", [P, HC, C2]) for w in range(2)]
    sm = [sb(f"sm{q}", [P, SC]) for q in range(3)]
    mx = sb("mx", [P, 3, 2]); rsum = sb("rsum", [P, 2, UNITS]); rinv = sb("rinv", [P, 2, UNITS])
    pr = [sb(f"pr{q}", [P, SC]) for q in range(3)]
    pT = [sb(f"pT{q}", [P, 3, WIN]) for q in range(2)]
    on = sb("on", [P, NQ, INNER])
    gg = [on[:, q, :] for q in range(2)]
    lnv, rstd, xc = on[:, 0, :], on[:, 1, :], on[:, 2:4, :]
    xn = split("xn", [P, KD, C2])
    sqx = xn[2]
    own = split("hh", [P, FK - 2, C2])
    hh = [[own[h][:, c, :] for c in range(FK - 2)] for h in range(3)]
    for q in range(2):
        hh[0].append(over(f"hh_hi_{q}", f"sq{q}", [P, C2], F32R)[:, :])
        hh[1].append(over(f"hh_lo_{q}", f"rs{q}", [P, C2], F32R)[:, :])
        hh[2].append(rs[q][:, :])
    bank = [ctx.enter_context(nc.psum_tensor(f"bank{q}", [P, 512], F32)) for q in range(8)]
    O_BANKS = [[5, 6], [5, 2]]
    DOWN_BANKS = [7, 6]
    TURN_BANKS = [6, 6, 3, 4]
    TURN_BEATS = {12: 0, 13: 1}

    cst_in, cst_ready = sem("tr_cst_in"), sem("tr_cst_ready")
    wqkv_in, wo_in, w1_in, w2_in = sem("wqkv_in"), sem("wo_in"), sem("tr_w1_in"), sem("tr_w2_in")
    wqkv_ready, wo_ready, w1_ready, w2_ready = sem("wqkv_ready"), sem("wo_ready"), sem("w1_ready"), sem("w2_ready")
    hs_step, xn_step, rn_step = sem("hs_step"), sem("xn_step"), sem("rn_step")
    oT_hi, hh_hi, hh_raw = sem("oT_hi"), sem("hh_hi"), sem("hh_raw")
    tab_ready, b1_sum, b1_ready = sem("tab_ready"), sem("b1_sum"), sem("b1_ready")
    hs_ready, qkv_done, sq_ready, rot_ready = sem("hs_ready"), sem("qkv_done"), sem("sq_ready"), sem("rot_ready")
    ss_ready, nrm_ready, rn_ready = sem("ss_ready"), sem("nrm_ready"), sem("rn_ready")
    added, normed, v_ready = sem("added"), sem("normed"), sem("v_ready")
    qk_turned, qkT_ready = sem("qk_turned"), sem("qkT_ready")
    waits_taken = sem("waits_taken")
    s_done, sm_ready, probs_ready, pt_done, pt_out, pv_done = (sem(n) for n in ("s_done", "sm_ready", "probs_ready", "pt_done", "pt_out", "pv_done"))
    rinv_ready, on_ready, o_turned, oT_ready, wo_done, xmid_ready = (sem(n) for n in ("rinv_ready", "on_ready", "o_turned", "oT_ready", "wo_done", "xmid_ready"))
    mean_done, xc_ready, sqx_ready, var_done, lnv_ready, rstd_ready, xn_ready = (sem(n) for n in ("mean_done", "xc_ready", "sqx_ready", "var_done", "lnv_ready", "rstd_ready", "xn_ready"))
    g_done, a_done, g_ready, hh_ready, w2_done, x_done = (sem(n) for n in ("g_done", "a_done", "g_ready", "hh_ready", "w2_done", "x_done"))

    def wait(e, s, v):
        if not isinstance(v, int) or v > 0:
            e.wait_ge(s, v)

    def x_mid(m, p, shifted=0):
        return x2[:, m, bass.ds(p * PAIR, PAIR), 1 - shifted:LX - shifted]

    pair = lambda a: a.rearrange("p (s t) -> p s t", s=PAIR)
    heads = lambda a: a.rearrange("p (h d) -> p h d", h=HEADS)
    QB = lambda m: m % 5

    def turns(e, body):
        body(0, (0, 0), None)
        for l in range(DEPTH):
            with e.Fori(1, NP_) as j:
                body(j + l * NP_, (l, j), (l, j - 1))
            body((l + 1) * NP_, (l + 1, 0) if l + 1 < DEPTH else None, (l, NP_ - 1))

    HALVES = ((0, 0), (0, 1), (1, 0))

    def split_weights(e, v, w, loaded, n_loaded, ready, l):
        parts = [(P, slice(0, w[0].shape[1]))]
        if w is w2:
            parts = [(P, slice(0, FK - 1)), (FSZ[-1], slice(FK - 1, FK))]
        e.wait_ge(loaded, n_loaded)
        for rows, c in parts:
            v.tensor_copy(w[0][0:rows, c, :], w[2][0:rows, c, :]).then_inc(ready, 1)
        e.wait_ge(ready, (2 * l + 1) * len(parts))
        for rows, c in parts:
            v.tensor_tensor(w[1][0:rows, c, :], w[2][0:rows, c, :], w[0][0:rows, c, :].bitcast(F32), ALU.subtract).then_inc(ready, 1)

    blk = ctx.enter_context(nc.Block())

    @blk.sync
    def _(sp):
        def load_wqkv(l):
            sp.dma_start(wqkv[2][:, :, :], A["L1_ffn_wqkv"][l].rearrange("(k p) n -> p k n", p=P)).then_inc(wqkv_in, 16)

        def load_wo(l):
            sp.dma_start(wo[2][:, :, :], A["L1_ffn_wo"][l].rearrange("(k p) n -> p k n", p=P)).then_inc(wo_in, 16)

        def load_w1(l):
            sp.dma_start(w1[2][:, :, :], A["L1_ffn_w1"][l].rearrange("(k p) n -> p k n", p=P)).then_inc(w1_in, 16)

        def load_w2(l):
            full = (FK - 1) * P
            sp.dma_start(w2[2][:, 0:FK - 1, :], A["L1_ffn_w2"][l][0:full].rearrange("(k p) n -> p k n", p=P)).then_inc(w2_in, 16)
            sp.dma_start(w2[2][0:FF - full, FK - 1, :], A["L1_ffn_w2"][l][full:FF]).then_inc(w2_in, 16)

        load_wqkv(0)
        for d, s in ((tabs[:, :, :, :, :], A["rot_tabs"]), (qks[:, :, :, :], A["qk_scales"].rearrange("l w d -> (l w d)").unsqueeze(0).broadcast_to([P, DEPTH * 2 * DH])),
                     (mask[:, :], A["mask"]), (b1[:, :, :], A["b1f"]), (b2[:, :, :], A["b2f"]), (lgb[:, :, :, :], A["lgb"])):
            if len(d.shape) > 2 and len(s.shape) == 2:
                d = d.rearrange("p l w d -> p (l w d)")
            sp.dma_start(d, s).then_inc(cst_in, 16)
        load_wo(0)
        load_w1(0)
        load_w2(0)
        sp.wait_ge(qkv_done, 12 * NP_)
        load_wqkv(1)
        sp.wait_ge(wo_done, 2 * NP_)
        load_wo(1)
        sp.wait_ge(a_done, FK * NP_)
        sp.wait_ge(g_done, FK * NP_)
        sp.wait_ge(b1_sum, 1)
        load_w1(1)
        sp.wait_ge(w2_done, 2 * NP_ + 1)
        load_w2(1)

    @blk.gpsimd
    def _(pool):
        pool.memset(mean_w[:, :], 1.0 / D).then_inc(cst_ready, 1)
        pool.memset(eps[:, :], 1e-5).then_inc(cst_ready, 1)

        def body(n, att, ffn):
            if att is None:
                return
            l, p = att
            wait(pool, qkv_done, 12 * n)
            if l and isinstance(n, int):
                split_weights(pool, nc.gpsimd, wqkv, wqkv_in, 32, wqkv_ready, 1)
            if l:
                wait(pool, x_done, 2 * (n - NP_ + 1) + 1)
            hi, lo, raw = hs
            for k in range(KD):
                last = nc.gpsimd.tensor_copy(raw[:, k, :, :], x2[:, k, bass.ds(p * PAIR, PAIR), :])
            last.then_inc(hs_step, 1)
            pool.wait_ge(hs_step, 2 * n + 1)
            pool.sem_inc(waits_taken, 1)
            nc.gpsimd.tensor_copy(hi[:, :, :, :], raw[:, :, :, :]).then_inc(hs_step, 1)
            pool.wait_ge(hs_step, 2 * n + 2)
            nc.gpsimd.tensor_tensor(lo[:, :, :, :], raw[:, :, :, :], hi[:, :, :, :].bitcast(F32), ALU.subtract).then_inc(hs_ready, 1)
            for m in range(2 * NQ):
                pool.wait_ge(rot_ready, 8 * n + m + 1)
                t = qk[m // 2][m % 2]
                nc.gpsimd.tensor_tensor(t, t, rs[m % 2][:, :], ALU.add).then_inc(added, 1)
            pool.wait_ge(rn_ready, n + 1)
            for m in range(2 * NQ):
                pool.wait_ge(added, 8 * n + m + 1)
                t = qk[m // 2][m % 2]
                nc.gpsimd.tensor_tensor(heads(t), heads(t), rn[:, m // 2, m % 2, :].unsqueeze(2).broadcast_to([P, HEADS, DH]), ALU.mult).then_inc(normed, 1)
            if isinstance(n, int):
                split_weights(pool, nc.gpsimd, wo, wo_in, 16 * (l + 1), wo_ready, l)
                split_weights(pool, nc.gpsimd, w1, w1_in, 16 * (l + 1), w1_ready, l)

        turns(pool, body)

    @blk.tensor
    def _(pe):
        mm, tr = nc.tensor.matmul, nc.tensor.transpose

        def qkv_products(n, ffn):
            pe.wait_ge(hs_ready, n + 1)
            for m in range(3 * NQ):
                if m == 2 and ffn is not None:
                    variance(n - 1)
                t, w = divmod(m, 3)
                if m < 5:
                    wait(pe, *[(xmid_ready, 2 * n), (xmid_ready, 2 * n), (on_ready, 4 * n), (xc_ready, 2 * n), (lnv_ready, n)][m])
                else:
                    t0, w0 = divmod(m - 5, 3)
                    if w0 == 2:
                        pe.wait_ge(v_ready, NQ * n + t0 + 1)
                    else:
                        pe.wait_ge(rot_ready, 8 * n + 2 * t0 + w0 + 1)
                s, win = divmod(t, WINS)
                for k in range(KD):
                    for a, b in HALVES:
                        tok = hs[a][:, k, s, 1 - k + win * WIN:1 - k + (win + 1) * WIN]
                        last = mm(bank[QB(m)][:, :], tok, wqkv[b][:, k, w * INNER:(w + 1) * INNER],
                                  start=(k == 0 and a + b == 0), stop=(k == KD - 1 and a == 1))
                last.then_inc(qkv_done, 1)

        def ffn_up(f):
            pe.wait_ge(xn_ready, f + 1)
            for c in range(FK):
                for half in (1, 0):
                    if half:
                        if c == 0:
                            pe.wait_ge(on_ready, 4 * f + 4)
                        elif c == 1:
                            pe.wait_ge(x_done, 2 * f + 1)
                        else:
                            pe.wait_ge(g_ready, FK * f + c - 1)
                    else:
                        if c == 0:
                            pe.wait_ge(x_done, 2 * f + 1)
                        else:
                            pe.wait_ge(hh_raw, FK * f + c + 1)
                    out = bank[5 + c % 2 if half else 7][0:FSZ[c], :]
                    o = half * FF + c * P
                    for k in range(KD):
                        for a, b in HALVES:
                            last = mm(out, w1[a][:, k, o:o + FSZ[c]], xn[b][:, k, :], start=(k == 0 and a + b == 0), stop=(k == KD - 1 and a == 1))
                    last.then_inc(g_done if half else a_done, 1)

        def ffn_down(f, m, c0, c1, attends=True):
            if c0 == 0:
                pe.wait_ge(hh_ready, FK * f + FK + 1)
                if m == 1:
                    pe.wait_ge(oT_ready, 4 * f + 4 + 2) if attends else pe.wait_ge(g_ready, FK * f + FK)
            for c in range(c0, c1):
                for a, b in HALVES:
                    last = mm(bank[DOWN_BANKS[m]][:, :], w2[a][0:FSZ[c], c, m * P:(m + 1) * P], hh[b][c][0:FSZ[c], :],
                              start=(c == 0 and a + b == 0), stop=(c == FK - 1 and a == 1))
            if c1 == FK:
                last.then_inc(w2_done, 1)

        def turn_qk(n):
            pe.wait_ge(rot_ready, 8 * n + 8)
            pe.wait_ge(v_ready, NQ * n + NQ)
            for m in range(2 * NQ):
                pe.wait_ge(normed, 8 * n + m + 1)
                if m >= 4:
                    pe.wait_ge(qkT_ready, 8 * n + m - 3)
                for c in range(HC):
                    last = tr(bank[1 + m % 4][:, c * P:(c + 1) * P], qk[m // 2][m % 2][:, c * P:(c + 1) * P], ident[:, :])
                last.then_inc(qk_turned, 1)

        def scores(n, u):
            s, h = divmod(u, HEADS)
            if u >= 2:
                pe.wait_ge(sm_ready, UNITS * n + u - 1)
            r = slice(DH * (h % 2), DH * (h % 2) + DH)
            q, k = qkT[0][r, h // 2, :], qkT[1][r, h // 2, :]
            b = s * L
            mm(bank[u % 2][:, 0:WIN], q[:, b:b + WIN], k[:, b:b + WIN], start=True, stop=True)
            mm(bank[u % 2][:, WIN:SC], q[:, b + WIN:b + L], k[:, b:b + L], start=True, stop=True).then_inc(s_done, 1)

        def turn_probs(n, u):
            pe.wait_ge(probs_ready, UNITS * n + u + 1)
            if u >= 2:
                pe.wait_ge(pt_out, UNITS * n + u - 1)
            for c in range(3):
                last = tr(bank[3 + u % 2][:, c * P:(c + 1) * P], pr[u % 3][:, c * P:(c + 1) * P], ident[:, :])
            last.then_inc(pt_done, 1)

        def values(n, u):
            s, h = divmod(u, HEADS)
            pe.wait_ge(pt_out, UNITS * n + u + 1)
            if u == 0:
                wait(pe, g_ready, FK * n)
            if u == HEADS:
                pe.wait_ge(on_ready, 4 * n + 1)
            hd = slice(h * DH, (h + 1) * DH)
            t = pT[u % 2]
            mm(bank[O_BANKS[s][0]][:, hd], t[:, 0, :], vv[2 * s][:, hd], start=True, stop=True)
            mm(bank[O_BANKS[s][1]][:, hd], t[:, 1, :], vv[2 * s][:, hd], start=True, stop=False)
            mm(bank[O_BANKS[s][1]][:, hd], t[:, 2, :], vv[2 * s + 1][:, hd], start=False, stop=True).then_inc(pv_done, 1)

        def turn_o(n, q):
            pe.wait_ge(on_ready, 4 * n + q + 1)
            if q == 0:
                pe.wait_ge(on_ready, 4 * n + 2)
            elif q == 1:
                pe.wait_ge(oT_ready, 4 * n + 1)
            else:
                pe.wait_ge(pt_out, UNITS * n + UNITS)
            for c in range(HC):
                last = tr(bank[TURN_BANKS[q]][:, c * P:(c + 1) * P], on[:, q, c * P:(c + 1) * P], ident[:, :])
            last.then_inc(o_turned, 1)

        def project(n, s):
            pe.wait_ge(oT_ready, 4 * n + 2 * s + 2)
            pe.wait_ge(sm_ready, UNITS * n + UNITS)
            cols = slice(s * L, (s + 1) * L)
            for m in range(KD):
                for c in range(HC):
                    for a, b in HALVES:
                        last = mm(bank[m][:, cols], wo[a][:, c, m * P:(m + 1) * P], oT[b][:, c, cols],
                                  start=(c == 0 and a + b == 0), stop=(c == HC - 1 and a == 1))
                if s:
                    last.then_inc(wo_done, 1)

        def mean(n, p):
            pe.wait_ge(xmid_ready, 2 * n + 2)
            for k in range(KD):
                last = mm(pair(bank[3][:, :]), mean_w[:, :], x_mid(k, p, k), start=(k == 0), stop=(k == KD - 1))
            last.then_inc(mean_done, 1)

        def variance(n):
            pe.wait_ge(sqx_ready, n + 1)
            for k in range(KD):
                last = mm(bank[4][:, :], mean_w[:, :], sqx[:, k, :], start=(k == 0), stop=(k == KD - 1))
            last.then_inc(var_done, 1)

        FILL = [[0, 2, 4, 6, 8, 11], [15, 16, 18]]

        def body(n, att, ffn):
            f = n - 1
            if att is not None:
                if isinstance(n, int):
                    pe.wait_ge(wqkv_ready, 2 * (att[0] + 1))
                qkv_products(n, ffn)
            else:
                variance(f)
            if ffn is not None:
                ffn_up(f)
            if att is not None:
                turn_qk(n)
                pe.wait_ge(qkT_ready, 8 * n + 8)
                for b in range(UNITS + 3):
                    if b < UNITS:
                        scores(n, b)
                    if ffn is not None:
                        for m in range(KD):
                            if b in FILL[m]:
                                c = FILL[m].index(b)
                                ffn_down(f, m, c, c + 1)
                    if 2 <= b < UNITS + 2:
                        turn_probs(n, b - 2)
                    if b >= 3:
                        values(n, b - 3)
                    if b in TURN_BEATS:
                        turn_o(n, TURN_BEATS[b])
            elif ffn is not None:
                ffn_down(f, 0, 0, FK, False)
            if att is not None:
                if isinstance(n, int):
                    pe.wait_ge(wo_ready, 2 * (att[0] + 1))
                project(n, 0)
                turn_o(n, 2)
                turn_o(n, 3)
                if ffn is not None:
                    ffn_down(f, 1, len(FILL[1]), FK - 1)
                project(n, 1)
                if ffn is not None:
                    ffn_down(f, 1, FK - 1, FK)
                mean(n, att[1])
            else:
                ffn_down(f, 1, 0, FK, False)
            if att is not None and isinstance(n, int):
                pe.wait_ge(w1_ready, 2 * (att[0] + 1))
                if n:
                    pe.wait_ge(x_done, 2 * f + 2)
                for j in range(2 * FK):
                    half, c = divmod(j, FK)
                    o = half * FF + c * P
                    for k in range(KD):
                        for a in range(2):
                            last = mm(bank[7][0:FSZ[c], j:j + 1], w1[a][:, k, o:o + FSZ[c]].bitcast(F32), lgb[:, att[0], 1, k:k + 1],
                                      start=(k + a == 0), stop=(k + a == KD))
                last.then_inc(b1_sum, 1)

        pe.wait_ge(cst_ready, 2)
        pe.wait_ge(cst_in, 96)
        pe.sem_inc(w2_done, 1)
        turns(pe, body)

    @blk.scalar
    def _(act):
        S = nc.scalar.activation

        def norm_values(n):
            act.wait_ge(var_done, n + 1)
            S(lnv, bank[4][:, :], ACT.Ln, bias=eps[:, :]).then_inc(lnv_ready, 1)
            act.wait_ge(lnv_ready, n + 1)
            S(rstd, lnv, ACT.Exp, scale=-0.5).then_inc(rstd_ready, 1)

        def gelus(f, c0, c1):
            for c in range(c0, c1):
                act.wait_ge(g_done, FK * f + c + 1)
                act.wait_ge(hh_raw, FK * f + max(c - 1, 0) + 1)
                S(gg[c % 2][0:FSZ[c], :], bank[5 + c % 2][0:FSZ[c], :], ACT.Gelu, bias=b1e[0:FSZ[c], FK + c:FK + c + 1]).then_inc(g_ready, 1)

        def turned_hi(n, q):
            act.wait_ge(o_turned, 4 * n + q + 1)
            S(oT[0][:, :, q * WIN:(q + 1) * WIN], bank[TURN_BANKS[q]][:, :].rearrange("p (c t) -> p c t", c=HC), ACT.Copy).then_inc(oT_hi, 1)

        def body(n, att, ffn):
            f = n - 1
            if att is not None:
                wait(act, pv_done, UNITS * n)
                for t in range(NQ):
                    for w in range(2):
                        m = 2 * t + w
                        act.wait_ge(qkv_done, 12 * n + 3 * t + w + 1)
                        wait(act, ss_ready, 8 * n + m - 1)
                        S(sq[m % 2][:, :], bank[QB(3 * t + w)][:, :], ACT.Square).then_inc(sq_ready, 1)
                    if t == 0 and ffn is not None:
                        norm_values(f)
                    act.wait_ge(qkv_done, 12 * n + 3 * t + 3)
                    S(vv[t][:, :], bank[QB(3 * t + 2)][:, :], ACT.Copy).then_inc(v_ready, 1)
            else:
                norm_values(f)
            if ffn is not None:
                act.wait_ge(b1_ready, ffn[0] + 1)
                gelus(f, 0, 2)
            if att is not None:
                act.wait_ge(ss_ready, 8 * n + 8)
                S(nrm[:, :, :, :], ss[:, :, :, :], ACT.Sqrt).then_inc(nrm_ready, 1)
            if ffn is not None:
                gelus(f, 2, FK)
            if att is None:
                return
            wait(act, s_done, UNITS * n)
            for m in range(2 * NQ):
                act.wait_ge(qk_turned, 8 * n + m + 1)
                S(qkT[m % 2][:, :, (m // 2) * WIN:(m // 2 + 1) * WIN], bank[1 + m % 4][:, :].rearrange("p (c t) -> p c t", c=HC),
                  ACT.Copy).then_inc(qkT_ready, 1)
            wait(act, on_ready, 4 * n)
            for u in range(UNITS):
                act.wait_ge(sm_ready, UNITS * n + u + 1)
                wait(act, pt_done, UNITS * n + u - 2)
                r = u % 3
                S(pr[r][:, 0:WIN], sm[r][:, 0:WIN], ACT.Exp, scale=-1.0, bias=mx[:, r, 0:1], accum_out=rsum[:, 0, u:u + 1])
                S(pr[r][:, WIN:SC], sm[r][:, WIN:SC], ACT.Exp, scale=-1.0, bias=mx[:, r, 1:2], accum_out=rsum[:, 1, u:u + 1]).then_inc(probs_ready, 1)
                if u in TURN_BEATS:
                    turned_hi(n, TURN_BEATS[u])
            for q in range(2, NQ):
                turned_hi(n, q)
            act.wait_ge(xc_ready, 2 * n + 2)
            S(sqx[:, :, :], xc, ACT.Square).then_inc(sqx_ready, 1)

        act.wait_ge(cst_ready, 2)
        turns(act, body)

    @blk.vector
    def _(dve):
        V = nc.vector

        def tables(l):
            H = DH // 2
            for w in range(2):
                ql = lambda a, b: qks[:, l, w, a:b].unsqueeze(1).broadcast_to([P, WINS, b - a])
                V.tensor_tensor(tab[:, w, 0, :, :], tabs[:, w, 0, :, :], ql(0, DH), ALU.mult)
                V.tensor_tensor(tab[:, w, 1, :, 0:H], tabs[:, w, 1, :, 0:H], ql(H, DH), ALU.mult)
                last = V.tensor_tensor(tab[:, w, 1, :, H:DH], tabs[:, w, 1, :, H:DH], ql(0, H), ALU.mult)
            last.then_inc(tab_ready, 1)
            dve.wait_ge(tab_ready, l + 1)

        def rotate(n, m):
            t, w = divmod(m, 2)
            win = t % WINS
            H = DH // 2
            src = heads(bank[QB(3 * t + w)][:, :])
            dve.wait_ge(sq_ready, 8 * n + m + 1)
            c = lambda a, b, i: tab[:, w, i, win, a:b].unsqueeze(1).broadcast_to([P, HEADS, b - a])
            V.tensor_tensor(heads(qk[t][w]), src, c(0, DH, 0), ALU.mult)
            wait(dve, added, 8 * n + m - 1)
            o = heads(rs[m % 2][:, :])
            V.tensor_tensor(o[:, :, 0:H], src[:, :, H:DH], c(0, H, 1), ALU.mult)
            V.tensor_tensor(o[:, :, H:DH], src[:, :, 0:H], c(H, DH, 1), ALU.mult).then_inc(rot_ready, 1)
            V.tensor_reduce(ss[:, t, w, :], heads(sq[m % 2][:, :]), AX.X, ALU.add).then_inc(ss_ready, 1)

        def norms(n):
            fl = lambda a: a.rearrange("p t w h -> p (t w h)")
            dve.wait_ge(nrm_ready, n + 1)
            V.tensor_scalar(nrm[:, :, :, :], nrm[:, :, :, :], 1e-12, None, ALU.max).then_inc(rn_step, 1)
            dve.wait_ge(rn_step, 2 * n + 1)
            wait(dve, normed, 8 * n)
            V.reciprocal(fl(rn[:, :, :, :]), fl(nrm[:, :, :, :])).then_inc(rn_step, 1)
            dve.wait_ge(rn_step, 2 * n + 2)
            V.tensor_scalar(rn[:, :, 0, :], rn[:, :, 0, :], QK_SCALE, None, ALU.mult).then_inc(rn_ready, 1)

        def gate(f, c):
            if c == 0:
                dve.wait_ge(w2_done, 2 * f + 1)
            dve.wait_ge(g_ready, FK * f + c + 1)
            dve.wait_ge(a_done, FK * f + c + 1)
            hi, lo, raw = (h[c][0:FSZ[c], :] for h in hh)
            V.scalar_tensor_tensor(raw, bank[7][0:FSZ[c], :], b1e[0:FSZ[c], c:c + 1], gg[c % 2][0:FSZ[c], :],
                                   ALU.add, ALU.mult).then_inc(hh_raw, 1)
            dve.wait_ge(hh_raw, FK * f + c + 2)
            V.tensor_copy(hi, raw).then_inc(hh_hi, 1)
            dve.wait_ge(hh_hi, FK * f + c + 1)
            V.tensor_tensor(lo, raw, hi.bitcast(F32), ALU.subtract).then_inc(hh_ready, 1)

        def mask_scores(n, u):
            dve.wait_ge(s_done, UNITS * n + u + 1)
            wait(dve, probs_ready, UNITS * n + u - 2)
            dve.sem_inc(waits_taken, 1)
            r = u % 3
            for w, (a, b) in enumerate(((0, WIN), (WIN, SC))):
                last = V.tensor_tensor_reduce(out=sm[r][:, a:b], in0=bank[u % 2][:, a:b], in1=mask[:, a:b], scale=-1.0, scalar=3e38,
                                              op0=ALU.add, op1=ALU.min, accum_out=mx[:, r, w:w + 1])
            last.then_inc(sm_ready, 1)

        def probs_out(n, u):
            dve.wait_ge(pt_done, UNITS * n + u + 1)
            wait(dve, pv_done, UNITS * n + u - 1)
            V.tensor_copy(pT[u % 2][:, :, :], bank[3 + u % 2][:, 0:SC].rearrange("p (c t) -> p c t", c=3)).then_inc(pt_out, 1)

        def normalise(n, s, w):
            us = slice(s * HEADS, (s + 1) * HEADS)
            if w == 0:
                dve.wait_ge(pv_done, UNITS * n + (s + 1) * HEADS)
                if s == 0:
                    wait(dve, o_turned, 4 * n)
                V.reciprocal(rinv[:, :, us], rsum[:, :, us]).then_inc(rinv_ready, 1)
                dve.wait_ge(rinv_ready, 2 * n + s + 1)
            V.tensor_tensor(heads(on[:, 2 * s + w, :]), heads(bank[O_BANKS[s][w]][:, :]),
                            rinv[:, w, us].unsqueeze(2).broadcast_to([P, HEADS, DH]), ALU.mult).then_inc(on_ready, 1)

        def result_lo(n, q):
            dve.wait_ge(oT_hi, 4 * n + q + 1)
            cols = slice(q * WIN, (q + 1) * WIN)
            V.tensor_tensor(oT[1][:, :, cols], bank[TURN_BANKS[q]][:, :].rearrange("p (c t) -> p c t", c=HC), oT[0][:, :, cols].bitcast(F32),
                            ALU.subtract).then_inc(oT_ready, 1)

        def residual(n, p):
            for m in range(KD):
                dve.wait_ge(wo_done, 2 * n + m + 1)
                V.tensor_tensor(x_mid(m, p), pair(bank[m][:, :]), x_mid(m, p), ALU.add).then_inc(xmid_ready, 1)

        def centre(n, p):
            dve.wait_ge(mean_done, n + 1)
            dve.wait_ge(xmid_ready, 2 * n + 2)
            for k in range(KD):
                V.tensor_tensor(pair(xc[:, k, :]), x_mid(k, p, k), pair(bank[3][:, :]), ALU.subtract).then_inc(xc_ready, 1)

        def scale(n, l):
            dve.wait_ge(rstd_ready, n + 1)
            hi, lo, raw = xn
            for k in range(KD):
                V.scalar_tensor_tensor(raw[:, k, :], xc[:, k, :], lgb[:, l, 0, k:k + 1], rstd, ALU.mult, ALU.mult).then_inc(xn_step, 1)
            dve.wait_ge(xn_step, 3 * n + 2)
            V.tensor_copy(hi[:, :, :], raw[:, :, :]).then_inc(xn_step, 1)
            dve.wait_ge(xn_step, 3 * n + 3)
            V.tensor_tensor(lo[:, :, :], raw[:, :, :], hi[:, :, :].bitcast(F32), ALU.subtract).then_inc(xn_ready, 1)

        def finish(f, l, p, m):
            dve.wait_ge(w2_done, 2 * f + m + 2)
            V.scalar_tensor_tensor(x_mid(m, p), pair(bank[DOWN_BANKS[m]][:, :]), b2[:, l, m:m + 1], x_mid(m, p), ALU.add, ALU.add).then_inc(x_done, 1)

        def body(n, att, ffn):
            f = n - 1
            if att is not None:
                if isinstance(n, int):
                    tables(att[0])
                wait(dve, qk_turned, 8 * n)
                for m in range(2 * NQ):
                    rotate(n, m)
                    if ffn is not None and m == 3:
                        scale(f, ffn[0])
                    if ffn is not None and m == 2 * NQ - 2:
                        gate(f, 0)
                if ffn is not None:
                    gate(f, 1)
                norms(n)
            else:
                scale(f, ffn[0])
            if ffn is not None:
                for c in range(2 if att is not None else 0, FK):
                    if c == FK - 2 and att is not None:
                        dve.wait_ge(added, 8 * n + 8)
                    gate(f, c)
            if att is not None:
                for b in range(UNITS + 2):
                    if b == HEADS + 3:
                        normalise(n, 0, 0)
                    if b < UNITS:
                        mask_scores(n, b)
                    if b >= 2:
                        probs_out(n, b - 2)
                    if b == HEADS + 3:
                        normalise(n, 0, 1)
                    if b - 1 in TURN_BEATS:
                        result_lo(n, TURN_BEATS[b - 1])
                for w in range(WINS):
                    normalise(n, 1, w)
                for q in range(2, NQ):
                    result_lo(n, q)
            if ffn is not None:
                finish(f, ffn[0], ffn[1], 0)
            if att is not None:
                residual(n, att[1])
                centre(n, att[1])
            if ffn is not None:
                finish(f, ffn[0], ffn[1], 1)
            if att is not None and isinstance(n, int):
                dve.wait_ge(b1_sum, att[0] + 1)
                V.tensor_tensor(b1e[:, 0:FK - 1], bank[7][:, 0:FK - 1], b1[:, att[0], 0:FK - 1], ALU.add)
                V.tensor_tensor(b1e[:, FK:2 * FK - 1], bank[7][:, FK:2 * FK - 1], b1[:, att[0], FK:2 * FK - 1], ALU.add)
                z = FSZ[-1]
                V.tensor_tensor(b1e[0:z, FK - 1:2 * FK:FK], bank[7][0:z, FK - 1:2 * FK:FK], b1[0:z, att[0], FK - 1:2 * FK:FK],
                                ALU.add).then_inc(b1_ready, 1)
                dve.wait_ge(b1_ready, att[0] + 1)
                split_weights(dve, V, w2, w2_in, 32 * (att[0] + 1), w2_ready, att[0])

        dve.wait_ge(cst_in, 96)
        split_weights(dve, V, wqkv, wqkv_in, 16, wqkv_ready, 0)
        for s in (x_done, hh_ready, hh_raw):
            dve.sem_inc(s, 1)
        turns(dve, body)


def finish_output(nc, ctx, mem, A):
    sem = lambda n: ctx.enter_context(nc.semaphore(n))
    x2 = mem["x2"]
    NPT = 2
    bs = B // NPT
    xo = ctx.enter_context(nc.sbuf_tensor("xo", [P, KD, B, L], F32))
    x1_in = [sem(f"x1_in{q}") for q in range(NPT)]
    added, stored = sem("out_added"), sem("out_stored")
    blk = ctx.enter_context(nc.Block())

    @blk.sync
    def _(sp):
        for q in range(NPT):
            for k in range(KD):
                sp.dma_start(xo[:, k, q * bs:(q + 1) * bs, :], mem["x1_dram"][k][:, q * bs:(q + 1) * bs, :]).then_inc(x1_in[q], 16)
        for q in range(NPT):
            sp.wait_ge(added, q + 1)
            for k in range(KD):
                sp.dma_start(A["outT"][k][:, q * bs:(q + 1) * bs, :], xo[:, k, q * bs:(q + 1) * bs, :]).then_inc(stored, 16)
        sp.wait_ge(stored, 16 * KD * NPT)

    @blk.vector
    def _(dve):
        for q in range(NPT):
            dve.wait_ge(x1_in[q], 16 * KD)
            for k in range(KD):
                v = xo[:, k, q * bs:(q + 1) * bs, :]
                last = nc.vector.tensor_tensor(v, v, x2[:, k, q * bs:(q + 1) * bs, 1:LX], ALU.add)
            last.then_inc(added, 1)


def build(nc, A, out):
    A["outT"] = out
    with ExitStack() as ctx:
        mem = {}

        def keep(c, name, shape, dt=F32):
            mem[name] = c.enter_context(nc.sbuf_tensor(name, shape, dt))

        keep(ctx, "ident", [P, P])
        keep(ctx, "x2", [P, KD, B, LX])
        mem["slots"] = nc.dram_tensor("slots", (NSLOTS, D), F32, kind="Internal").ap()
        mem["ydram"] = nc.dram_tensor("expert_rows", (NSLOTS, D), F32, kind="Internal").ap()
        mem["x1_dram"] = nc.dram_tensor("x1_kept", (KD, P, B, L), F32, kind="Internal").ap()
        mem["n_slots"] = NSLOTS
        mem["zero_ready"] = ctx.enter_context(nc.semaphore("zero_ready"))
        mem["zeroed"] = ctx.enter_context(nc.semaphore("slots_zeroed"))
        with ExitStack() as c0:
            keep(c0, "cw", [P, TOP, NT])
            keep(c0, "put", [P, TOP, NT], U32)
            keep(c0, "get", [P, TOP, NT], U32)
            with ExitStack() as c1:
                keep(c1, "hst", [P, KD, T])
                with ExitStack() as c2:
                    keep(c2, "xt", [P, KD, T])
                    keep(c2, "zero", [P, 8 * D])
                    gated_recurrence(nc, c2, mem, A)
                with ExitStack() as c2:
                    keep(c2, "rows", [P, NT, D])
                    route(nc, c2, mem, A)
            with ExitStack() as c1:
                experts(nc, c1, mem, A)
            with ExitStack() as c1:
                keep(c1, "x1", [P, KD, B, LP])
                with ExitStack() as c2:
                    combine(nc, c2, mem, A)
                with ExitStack() as c2:
                    state_scan(nc, c2, mem, A)
        with ExitStack() as c1:
            transformer(nc, c1, mem, A)
        with ExitStack() as c1:
            finish_output(nc, c1, mem, A)



def shape_constants():
    f = np.float32
    half = np.arange(0, DH, 2, dtype=f)
    inv = (f(1) / f(10000) ** (half / f(DH))).astype(f)
    t = np.arange(L, dtype=f)
    fr = t[:, None] * inv[None]
    base = (half + f(0.4 * DH)) / f(1.4 * DH)
    sc = base[None] ** ((t - L // 2) / f(WIN // 2))[:, None]
    cos, sin = np.cos(fr), np.sin(fr)
    cat = lambda a, b: np.concatenate([a, b], 1)
    tabs = np.stack([np.stack([cat(cos * sc, cos * sc), cat(-sin * sc, sin * sc)]),
                     np.stack([cat(cos / sc, cos / sc), cat(-sin / sc, sin / sc)])])
    tabs = tabs.reshape(2, 2, WINS, WIN, DH).transpose(3, 0, 1, 2, 4).astype(f)
    i, j = np.arange(WIN)[:, None], np.arange(WIN)[None]
    own, before = np.where(j <= i, 0, NEVER), np.where(j >= i, 0, NEVER)
    mask = np.concatenate([own, before, own], 1).astype(f)
    bb, tt = np.arange(P) % B, np.arange(P) // B
    same = bb[:, None] == bb[None]
    routes = np.stack([bb[:, None] < bb[None], np.ones((P, P), bool), same]).astype(f)
    routes = np.concatenate([routes, ((same & (tt[:, None] < tt[None])).astype(f) - same.astype(f))[None]])
    keepcol = np.ones((E * TOP, NT), f)
    keepcol[0::TOP, 0] = 0
    keepcol[1::TOP, 0] = 0
    return {
        "rot_tabs": tabs, "mask": mask, "ident": np.eye(P, dtype=f), "route_masks": routes.transpose(1, 0, 2),
        "iota": np.broadcast_to(np.tile(np.arange(E, dtype=f), NT), (P, NT * E)),
        "keepcol": np.broadcast_to(keepcol.ravel(), (P, E * TOP * NT)),
    }


def layouts(x, cond_1024, L0_ffn_Wg, L0_ffn_b1, L1_cond_conv_b, L1_cond_bp, L1_cond_bs, L1_cond_A_log, L1_cond_dt_log, L1_cond_bo,
            L1_ffn_q_scale, L1_ffn_k_scale, L1_ffn_ln_g, L1_ffn_ln_b, L1_ffn_b1, L1_ffn_b2, **whole):
    cols = lambda a: a.reshape(KD, P).T
    b1 = np.zeros((DEPTH, 2, FK * P), np.float32)
    b1[:, :, :FF] = L1_ffn_b1.reshape(DEPTH, 2, FF)
    return {
        "xT_tb": x.transpose(2, 1, 0).reshape(D, T), "x_rows": x.transpose(1, 0, 2).reshape(T, D), "condT": cond_1024.T,
        "WgT": L0_ffn_Wg.T, "b1T": L0_ffn_b1.reshape(E, KH, P).transpose(2, 0, 1).reshape(P, E * KH),
        "conv_bT": cols(L1_cond_conv_b), "bpT": L1_cond_bp[:, None], "bsT": L1_cond_bs[:, None], "boT": cols(L1_cond_bo),
        "A_logT": L1_cond_A_log[:, None], "dt_logT": L1_cond_dt_log[:, None],
        "qk_scales": np.stack([L1_ffn_q_scale, L1_ffn_k_scale], 1), "b1f": b1.reshape(DEPTH, 2 * FK, P).transpose(2, 0, 1),
        "b2f": L1_ffn_b2.reshape(DEPTH, KD, P).transpose(2, 0, 1),
        "lgb": np.stack([L1_ffn_ln_g, L1_ffn_ln_b], 1).reshape(DEPTH, 2, KD, P).transpose(3, 0, 1, 2),
        **whole,
    }


def kernel(**inputs):
    import concourse.bacc as _bacc
    from concourse.bass_utils import run_bass_kernel_spmd as _run

    nc = _bacc.Bacc("TRN2", target_bir_lowering=False, num_devices=1)
    given = {**layouts(**{k: np.asarray(v) for k, v in inputs.items()}), **shape_constants()}
    arrays, A = {}, {}
    for name, a in given.items():
        arrays[f"in_{name}"] = np.ascontiguousarray(a)
        A[name] = nc.dram_tensor(f"in_{name}", a.shape, mybir.dt.from_np(a.dtype), kind="ExternalInput").ap()
    out = nc.dram_tensor("out_features", (KD, P, B, L), F32, kind="ExternalOutput").ap()
    build(nc, A, out)
    r = _run(nc, [arrays], core_ids=[0])
    got = r.results[0]["out_features"]
    return np.ascontiguousarray(got.reshape(D, B, L).transpose(1, 2, 0))
```

```python
import numpy as np
import concourse.bass as bass
from concourse import mybir
from concourse.alu_op_type import AluOpType as ALU
from contextlib import ExitStack

ACT = mybir.ActivationFunctionType
AX = mybir.AxisListType
F32 = mybir.dt.float32
F16 = mybir.dt.float16
F32R = mybir.dt.float32r
U32 = mybir.dt.uint32
I32 = mybir.dt.int32

B = 16
L = 256
D = 256
T = B * L
P = 128
KD = D // P


def placing(nc, ctx):
    place = {}

    def sb(n, s, d=F32):
        t = ctx.enter_context(nc.sbuf_tensor(n, s, d))
        place[n] = nc.sbuf_base - 4 * int(np.prod(s[1:]))
        return t

    def over(n, below, s, d=F32):
        return nc.alloc_sbuf_tensor_at(n, s, d, offset=place[below])

    def split(n, s):
        hi, lo = sb(n + "_hi", s, F32R), sb(n + "_lo", s, F32R)
        return [hi, lo, over(n + "_raw", n + "_lo", s)]

    return sb, over, split


def gated_recurrence(nc, ctx, mem, A):
    G = 3 * D
    W_SCALE = 256.0
    xt, rows, p_lg, ident, wg = mem["xt"], mem["rows"], mem["p_lg"], mem["ident"], mem["wg"]
    sb = lambda n, s, d: ctx.enter_context(nc.sbuf_tensor(n, s, d))
    pb = lambda n, s: ctx.enter_context(nc.psum_tensor(n, s, F32))
    sem = lambda n: ctx.enter_context(nc.semaphore(n))
    wk32 = sb("wk32", [P, KD, G], F32)
    wr32 = sb("wr32", [P, KD, G], F32)
    wk = [sb("wk_hi", [P, KD, G], F16), sb("wk_lo", [P, KD, G], F16)]
    wr = [sb("wr_hi", [P, KD, G], F16), sb("wr_lo", [P, KD, G], F16)]
    xs = [[sb(f"xs_{h}{p}", [P, KD, 2 * B], F16) for h in ("hi", "lo")] for p in range(2)]
    x_now = [sb(f"x_now{p}", [P, KD, 2 * B], F32) for p in range(2)]
    hh = [[sb(f"h_{h}{p}", [P, KD, B], F16) for h in ("hi", "lo")] for p in range(2)]
    hf = [sb(f"h_full{p}", [P, KD, B], F32) for p in range(2)]
    t_f = sb("t_f", [P, KD, B], F32)
    t_g = sb("t_g", [P, KD, B], F32)
    t_o = sb("t_o", [P, KD, B], F32)
    t_c = sb("t_c", [P, KD, B], F32)
    cell = sb("cell", [P, KD, B], F32)
    keep = sb("keep", [P, KD, B], F32)
    fresh = sb("fresh", [P, KD, B], F32)
    cnd = sb("cnd", [P, KD, B], F32)
    zero = mem["zero"]
    zero_kb = zero[:, 0:KD * B].rearrange("p (k b) -> p k b", k=KD)
    zero_kbb = zero[:, 0:KD * 2 * B].rearrange("p (k b) -> p k b", k=KD)
    h_tile = [sb(f"h_tile{q}", [P, KD, P], F32) for q in range(2)]
    p_rows = pb("p_rows", [P, D])
    p_f = [pb(f"p_f{p}", [P, KD, 2 * B]) for p in range(2)]
    p_g = [pb(f"p_g{p}", [P, KD, 2 * B]) for p in range(2)]
    p_o = [pb(f"p_o{p}", [P, KD, 2 * B]) for p in range(2)]

    w_loaded, x_loaded, c_loaded = sem("w_loaded"), [sem(f"x_loaded{c}") for c in range(4)], sem("c_loaded")
    w_scaled, w_hi, w_split = sem("w_scaled"), sem("w_hi"), sem("w_split")
    x_step, x_split = sem("x_step"), sem("x_split")
    x_used = sem("x_used")
    f_sums, g_sums, o_sums = sem("f_sums"), sem("g_sums"), sem("o_sums")
    f_ready, g_ready, tc_ready = sem("f_ready"), sem("g_tanh_ready"), sem("tc_ready")
    kept, cell_ready = sem("kept"), sem("cell_ready")
    h_hi_ready, h_full_ready, h_split = sem("h_hi_ready"), sem("h_full_ready"), sem("h_split")
    h_stored = sem("h_stored")
    tile_turned, rows_ready, loaded = sem("tile_turned"), sem("rows_ready"), mem["route_loaded"]
    TT = P // B
    zero_ready, zeroed = mem["zero_ready"], mem["zeroed"]
    QT = T // 4
    slots = mem["slots"]
    NSLOT = mem["n_slots"]

    STEPS = L
    U = 16
    blk = ctx.enter_context(nc.Block())

    @blk.sync
    def _(sp):
        sp.dma_start(wr32[:, :, :], A["L0_cond_Wr"].rearrange("(k p) n -> p k n", p=P)).then_inc(w_loaded, 16)
        sp.dma_start(wk32[:, :, :], A["L0_cond_Wk"].rearrange("(k p) n -> p k n", p=P)).then_inc(w_loaded, 16)
        sp.dma_start(cnd[:, :, :], A["condT"].rearrange("(k p) b -> p k b", p=P)).then_inc(c_loaded, 16)
        sp.dma_start(wg[:, :, :], A["WgT"].rearrange("(k p) e -> p k e", p=P)).then_inc(loaded, 16)
        sp.dma_start(ident[:, :], A["ident"]).then_inc(loaded, 16)
        xv = A["xT_tb"].rearrange("(k p) n -> p k n", p=P)
        for c in range(4):
            sp.dma_start(xt[:, :, c * QT:(c + 1) * QT], xv[:, :, c * QT:(c + 1) * QT]).then_inc(x_loaded[c], 16)
        sp.wait_ge(zero_ready, 1)
        rows = 8
        sv = slots.rearrange("(a p r) d -> a p (r d)", p=120, r=rows)
        for a in range(NSLOT // (120 * rows)):
            sp.dma_start(sv[a], zero[0:120, :]).then_inc(zeroed, 16)
        sp.wait_ge(zeroed, 16 * (NSLOT // (120 * rows)))

    @blk.gpsimd
    def _(pool):
        pool.memset(zero[:, :], 0.0).then_inc(zero_ready, 1)
        pool.wait_ge(zero_ready, 1)

        def split_x(i, m, first=False):
            par = m % 2
            if not first:
                pool.wait_ge(x_used, U // 2 * i + m - 1)
            col = bass.ds(i * (U * B) + m * 2 * B, 2 * B)
            nc.gpsimd.tensor_copy(x_now[par][:, :, :], xt[:, :, col]).then_inc(x_step, 1)
            pool.wait_ge(x_step, 2 * (U // 2 * i + m) + 1)
            nc.gpsimd.tensor_tensor(xs[par][0][:, :, :], x_now[par][:, :, :], zero_kbb, ALU.add).then_inc(x_step, 1)
            pool.wait_ge(x_step, 2 * (U // 2 * i + m) + 2)
            nc.gpsimd.tensor_tensor(xs[par][1][:, :, :], x_now[par][:, :, :], xs[par][0][:, :, :],
                                    ALU.subtract).then_inc(x_split, 1)

        def store_h(i, t):
            pool.wait_ge(h_full_ready, U * i + t + 1)
            s = t % TT
            nc.gpsimd.tensor_tensor(h_tile[t // TT % 2][:, :, s * B:(s + 1) * B], hf[t % 2][:, :, :], zero_kb, ALU.add).then_inc(h_stored, 1)

        pool.wait_ge(x_loaded[0], 16)
        split_x(0, 0, True)
        split_x(0, 1, True)
        for c in range(1, 4):
            pool.wait_ge(x_loaded[c], 16)
        with pool.Fori(0, STEPS // U - 1) as i:
            for t in range(U):
                if t % 2 == 0:
                    split_x(i, t // 2 + 2)
                store_h(i, t)
        for t in range(U):
            if t % 2 == 0 and t // 2 + 2 < U // 2:
                split_x(STEPS // U - 1, t // 2 + 2)
            store_h(STEPS // U - 1, t)

    @blk.tensor
    def _(pe):
        FS, OS, GS = [0, 1], [2, 3], [4, 5]

        def part(psum, chunks, w, a, start, order, cols=slice(0, 2 * B)):
            for n, (wh, ah) in enumerate(order):
                for j, c in enumerate(chunks):
                    for k in range(KD):
                        last = nc.tensor.matmul(psum[:, j, cols], w[wh][:, k, c * P:(c + 1) * P], a[ah][:, k, :],
                                                start=(start and n == 0 and j == 0 and k == 0), stop=False,
                                                skip_group_check=True)
            return last

        def x_products(i, m, half):
            par = m % 2
            pe.wait_ge(x_split, U // 2 * i + m + 1)
            for psum, chunks in (((p_f, FS), (p_g, GS)), ((p_o, OS),))[half]:
                last = part(psum[par], chunks, wk, xs[par], True, [(0, 0), (1, 0), (0, 1)])
            if half:
                last.then_inc(x_used, 1)

        def h_products(i, t):
            par, cols = t // 2 % 2, slice(t % 2 * B, (t % 2 + 1) * B)
            h = hh[1 - t % 2]
            pe.wait_ge(h_hi_ready, U * i + t + 1)
            part(p_f[par], FS, wr, h, False, [(0, 0), (1, 0)], cols)
            part(p_g[par], GS, wr, h, False, [(0, 0), (1, 0)], cols)
            pe.wait_ge(h_split, U * i + t + 1)
            part(p_f[par], FS, wr, h, False, [(0, 1)], cols).then_inc(f_sums, 1)
            part(p_g[par], GS, wr, h, False, [(0, 1)], cols).then_inc(g_sums, 1)
            part(p_o[par], OS, wr, h, False, [(0, 0), (1, 0), (0, 1)], cols).then_inc(o_sums, 1)

        def tile_products(n, q, s):
            h = h_tile[q]
            if s == 2:
                pe.wait_ge(h_stored, TT * n + TT + 2)
                if not isinstance(n, int) or n:
                    pe.wait_ge(rows_ready, n)
            if s in (2, 3):
                last = nc.tensor.transpose(p_rows[:, (s - 2) * P:(s - 1) * P], h[:, s - 2, :], ident[:, :])
                if s == 3:
                    last.then_inc(tile_turned, 1)
            elif s in (4, 5):
                nc.tensor.matmul(p_lg[:, bass.ds(n, 1), :].rearrange("p o e -> p (o e)"), h[:, s - 4, :], wg[:, s - 4, :],
                                 start=(s == 4), stop=(s == 5), skip_group_check=True)

        def body(i, first=False, tail=False):
            for t in range(U):
                h_products(i, t)
                if not (tail and t // 2 == U // 2 - 1):
                    x_products(i, t // 2 + 1, t % 2)
                if not (first and t < TT):
                    tile_products(i * (U // TT) + t // TT - 1, (t // TT - 1) % 2, t % TT)

        pe.wait_ge(w_split, 2)
        pe.wait_ge(loaded, 32)
        for half in range(2):
            x_products(0, 0, half)
        body(0, first=True)
        with pe.Fori(1, STEPS // U - 1) as i:
            body(i)
        body(STEPS // U - 1, tail=True)
        for s in range(2, 6):
            tile_products(STEPS // TT - 1, 1, s)

    @blk.scalar
    def _(act):
        def step(i, t):
            par, cols = t // 2 % 2, slice(t % 2 * B, (t % 2 + 1) * B)
            act.wait_ge(f_sums, U * i + t + 1)
            nc.scalar.activation(t_f[:, :, :], p_f[par][:, :, cols], ACT.Tanh, scale=1.0 / W_SCALE).then_inc(f_ready, 1)
            act.wait_ge(g_sums, U * i + t + 1)
            nc.scalar.activation(t_g[:, :, :], p_g[par][:, :, cols], ACT.Tanh, scale=1.0 / W_SCALE).then_inc(g_ready, 1)
            act.wait_ge(o_sums, U * i + t + 1)
            nc.scalar.activation(t_o[:, :, :], p_o[par][:, :, cols], ACT.Tanh, scale=1.0 / W_SCALE)
            act.wait_ge(cell_ready, U * i + t + 2)
            nc.scalar.activation(t_c[:, :, :], cell[:, :, :], ACT.Tanh, scale=0.5).then_inc(tc_ready, 1)

        act.sem_inc(rows_ready, 1)

        def tile_rows(n):
            act.wait_ge(tile_turned, n + 1)
            nc.scalar.activation(rows[:, bass.ds(n, 1), :].rearrange("p o d -> p (o d)"), p_rows[:, :], ACT.Copy, scale=0.5).then_inc(rows_ready, 1)

        def body(i, first=False):
            for t in range(U):
                step(i, t)
                if t % TT == 5 and not (first and t < TT):
                    tile_rows(i * (U // TT) + t // TT - 1)

        body(0, first=True)
        with act.Fori(1, STEPS // U) as i:
            body(i)
        tile_rows(STEPS // TT - 1)

    @blk.vector
    def _(dve):
        dve.wait_ge(w_loaded, 32)
        for n, (w, sc) in enumerate([(wr32, 0.25), (wk32, 0.5)]):
            nc.vector.tensor_scalar(w[:, :, 0:2 * D], w[:, :, 0:2 * D], sc * W_SCALE, None, ALU.mult).then_inc(w_scaled, 1)
            nc.vector.tensor_scalar(w[:, :, 2 * D:G], w[:, :, 2 * D:G], 2 * sc * W_SCALE, None, ALU.mult).then_inc(w_scaled, 1)
            dve.wait_ge(w_scaled, 2 * n + 2)
            wp = (wr, wk)[n]
            nc.vector.tensor_copy(wp[0][:, :, :], w[:, :, :]).then_inc(w_hi, 1)
            dve.wait_ge(w_hi, n + 1)
            nc.vector.tensor_tensor(wp[1][:, :, :], w[:, :, :], wp[0][:, :, :], ALU.subtract).then_inc(w_split, 1)
        dve.wait_ge(c_loaded, 16)
        nc.vector.tensor_scalar(cell[:, :, :], cnd[:, :, :], 2.0, None, ALU.mult).then_inc(cell_ready, 1)
        dve.wait_ge(cell_ready, 1)
        nc.vector.tensor_copy(hh[1][0][:, :, :], cell[:, :, :]).then_inc(h_hi_ready, 1)
        dve.wait_ge(h_hi_ready, 1)
        nc.vector.tensor_tensor(hh[1][1][:, :, :], cell[:, :, :], hh[1][0][:, :, :], ALU.subtract).then_inc(h_split, 1)

        def step(i, t):
            par, t1 = t % 2, U * i + t + 1
            dve.wait_ge(f_ready, t1)
            nc.vector.scalar_tensor_tensor(keep[:, :, :], t_f[:, :, :], 1.0, cell[:, :, :], ALU.add, ALU.mult)
            dve.wait_ge(g_ready, t1)
            nc.vector.scalar_tensor_tensor(fresh[:, :, :], t_f[:, :, :], 1.0, t_g[:, :, :],
                                           ALU.subtract, ALU.mult).then_inc(kept, 1)
            dve.wait_ge(kept, t1)
            nc.vector.scalar_tensor_tensor(cell[:, :, :], keep[:, :, :], 0.5, fresh[:, :, :],
                                           ALU.mult, ALU.subtract).then_inc(cell_ready, 1)
            dve.wait_ge(tc_ready, t1)
            nc.vector.scalar_tensor_tensor(hh[par][0][:, :, :], t_o[:, :, :], 1.0, t_c[:, :, :],
                                           ALU.add, ALU.mult).then_inc(h_hi_ready, 1)
            dve.wait_ge(h_stored, t1)
            nc.vector.scalar_tensor_tensor(hf[par][:, :, :], t_o[:, :, :], 1.0, t_c[:, :, :],
                                           ALU.add, ALU.mult).then_inc(h_full_ready, 1)
            dve.wait_ge(h_full_ready, t1)
            nc.vector.tensor_tensor(hh[par][1][:, :, :], hf[par][:, :, :], hh[par][0][:, :, :],
                                    ALU.subtract).then_inc(h_split, 1)

        dve.sem_inc(h_stored, 2)
        with dve.Fori(0, STEPS // U) as i:
            for t in range(U):
                step(i, t)


E = 8
TOP = 2
HID = 1024
KH = HID // P
CAP = int(round(TOP * T * 1.05 / E))
CHUNK = 360
SUB = CHUNK // 3
CPE = -(-CAP // CHUNK)
STRIDE = CPE * CHUNK
NSLOTS = E * STRIDE
NT = T // P
TT = P // B
DROPPED = 4.0 * NSLOTS


def route(nc, ctx, mem, A):
    sb = lambda n, s, d=F32: ctx.enter_context(nc.sbuf_tensor(n, s, d))
    pb = lambda n, s: ctx.enter_context(nc.psum_tensor(n, s, F32))
    sem = lambda n: ctx.enter_context(nc.semaphore(n))
    rows, p_lg, loaded = mem["rows"], mem["p_lg"], mem["route_loaded"]
    cst = sb("route_masks", [P, 4, P])
    iota = sb("iota", [P, NT, E])
    keepcol = sb("keepcol", [P, E * TOP, NT])
    ebase = sb("ebase", [P, E])
    lg = sb("lg", [P, NT, E])
    m1 = sb("m1", [P, NT]); dl = sb("dl", [P, NT, E]); ex = sb("ex", [P, NT, E]); sm = sb("sm", [P, NT]); rs = sb("rs", [P, NT])
    g = sb("g", [P, NT, E]); gk = sb("gk", [P, TOP, NT]); eq = sb("eq", [P, NT, E]); cand = sb("cand", [P, NT, E])
    idx = sb("idx", [P, TOP, NT]); hot = sb("hot", [P, E, TOP, NT])
    rest = sb("rest", [P, NT, E])
    tot = sb("tot", [P, E * TOP]); base = sb("base", [P, E, TOP])
    scan = sb("scan", [P, E * TOP, NT]); cnt = sb("cnt", [P, E, TOP, NT])
    pos = sb("pos", [P, TOP, NT]); fits = sb("fits", [P, TOP, NT]); off = sb("off", [P, TOP, NT])
    sl = sb("sl", [P, TOP, NT]); miss = sb("miss", [P, TOP, NT])
    put, get, cw = mem["put"], mem["get"], mem["cw"]
    p_same = pb("p_same", [P, E * TOP, NT])
    p_cor = pb("p_cor", [P, E * TOP, NT])
    p_base = pb("p_base", [P, 2, E * TOP])

    v = sem("route_step")
    logit_sub, exps = sem("logit_sub"), sem("exps")
    hot_ready, counted, tot_ready, tot_summed = sem("hot_ready"), sem("counted"), sem("tot_ready"), sem("tot_summed")
    put_ready, scattered = sem("put_ready"), sem("scattered")
    slots = mem["slots"]
    blk = ctx.enter_context(nc.Block())

    @blk.sync
    def _(sp):
        sp.dma_start(cst[:, :, :], A["route_masks"]).then_inc(loaded, 16)
        sp.dma_start(iota[:, :, :], A["iota"].rearrange("p (n e) -> p n e", e=E)).then_inc(loaded, 16)
        sp.dma_start(keepcol[:, :, :], A["keepcol"].rearrange("p (a n) -> p a n", n=NT)).then_inc(loaded, 16)

    @blk.tensor
    def _(pe):
        pe.wait_ge(loaded, 80)
        hv = hot[:, :, :, :].rearrange("p e k n -> p (e k n)")
        pe.wait_ge(hot_ready, 2)
        nc.tensor.matmul(p_same[:, :, :], cst[:, 2, :], hv, start=True, stop=True).then_inc(counted, 1)
        nc.tensor.matmul(p_cor[:, :, :], cst[:, 3, :], hv, start=True, stop=True).then_inc(counted, 1)
        pe.wait_ge(tot_ready, 1)
        nc.tensor.matmul(p_base[:, 0, :], cst[:, 0, :], tot[:, :], start=True, stop=True)
        nc.tensor.matmul(p_base[:, 1, :], cst[:, 1, :], tot[:, :], start=True, stop=True).then_inc(tot_summed, 1)

    @blk.scalar
    def _(act):
        act.wait_ge(logit_sub, 1)
        nc.scalar.activation(ex[:, :, :], dl[:, :, :], ACT.Exp).then_inc(exps, 1)

    @blk.vector
    def _(dve):
        count = [0]

        def then(ins):
            count[0] += 1
            ins.then_inc(v, 1)
            dve.wait_ge(v, count[0])

        V = nc.vector
        over = lambda a: a.unsqueeze(2).broadcast_to([P, NT, E])
        dve.wait_ge(loaded, 80)
        then(V.tensor_scalar(lg[:, :, :], p_lg[:, :, :], 0.5, None, ALU.mult))
        then(V.tensor_reduce(m1[:, :], lg[:, :, :], AX.X, ALU.max))
        V.tensor_tensor(dl[:, :, :], lg[:, :, :], over(m1[:, :]), ALU.subtract).then_inc(logit_sub, 1)
        dve.wait_ge(exps, 1)
        then(V.tensor_reduce(sm[:, :], ex[:, :, :], AX.X, ALU.add))
        then(V.reciprocal(rs[:, :], sm[:, :]))
        then(V.tensor_tensor(g[:, :, :], ex[:, :, :], over(rs[:, :]), ALU.mult))
        cur = g
        for k in range(TOP):
            then(V.tensor_reduce(gk[:, k, :], cur[:, :, :], AX.X, ALU.max))
            then(V.tensor_tensor(eq[:, :, :], cur[:, :, :], over(gk[:, k, :]), ALU.is_equal))
            then(V.scalar_tensor_tensor(cand[:, :, :], eq[:, :, :], -float(E), iota[:, :, :], ALU.mult, ALU.add))
            then(V.tensor_reduce(idx[:, k, :], cand[:, :, :], AX.X, ALU.min))
            then(V.tensor_scalar(idx[:, k, :], idx[:, k, :], float(E), None, ALU.add))
            then(V.tensor_tensor(eq[:, :, :], iota[:, :, :], over(idx[:, k, :]), ALU.is_equal))
            V.tensor_copy(hot[:, :, k, :].rearrange("p e n -> p n e"), eq[:, :, :]).then_inc(hot_ready, 1)
            if k == 0:
                then(V.scalar_tensor_tensor(rest[:, :, :], eq[:, :, :], -2.0, g[:, :, :], ALU.mult, ALU.add))
                cur = rest
        dve.wait_ge(hot_ready, 2)
        hv = hot[:, :, :, :].rearrange("p e k n -> p (e k) n")
        V.tensor_reduce(tot[:, :], hv, AX.X, ALU.add).then_inc(tot_ready, 1)
        dve.wait_ge(counted, 2)
        flat = lambda a: a.rearrange("p a n -> p (a n)")
        then(V.tensor_tensor_scan(flat(scan[:, :, :]), flat(keepcol[:, :, :]), flat(p_same[:, :, :]), 0.0, ALU.mult, ALU.add))
        cv = cnt[:, :, :, :].rearrange("p e k n -> p (e k) n")
        then(V.tensor_tensor(cv, scan[:, :, :], p_cor[:, :, :], ALU.add))
        dve.wait_ge(tot_summed, 1)
        bv = base[:, :, :].rearrange("p e k -> p (e k)")
        then(V.tensor_copy(bv, p_base[:, 0, :]))
        then(V.tensor_tensor(base[:, :, 1], base[:, :, 1], p_base[:, 1, 0:2 * E:2], ALU.add))
        then(V.tensor_tensor(cv, cv, bv.unsqueeze(2).broadcast_to([P, E * TOP, NT]), ALU.add))
        then(V.tensor_tensor(cv, cv, hv, ALU.mult))
        for k in range(TOP):
            then(V.tensor_reduce(pos[:, k, :], cnt[:, :, k, :].rearrange("p e n -> p n e"), AX.X, ALU.add))
        then(V.tensor_scalar(fits[:, :, :], pos[:, :, :], float(CAP), None, ALU.is_lt))
        by_half = lambda a, k: a[:, k, :].rearrange("p (h m) -> p m h", h=L // P)
        for k in range(TOP):
            then(V.tensor_tensor(cw[:, :, k, :], by_half(gk, k), by_half(fits, k), ALU.mult))
        then(V.tensor_scalar(off[:, :, :], pos[:, :, :], float(CAP - 1), None, ALU.min))
        then(V.scalar_tensor_tensor(sl[:, :, :], idx[:, :, :], float(STRIDE), off[:, :, :], ALU.mult, ALU.add))
        then(V.tensor_scalar(miss[:, :, :], fits[:, :, :], -DROPPED, DROPPED, ALU.mult, ALU.add))
        then(V.tensor_tensor(miss[:, :, :], miss[:, :, :], sl[:, :, :], ALU.add))
        V.tensor_copy(put[:, :, :], miss[:, :, :]).then_inc(put_ready, 1)
        for k in range(TOP):
            V.tensor_copy(get[:, :, k, :], by_half(sl, k))

    @blk.gpsimd
    def _(pool):
        pool.wait_ge(put_ready, 1)
        for n in range(NT):
            for k in range(TOP):
                nc.gpsimd.indirect_dma_start(slots, bass.IndirectOffsetOnAxis(put[:, k, n:n + 1], 0), rows[:, n, :], None,
                                             bounds_check=NSLOTS - 1, oob_is_err=False).then_inc(scattered, 16)
        pool.wait_ge(scattered, 16 * NT * TOP)


def experts(nc, ctx, mem, A):
    sb = lambda n, s, d=F32: ctx.enter_context(nc.sbuf_tensor(n, s, d))
    pb = lambda n, s: ctx.enter_context(nc.psum_tensor(n, s, F32))
    sem = lambda n: ctx.enter_context(nc.semaphore(n))
    ident, slots, ydram = mem["ident"], mem["slots"], mem["ydram"]
    w1_raw, w2_raw = sb("w1_raw", [P, KD, HID]), sb("w2_raw", [P, KH, D])
    w1 = [[sb(f"w1_{h}{q}", [P, KD, HID], F32R) for h in ("hi", "lo")] for q in range(2)]
    w2 = [[sb(f"w2_{h}{q}", [P, KH, D], F32R) for h in ("hi", "lo")] for q in range(2)]
    b1 = [sb(f"b1_{q}", [P, KH]) for q in range(2)]
    b2 = [sb(f"b2_{q}", [P, D]) for q in range(2)]
    rin = [sb(f"rin{q}", [SUB, 3, D]) for q in range(3)]
    xin = [[sb(f"xin_{h}{q}", [P, KD, CHUNK], F32R) for h in ("hi", "lo")] for q in range(2)]
    gelu = [sb(f"gelu{q}", [P, CHUNK]) for q in range(3)]
    hid = [[sb(f"hid_{h}{q}", [P, KH, CHUNK], F32R) for h in ("hi", "lo")] for q in range(2)]
    yout = [sb(f"yout{q}", [SUB, 3, D]) for q in range(2)]
    p_t = pb("p_t", [P, KD, 512])
    p_h = [pb(f"p_h{q}", [P, CHUNK]) for q in range(3)]
    p_y = [pb(f"p_y{q}", [SUB, D]) for q in range(3)]
    w_in, b_in, w_hi, w_split = [sem("w1_in"), sem("w2_in")], [sem(f"b_in{q}") for q in range(2)], sem("w_hi"), sem("w_split")
    r_in = [sem(f"r_in{q}") for q in range(3)]
    turned, xin_hi, xin_ready, h_sum, gelu_ready, h_hi, h_ready, y_sum, y_ready = (
        sem(n) for n in ("turned", "xin_hi", "xin_ready", "h_sum", "gelu_ready", "hid_hi", "h_ready", "y_sum", "y_ready"))
    y_stored = [sem(f"y_stored{q}") for q in range(2)]
    order_written, order_read = sem("order_written"), sem("order_read")
    orders = [(mem["get"], mem["get_dram"], mem["get_seq"]), (mem["cw"], mem["cw_dram"], mem["cw_seq"])]
    CB = 2 * CPE
    NI = E // 2
    blk = ctx.enter_context(nc.Block())
    sv = slots.rearrange("(a s p) d -> a p s d", p=SUB, s=3)
    yv = ydram.rearrange("(a s p) d -> a p s d", p=SUB, s=3)
    HALVES = ((0, 0), (0, 1), (1, 0))

    @blk.sync
    def _(sp):
        sp.sem_inc(turned, CB)
        sp.sem_inc(w_split, 2)

        def weights(i, q):
            e = i * 2 + q
            sp.wait_ge(w_split, 2 * e + 2)
            sp.dma_start(w1_raw[:, :, :], A["L0_ffn_W1"].rearrange("e (k p) n -> e p k n", p=P)[bass.ds(e, 1)].rearrange("o p k n -> (o p) k n")).then_inc(w_in[0], 16)
            sp.dma_start(w2_raw[:, :, :], A["L0_ffn_W2"].rearrange("e (k p) n -> e p k n", p=P)[bass.ds(e, 1)].rearrange("o p k n -> (o p) k n")).then_inc(w_in[1], 16)

        def biases(i, q):
            e = i * 2 + q
            sp.wait_ge(y_ready, 3 * CB * i + 3 * CPE * (q + 1))
            sp.dma_start(b1[q][:, :], A["b1T"][:, bass.ds(e * KH, KH)]).then_inc(b_in[q], 16)
            sp.dma_start(b2[q][:, :], A["L0_ffn_b2"][bass.ds(e, 1), :].broadcast_to([P, D])).then_inc(b_in[q], 16)

        def slot_rows(i, c):
            sp.wait_ge(turned, CB + CB * i + c - 2)
            sp.dma_start(rin[c % 3][:, :, :], sv[bass.ds(i * CB + c, 1)].rearrange("o p s d -> (o p) s d")).then_inc(r_in[c % 3], 16)

        with sp.Fori(0, NI) as i:
            for q in range(2):
                weights(i, q)
                for c in range(CPE):
                    slot_rows(i, q * CPE + c)
                    if c == 0:
                        biases(i, q)
        for d, src in mem["scan_loads"]:
            sp.dma_start(d, src).then_inc(mem["scan_loaded"], 16)
        sp.wait_ge(order_written, 16 * TT * len(orders))
        for _, dram, seq in orders:
            sp.dma_start(seq[:, :, :, :], dram).then_inc(order_read, 16)
        sp.wait_ge(order_read, 16 * len(orders))

    @blk.tensor
    def _(pe):
        def turn(i, c):
            pe.wait_ge(r_in[c % 3], 16 * ((CB // 3) * i + c // 3 + 1))
            for s in range(3):
                for k in range(KD):
                    last = nc.tensor.transpose(p_t[:, k, s * SUB:(s + 1) * SUB], rin[c % 3][:, s, k * P:(k + 1) * P], ident[0:SUB, 0:SUB])
            last.then_inc(turned, 1)

        def up(i, c):
            q = c // CPE
            if c % CPE == 0:
                pe.wait_ge(w_split, 2 * (2 * i + q) + 3)
            pe.wait_ge(xin_ready, CB * i + c + 1)
            for j in range(KH):
                pe.wait_ge(gelu_ready, KH * (CB * i + c) + j + 1)
                out = p_h[(c * KH + j) % 3][:, :]
                for k in range(KD):
                    for a, b in HALVES:
                        last = nc.tensor.matmul(out, w1[q][a][:, k, j * P:(j + 1) * P], xin[c % 2][b][:, k, :],
                                                start=(k == 0 and a + b == 0), stop=(k == KD - 1 and a == 1))
                last.then_inc(h_sum, 1)

        def down(i, c):
            q = c // CPE
            if c % CPE == 0:
                pe.wait_ge(w_split, 2 * (2 * i + q) + 4)
            pe.wait_ge(h_ready, KH * (CB * i + c + 1) + 3)
            for s in range(3):
                pe.wait_ge(y_ready, 3 * (CB * i + c) + s + 3 * CB - 2)
                for j in range(KH):
                    for a, b in HALVES:
                        last = nc.tensor.matmul(p_y[s][:, :], hid[c % 2][a][:, j, s * SUB:(s + 1) * SUB], w2[q][b][:, j, :],
                                                start=(j == 0 and a + b == 0), stop=(j == KH - 1 and a == 1))
                last.then_inc(y_sum, 1)

        def body(i, first=False, tail=False):
            for c in range(CB):
                up(i, c)
                if not (tail and c == CB - 1):
                    turn(i, c + 1)
                if c:
                    down(i, c - 1)
                elif not first:
                    down(i - 1, CB - 1)

        turn(0, 0)
        body(0, first=True)
        with pe.Fori(1, NI - 1) as i:
            body(i)
        body(NI - 1, tail=True)
        down(NI - 1, CB - 1)

    @blk.scalar
    def _(act):
        for timed, dram, _ in orders:
            for tt in range(TT):
                act.dma_start(dram.rearrange("(m t) b k h -> t b m (k h)", t=TT)[tt],
                              timed[tt * B:(tt + 1) * B, :, :, :].rearrange("b m k h -> b m (k h)")).then_inc(order_written, 16)
        act.sem_inc(gelu_ready, 3)
        act.sem_inc(h_ready, 3)
        with act.Fori(0, NI) as i:
            for c in range(CB):
                if c % CPE == 0:
                    act.wait_ge(b_in[c // CPE], 32 * i + 32)
                for j in range(KH):
                    u = c * KH + j
                    act.wait_ge(h_sum, KH * CB * i + u + 1)
                    act.wait_ge(h_ready, KH * CB * i + u + 1)
                    nc.scalar.activation(gelu[u % 3][:, :], p_h[u % 3][:, :], ACT.Gelu,
                                         bias=b1[c // CPE][:, j:j + 1]).then_inc(gelu_ready, 1)

    @blk.vector
    def _(dve):
        dve.sem_inc(y_ready, 3 * CB)

        def take(i, c):
            hi, lo = xin[c % 2]
            dve.wait_ge(turned, CB * i + CB + c + 1)
            nc.vector.tensor_copy(hi[:, :, :], p_t[:, :, 0:CHUNK]).then_inc(xin_hi, 1)
            dve.wait_ge(xin_hi, CB * i + c + 1)
            nc.vector.tensor_tensor(lo[:, :, :], p_t[:, :, 0:CHUNK], hi[:, :, :].bitcast(F32), ALU.subtract).then_inc(xin_ready, 1)

        def weights_hi(i, q):
            e = i * 2 + q
            for n, (raw, (hi, lo)) in enumerate(((w1_raw, w1[q]), (w2_raw, w2[q]))):
                dve.wait_ge(w_in[n], 16 * e + 16)
                nc.vector.tensor_copy(hi[:, :, :], raw[:, :, :]).then_inc(w_hi, 1)

        def split_hidden(i, c):
            hi, lo = hid[c % 2]
            for j in range(KH):
                u = c * KH + j
                dve.wait_ge(gelu_ready, KH * CB * i + u + 4)
                nc.vector.tensor_copy(hi[:, j, :], gelu[u % 3][:, :]).then_inc(h_hi, 1)
                dve.wait_ge(h_hi, KH * CB * i + u + 1)
                nc.vector.tensor_tensor(lo[:, j, :], gelu[u % 3][:, :], hi[:, j, :].bitcast(F32), ALU.subtract).then_inc(h_ready, 1)

        def bias(i, c):
            if not (isinstance(i, int) and i == 0 and c < 2):
                dve.wait_ge(y_stored[c % 2], 16 * (CB // 2 * i + c // 2))
            for s in range(3):
                dve.wait_ge(y_sum, 3 * (CB * i + c) + s + 1)
                nc.vector.tensor_tensor(yout[c % 2][:, s, :], p_y[s][:, :], b2[c // CPE][0:SUB, :], ALU.add).then_inc(y_ready, 1)

        def body(i, first=False, tail=False):
            for c in range(CB):
                split_hidden(i, c)
                if not (tail and c == CB - 1):
                    take(i, c + 1)
                if c:
                    bias(i, c - 1)
                elif not first:
                    bias(i - 1, CB - 1)
                if c == 0:
                    weights_hi(i, 1)
                elif c == CPE and not tail:
                    weights_hi(i + 1, 0)

        take(0, 0)
        for n, (raw, (hi, lo)) in enumerate(((w1_raw, w1[0]), (w2_raw, w2[0]))):
            dve.wait_ge(w_in[n], 16)
            nc.vector.tensor_copy(hi[:, :, :], raw[:, :, :]).then_inc(w_hi, 1)
            dve.wait_ge(w_hi, n + 1)
            nc.vector.tensor_tensor(lo[:, :, :], raw[:, :, :], hi[:, :, :].bitcast(F32), ALU.subtract).then_inc(w_split, 1)
        body(0, first=True)
        with dve.Fori(1, NI - 1) as i:
            body(i)
        body(NI - 1, tail=True)
        bias(NI - 1, CB - 1)

    @blk.gpsimd
    def _(pool):
        def weights_lo(i, q):
            e = i * 2 + q
            for n, (raw, (hi, lo)) in enumerate(((w1_raw, w1[q]), (w2_raw, w2[q]))):
                pool.wait_ge(w_hi, 2 * e + n + 1)
                pool.tensor_tensor(lo[:, :, :], raw[:, :, :], hi[:, :, :].bitcast(F32), ALU.subtract).then_inc(w_split, 1)

        def store(i, q):
            for c in range(q * CPE, (q + 1) * CPE):
                pool.wait_ge(y_ready, 3 * (CB * i + c + 1) + 3 * CB)
                pool.dma_start(yv[bass.ds(i * CB + c, 1)].rearrange("o p s d -> (o p) s d"), yout[c % 2][:, :, :]).then_inc(y_stored[c % 2], 16)

        with pool.Fori(0, NI - 1) as i:
            weights_lo(i, 1)
            store(i, 0)
            weights_lo(i + 1, 0)
            store(i, 1)
        weights_lo(NI - 1, 1)
        store(NI - 1, 0)
        store(NI - 1, 1)
        for q in range(2):
            pool.wait_ge(y_stored[q], 16 * (CB // 2) * NI)


PAD = 15
LP = L + PAD


PAD = 15
LP = L + PAD
NS = 64
TAPS = B
PAIR = 2
NP_ = B // PAIR
C2 = PAIR * L
LX = L + 1


def scan_constants(nc, ctx, mem, A):
    sb, _, _ = placing(nc, ctx)
    wp = sb("wp", [P, KD, 2 * NS]); ws = sb("ws", [P, KD, NS]); wo_s = sb("wo_s", [NS, D])
    cnd = sb("cnd2", [P, KD, TAPS]); cb = sb("cb", [P, KD]); bp = sb("bp", [P, 1]); bs = sb("bs", [NS, 1]); bo = sb("bo", [P, KD])
    logs = sb("logs", [NS, 2])
    mem["scan_constants"] = wp, ws, wo_s, cnd, cb, bp, bs, bo, logs
    return ((wp[:, :, :], A["L1_cond_Wp"].rearrange("(k p) n -> p k n", p=P)),
            (ws[:, :, :], A["L1_cond_Ws"].rearrange("(k p) n -> p k n", p=P)),
            (wo_s[:, :], A["L1_cond_Wo"]),
            (cnd[:, :, :], A["condT"].rearrange("(k p) b -> p k b", p=P)),
            (cb[:, :], A["conv_bT"]), (bp[:, :], A["bpT"]), (bs[:, :], A["bsT"]), (bo[:, :], A["boT"]),
            (logs[:, 0:1], A["A_logT"]), (logs[:, 1:2], A["dt_logT"]))


def combine_and_scan(nc, ctx, mem, A):
    sb, _, split = placing(nc, ctx)
    pb = lambda n, s: ctx.enter_context(nc.psum_tensor(n, s, F32))
    sem = lambda n: ctx.enter_context(nc.semaphore(n))
    x1, x2 = mem["x1"], mem["x2"]
    wp, ws, wo_s, cnd, cb, bp, bs, bo, logs = mem["scan_constants"]
    wpr = split("wpk", [P, TAPS, 2 * NS])
    wpk = wpr[2]
    sp_a = sb("sp_a", [NS, 2]); sp_e = sb("sp_e", [NS, 2]); sp_l = sb("sp_l", [NS, 2]); sp_v = sb("sp_v", [NS, 2])
    prod = sb("prod", [NS, 1]); decay = sb("decay", [NS, L]); bias = sb("bias_bc", [P, 1])
    acc = [[sb(f"acc{q}_{r}", [P, PAIR, L]) for r in range(2)] for q in range(2)]
    conv = [sb(f"conv{q}", [P, PAIR, L]) for q in range(2)]
    zz = [sb(f"zz{q}", [NS, C2]) for q in range(2)]; az = sb("az", [NS, C2]); ez = sb("ez", [NS, C2]); lz = [sb(f"lz{q}", [NS, C2]) for q in range(2)]
    ct = [sb(f"ct{q}", [NS, C2]) for q in range(2)]; uu = [sb(f"uu{q}", [NS, C2]) for q in range(2)]
    rz = sb("rz", [NS, C2]); bt = sb("bt", [NS, C2]); d1 = sb("d1", [NS, C2]); st = sb("st", [NS, C2])
    yy = [sb(f"yy{q}", [NS, C2]) for q in range(2)]
    p_bc = [pb(f"p_bc{q}", [P, C2]) for q in range(2)]
    p_u = [pb(f"p_u{q}", [NS, C2]) for q in range(2)]
    p_2 = [pb(f"p_2{q}", [P, PAIR, L]) for q in range(2)]
    p_x = [pb(f"p_x{q}", [P, KD, L]) for q in range(2)]
    p_b = p_x[0][:, 0, 0:1]
    ydram, get, cw, ident = mem["ydram"], mem["get_seq"], mem["cw_seq"], mem["ident"]
    TILES = PAIR * L // P
    yk = [[sb(f"yk{k}_{j}", [P, D]) for j in range(TILES)] for k in range(TOP)]
    xr = [sb(f"xr{q}", [P, TILES, D]) for q in range(2)]
    half = [sb(f"half{j}", [P, D]) for j in range(TILES)]
    x1r = [sb(f"x1_{h}", [P, B, LP], F32R) for h in ("hi", "lo")]
    XO = 2 * PAIR
    whole = [sb(f"whole{j}", [P, D]) for j in range(TILES)]
    gathered = [sem(f"gathered{j}") for j in range(TILES)]
    x_rows = [sem(f"x_rows{q}") for q in range(2)]
    half_ready, whole_ready, x1_turned, x1_out, x1_split, padded = (sem(n) for n in ("half_ready", "whole_ready", "x1_turned", "x1_out", "x1_split", "padded"))
    loaded = mem["scan_loaded"]
    setup, bias_sum, bias_ready = sem("scan_setup"), sem("bias_sum"), sem("bias_ready")
    sp_step = sem("sp_step")
    part, conv_ready, bc_sum, u_sum = sem("part"), sem("conv_ready"), sem("bc_sum"), sem("u_sum")
    z_ready, abs_ready, exp_ready, ln_ready, ct_ready, u_ready = sem("z_ready"), sem("abs_ready"), sem("exp_ready"), sem("ln_ready"), sem("ct_ready"), sem("u_ready")
    relu_ready, b_ready, d_ready, st_ready, yy_ready = sem("relu_ready"), sem("b_ready"), sem("d_ready"), sem("st_ready"), sem("yy_ready")
    x2_sum, x2_ready, saved = sem("x2_sum"), sem("x2_ready"), sem("x1_saved")
    blk = ctx.enter_context(nc.Block())
    col = lambda a: a.rearrange("(k p) -> p k", p=P)
    LOADS = 10

    def tap(k, i, t):
        return x1[:, k, bass.ds(i * PAIR, PAIR), t:t + L]

    @blk.sync
    def _(sp):
        for d, src in attention_constants(mem, A):
            sp.dma_start(d, src).then_inc(mem["cst_in"], 16)

        def rows(n):
            if n >= 2:
                sp.wait_ge(whole_ready, TILES * (n - 1))
            sp.dma_start(xr[n % 2][:, :, :], A["x_rows"].rearrange("(n j p) d -> n p j d", j=TILES, p=P)[n]).then_inc(x_rows[n % 2], 16)

        rows(0)
        rows(1)
        for n in range(NP_):
            sp.wait_ge(x1_out, XO * (n + 1))
            b = slice(n * PAIR, (n + 1) * PAIR)
            for k in range(KD):
                sp.dma_start(mem["x1_dram"][k][:, b, :], x1[:, k, b, PAD:LP]).then_inc(saved, 16)
            if n + 2 < NP_:
                rows(n + 2)
        sp.wait_ge(saved, 16 * KD * NP_)

    @blk.gpsimd
    def _(pool):
        def fetch(n):
            for j in range(TILES):
                if n:
                    pool.wait_ge(whole_ready, TILES * (n - 1) + j + 1)
                for k in range(TOP):
                    b, h = n * PAIR + j // 2, j % 2
                    nc.gpsimd.indirect_dma_start(yk[k][j][:, :], None, ydram, bass.IndirectOffsetOnAxis(get[:, b, k, h:h + 1], 0),
                                                 bounds_check=NSLOTS - 1, oob_is_err=False).then_inc(gathered[j], 16)

        def rest(n):
            pool.wait_ge(x1_out, XO * (n + 1))
            b = slice(n * PAIR, (n + 1) * PAIR)
            pool.tensor_tensor(x1r[1][:, b, PAD:LP], x1[:, 1, b, PAD:LP], x1r[0][:, b, PAD:LP].bitcast(F32), ALU.subtract).then_inc(x1_split, 1)

        fetch(0)
        for k in range(KD):
            pool.memset(x1[:, k, :, 0:PAD], 0.0).then_inc(padded, 1)
        pool.wait_ge(padded, KD)
        pad = x1[:, 1, :, 0:PAD]
        for h in range(2):
            pool.tensor_tensor(x1r[h][:, :, 0:PAD], pad, pad, ALU.add).then_inc(padded, 1)
        pool.memset(x2[:, :, :, 0:1], 0.0).then_inc(padded, 1)
        rest(0)
        fetch(1)
        for n in range(1, NP_):
            if n + 1 < NP_:
                fetch(n + 1)
            rest(n)
        pool.wait_ge(x2_ready, KD + 1)
        pool.wait_ge(padded, KD + 3)
        x_halves(pool, mem, 0, mem["hs_step"], mem["hs_ready"], 0)

    @blk.scalar
    def _(act):
        act.wait_ge(loaded, 16 * LOADS)
        act.activation(sp_a[:, :], logs[:, :], ACT.Abs).then_inc(sp_step, 1)
        act.wait_ge(sp_step, 1)
        act.activation(sp_e[:, :], sp_a[:, :], ACT.Exp, scale=-1.0).then_inc(sp_step, 1)
        act.wait_ge(sp_step, 2)
        act.activation(sp_l[:, :], sp_e[:, :], ACT.Ln, bias=1.0).then_inc(sp_step, 1)
        act.wait_ge(bias_ready, 1)

        def rows_out(n):
            for s in range(PAIR):
                act.wait_ge(x1_turned, PAIR * n + s + 1)
                b = bass.ds(n * PAIR + s, 1)
                nc.scalar.activation(x1[:, :, b, PAD:LP].rearrange("p k o t -> p k (o t)"), p_x[s][:, :, :], ACT.Copy).then_inc(x1_out, 1)
                nc.scalar.activation(x1r[0][:, b, PAD:LP].rearrange("p o t -> p (o t)"), p_x[s][:, 1, :], ACT.Copy).then_inc(x1_out, 1)

        def body(i, q):
            n = 2 * i + q
            act.wait_ge(bc_sum, n + 1)
            act.wait_ge(yy_ready, n + 1)
            nc.scalar.activation(zz[q][:, :], p_bc[q][0:NS, :], ACT.Identity, bias=bias[0:NS, :]).then_inc(z_ready, 1)
            nc.scalar.activation(ct[q][:, :], p_bc[q][NS:P, :], ACT.Tanh, bias=bias[NS:P, :]).then_inc(ct_ready, 1)
            act.wait_ge(z_ready, n + 1)
            nc.scalar.activation(az[:, :], zz[q][:, :], ACT.Abs).then_inc(abs_ready, 1)
            act.wait_ge(abs_ready, n + 1)
            nc.scalar.activation(ez[:, :], az[:, :], ACT.Exp, scale=-1.0).then_inc(exp_ready, 1)
            act.wait_ge(exp_ready, n + 1)
            nc.scalar.activation(lz[q][:, :], ez[:, :], ACT.Ln, bias=1.0).then_inc(ln_ready, 1)
            act.wait_ge(u_sum, n + 1)
            nc.scalar.activation(uu[q][:, :], p_u[q][:, :], ACT.Identity, bias=bs[:, :]).then_inc(u_ready, 1)

        def out(i, q):
            n = 2 * i + q
            for m in range(KD):
                act.wait_ge(x2_sum, 2 * n + m + 2)
                nc.scalar.activation(x2[:, m, bass.ds(n * PAIR, PAIR), 1:LX], p_2[m][:, :, :],
                                     ACT.Identity, bias=bo[:, m:m + 1]).then_inc(x2_ready, 1)

        rows_out(0)
        rows_out(1)
        with act.Fori(0, NP_ // 2 - 1) as i:
            for q in range(2):
                body(i, q)
                rows_out(i * 2 + q + 2)
                out(i, q)
        for q in range(2):
            body(NP_ // 2 - 1, q)
            out(NP_ // 2 - 1, q)

    @blk.vector
    def _(dve):
        V = nc.vector
        dve.wait_ge(loaded, 16 * LOADS)
        for k in range(TAPS):
            V.tensor_scalar(wpk[:, k, :], wp[:, 1, :], cnd[:, 1, k:k + 1], None, ALU.mult).then_inc(setup, 1)
        dve.wait_ge(setup, TAPS)
        V.tensor_copy(wpr[0][:, :, :], wpk[:, :, :]).then_inc(setup, 1)
        dve.wait_ge(setup, TAPS + 1)
        V.tensor_tensor(wpr[1][:, :, :], wpk[:, :, :], wpr[0][:, :, :].bitcast(F32), ALU.subtract).then_inc(setup, 1)
        V.memset(decay[:, :], 1.0).then_inc(setup, 1)
        V.tensor_scalar(sp_v[:, :], logs[:, :], 0.0, None, ALU.max).then_inc(setup, 1)
        dve.wait_ge(sp_step, 3)
        dve.wait_ge(setup, TAPS + 4)
        V.tensor_tensor(sp_v[:, :], sp_v[:, :], sp_l[:, :], ALU.add).then_inc(setup, 1)
        dve.wait_ge(setup, TAPS + 5)
        V.tensor_scalar(prod[:, :], sp_v[:, 0:1], sp_v[:, 1:2], -1.0, ALU.mult, ALU.mult).then_inc(setup, 1)
        dve.wait_ge(setup, TAPS + 6)
        V.tensor_scalar(prod[:, :], prod[:, :], 1.0, None, ALU.add).then_inc(setup, 1)
        dve.wait_ge(setup, TAPS + 7)
        V.tensor_scalar(decay[:, :], decay[:, :], prod[:, 0:1], None, ALU.mult).then_inc(setup, 1)
        dve.wait_ge(bias_sum, 1)
        V.tensor_tensor(bias[:, :], p_b, bp[:, :], ALU.add).then_inc(bias_ready, 1)

        def gate(n, j, k):
            return cw[:, bass.ds(n * PAIR + j // 2, 1), k, j % 2]

        def combine(n, q):
            dve.wait_ge(x_rows[q], 16 * (n // 2 + 1) if isinstance(n, int) else n * 8 + 16 - 8 * q)
            for j in range(TILES):
                dve.wait_ge(gathered[j], 32 * n + 32)
                V.scalar_tensor_tensor(half[j][:, :], yk[0][j][:, :], gate(n, j, 0), xr[q][:, j, :], ALU.mult, ALU.add).then_inc(half_ready, 1)
            if not isinstance(n, int) or n:
                dve.wait_ge(x1_turned, PAIR * n)
            for j in range(TILES):
                dve.wait_ge(half_ready, TILES * n + j + 1)
                V.scalar_tensor_tensor(whole[j][:, :], yk[1][j][:, :], gate(n, j, 1), half[j][:, :], ALU.mult, ALU.add).then_inc(whole_ready, 1)

        def convolve(i, q):
            n = 2 * i + q
            dve.wait_ge(x1_out, XO * n + XO)
            for k in range(TAPS):
                a = acc[k % 2]
                if k < 2:
                    if k == 0:
                        V.tensor_scalar(a[0][:, :, :], tap(0, i * 2 + q, k), cnd[:, 0, k:k + 1], cb[:, 0:1], ALU.mult, ALU.add).then_inc(part, 1)
                    else:
                        V.tensor_scalar(a[0][:, :, :], tap(0, i * 2 + q, k), cnd[:, 0, k:k + 1], None, ALU.mult).then_inc(part, 1)
                else:
                    dve.wait_ge(part, TAPS * n + k - 1)
                    V.scalar_tensor_tensor(a[(k // 2) % 2][:, :, :], tap(0, i * 2 + q, k), cnd[:, 0, k:k + 1],
                                           a[1 - (k // 2) % 2][:, :, :], ALU.mult, ALU.add).then_inc(part, 1)
            dve.wait_ge(part, TAPS * n + TAPS)
            r = (TAPS // 2 - 1) % 2
            V.tensor_tensor(conv[q][:, :, :], acc[0][r][:, :, :], acc[1][r][:, :, :], ALU.add).then_inc(conv_ready, 1)

        def step(i, q):
            n = 2 * i + q
            dve.wait_ge(z_ready, n + 1)
            V.tensor_scalar(rz[:, :], zz[q][:, :], 0.0, None, ALU.max).then_inc(relu_ready, 1)
            dve.wait_ge(relu_ready, n + 1)
            dve.wait_ge(ln_ready, n + 1)
            V.tensor_tensor(bt[:, :], rz[:, :], lz[q][:, :], ALU.add).then_inc(b_ready, 1)
            dve.wait_ge(b_ready, n + 1)
            dve.wait_ge(u_ready, n + 1)
            V.scalar_tensor_tensor(d1[:, :], bt[:, :], sp_v[:, 1:2], uu[q][:, :], ALU.mult, ALU.mult).then_inc(d_ready, 1)
            dve.wait_ge(d_ready, n + 1)
            for s in range(PAIR):
                w = slice(s * L, (s + 1) * L)
                last = V.tensor_tensor_scan(st[:, w], decay[:, :], d1[:, w], 0.0, ALU.mult, ALU.add)
            last.then_inc(st_ready, 1)
            dve.wait_ge(st_ready, n + 1)
            dve.wait_ge(ct_ready, n + 1)
            dve.wait_ge(x2_sum, 2 * n + 1)
            V.tensor_tensor(yy[q][:, :], st[:, :], ct[q][:, :], ALU.mult).then_inc(yy_ready, 1)

        V.sem_inc(yy_ready, 2)
        V.sem_inc(x2_sum, 1)
        combine(0, 0)
        dve.wait_ge(padded, KD + 2)
        convolve(0, 0)
        combine(1, 1)
        with dve.Fori(0, NP_ // 2 - 1) as i:
            combine(i * 2 + 2, 0)
            convolve(i, 1)
            step(i, 0)
            combine(i * 2 + 3, 1)
            convolve(i + 1, 0)
            step(i, 1)
        i = NP_ // 2 - 1
        convolve(i, 1)
        step(i, 0)
        step(i, 1)

    @blk.tensor
    def _(pe):
        pe.wait_ge(loaded, 16 * LOADS)
        nc.tensor.matmul(p_b, wp[:, 1, :], cb[:, 1:2], start=True, stop=True).then_inc(bias_sum, 1)
        pe.wait_ge(setup, TAPS + 2)

        def turn(n):
            for s in range(PAIR):
                if not isinstance(n, int) or n:
                    pe.wait_ge(x1_out, XO * (n - 1) + 2 * s + 2)
                for h in range(L // P):
                    j = s * (L // P) + h
                    pe.wait_ge(whole_ready, TILES * n + j + 1)
                    for k in range(KD):
                        last = nc.tensor.transpose(p_x[s][:, k, h * P:(h + 1) * P], whole[j][:, k * P:(k + 1) * P], ident[:, :])
                last.then_inc(x1_turned, 1)

        HALVES = ((0, 0), (0, 1), (1, 0))

        def project(i, q, more=True):
            n = 2 * i + q
            pe.wait_ge(x1_split, n + 1)
            pe.wait_ge(yy_ready, n + 1)
            for k in range(TAPS):
                for a, b in HALVES:
                    nc.tensor.matmul(p_bc[q][:, :], wpr[a][:, k, :], x1r[b][:, bass.ds(n * PAIR, PAIR), k:k + L],
                                     start=(k == 0 and a + b == 0), stop=False)
                if k == 3 and more:
                    turn(n + 1)
            pe.wait_ge(conv_ready, n + 1)
            nc.tensor.matmul(p_bc[q][:, :], wp[:, 0, :], conv[q][:, :, :], start=False, stop=True).then_inc(bc_sum, 1)
            for k in range(KD):
                last = nc.tensor.matmul(p_u[q][:, :], ws[:, k, :], tap(k, n, PAD), start=(k == 0), stop=(k == KD - 1))
            last.then_inc(u_sum, 1)

        def out(i, q):
            n = 2 * i + q
            pe.wait_ge(yy_ready, n + 3)
            pe.wait_ge(x2_ready, 2 * n + 1)
            for m in range(KD):
                nc.tensor.matmul(p_2[m][:, :, :], wo_s[:, m * P:(m + 1) * P], yy[q][:, :], start=True, stop=True).then_inc(x2_sum, 1)

        pe.sem_inc(x2_ready, 1)
        pe.wait_ge(bias_ready, 1)
        turn(0)
        pe.wait_ge(padded, KD + 2)
        project(0, 0, False)
        turn(1)
        with pe.Fori(0, NP_ // 2 - 1) as i:
            project(i, 1)
            out(i, 0)
            project(i + 1, 0)
            out(i, 1)
        i = NP_ // 2 - 1
        project(i, 1, False)
        out(i, 0)
        out(i, 1)


DEPTH = 2
HEADS = 8
DH = 64
INNER = HEADS * DH
WIN = 128
HC = INNER // P
FF = int(D * 4 * 2 / 3)
FK = -(-FF // P)
FSZ = [min(P, FF - c * P) for c in range(FK)]
WINS = L // WIN
NQ = PAIR * WINS
UNITS = PAIR * HEADS
SC = 3 * WIN
QK_SCALE = 8.0
FULL = (FK - 1) * P
G_TAIL = 64
W1_COLS = 2 * FULL + G_TAIL + FF - FULL
W1_PARTS = ((0, 0, FULL), (FULL, FF, FULL), (2 * FULL, FULL, G_TAIL), (2 * FULL + G_TAIL, FF + FULL, FF - FULL))
NEVER = -1e30


def attention_places(nc, ctx, mem):
    sb, over, split = placing(nc, ctx)
    b1 = sb("b1f", [P, DEPTH, 2 * FK - 1]); b2 = sb("b2f", [P, DEPTH, KD]); lgb = sb("lgb", [P, DEPTH, 2, KD])
    tabs = sb("rot_tabs", [P, 2, 2, WINS, DH])
    qks = sb("qk_scales", [P, DEPTH, 2, DH]); mask = sb("mask", [P, SC])
    mem["attention_constants"] = b1, b2, lgb, tabs, qks, mask
    mem["x1_chunk"] = over("x1_chunk", "rot_tabs", [P, PAIR, L])
    mem["hs"] = split("hs", [P, KD, PAIR, LX])


def attention_constants(mem, A):
    b1, b2, lgb, tabs, qks, mask = mem["attention_constants"]
    return ((tabs[:, :, :, :, :], A["rot_tabs"]),
            (qks[:, :, :, :].rearrange("p l w d -> p (l w d)"),
             A["qk_scales"].rearrange("l w d -> (l w d)").unsqueeze(0).broadcast_to([P, DEPTH * 2 * DH])),
            (mask[:, :], A["mask"]), (b1[:, :, :], A["b1f"]), (b2[:, :, :], A["b2f"]), (lgb[:, :, :, :], A["lgb"]))


def x_halves(pool, mem, p, step, ready, n):
    hi, lo, raw = mem["hs"]
    for k in range(KD):
        last = pool.tensor_copy(raw[:, k, :, :], mem["x2"][:, k, bass.ds(p * PAIR, PAIR), :])
    last.then_inc(step, 1)
    pool.wait_ge(step, 2 * n + 1)
    pool.sem_inc(mem["waits_taken"], 1)
    pool.tensor_copy(hi[:, :, :, :], raw[:, :, :, :]).then_inc(step, 1)
    pool.wait_ge(step, 2 * n + 2)
    pool.tensor_tensor(lo[:, :, :, :], raw[:, :, :, :], hi[:, :, :, :].bitcast(F32), ALU.subtract).then_inc(ready, 1)


def transformer(nc, ctx, mem, A):
    sem = lambda n: ctx.enter_context(nc.semaphore(n))
    x2, ident = mem["x2"], mem["ident"]
    sb, over, split = placing(nc, ctx)
    wqkv = split("wqkv", [P, KD, 3 * INNER]); wo = split("wo_a", [P, HC, D])
    w1 = split("w1f", [P, KD, W1_COLS]); w2 = split("w2f", [P, FK, D])
    b1, b2, lgb, tabs, qks, mask = mem["attention_constants"]
    hs = mem["hs"]
    x1_chunk = mem["x1_chunk"]
    b1e = sb("b1e", [P, 2 * FK - 1])
    tab = sb("tab", [P, 2, 2, WINS, DH])
    mean_w = sb("mean_w", [P, P]); eps = sb("eps", [P, 1])
    qk_rows = [sb(f"qk_rows{w}", [P, NQ, INNER]) for w in range(2)]
    qk = [[qk_rows[w][:, t, :] for w in range(2)] for t in range(NQ)]
    oT = [over(f"oT_{h}", f"qk_rows{w}", [P, HC, C2], F32R) for w, h in enumerate(("hi", "lo"))]
    rs = [sb(f"rs{q}", [P, INNER]) for q in range(2)]
    sq = [sb(f"sq{q}", [P, INNER]) for q in range(2)]
    ss = sb("ss", [P, NQ, 2, HEADS]); nrm = sb("nrm", [P, NQ, 2, HEADS]); rn = sb("rn", [P, NQ, 2, HEADS])
    vv = [sb(f"vv{t}", [P, INNER]) for t in range(NQ)]
    qkT = [sb(f"qkT{w}", [P, HC, C2]) for w in range(2)]
    sm = [sb(f"sm{q}", [P, SC]) for q in range(3)]
    mx = sb("mx", [P, 3, 2]); rsum = sb("rsum", [P, 2, UNITS]); rinv = sb("rinv", [P, 2, UNITS])
    pr = [sb(f"pr{q}", [P, SC]) for q in range(3)]
    pT = [sb(f"pT{q}", [P, 3, WIN]) for q in range(2)]
    on = sb("on", [P, NQ, INNER])
    gg = [on[:, q, :] for q in range(2)]
    lnv, rstd, xc = on[:, 0, :], on[:, 1, :], on[:, 2:4, :]
    xn = split("xn", [P, KD, C2])
    sqx = xn[2]
    own = split("hh", [P, FK - 2, C2])
    hh = [[own[h][:, c, :] for c in range(FK - 2)] for h in range(3)]
    for q in range(2):
        hh[0].append(over(f"hh_hi_{q}", f"sq{q}", [P, C2], F32R)[:, :])
        hh[1].append(over(f"hh_lo_{q}", f"rs{q}", [P, C2], F32R)[:, :])
        hh[2].append(rs[q][:, :])
    bank = [ctx.enter_context(nc.psum_tensor(f"bank{q}", [P, 512], F32)) for q in range(8)]
    O_BANKS = [[5, 6], [5, 2]]
    A_BANKS = [7, 3]
    DOWN_BANKS = [7, 6]
    TURN_BANKS = [6, 6, 3, 4]
    TURN_BEATS = {13: 0, 15: 1}

    cst_in, cst_ready = mem["cst_in"], sem("tr_cst_ready")
    wqkv_in, wo_in, w1_in, w2_in = sem("wqkv_in"), sem("wo_in"), sem("tr_w1_in"), sem("tr_w2_in")
    wqkv_ready, wo_ready, w1_ready, w2_ready = sem("wqkv_ready"), sem("wo_ready"), sem("w1_ready"), sem("w2_ready")
    hs_step, xn_step, rn_step = mem["hs_step"], sem("xn_step"), sem("rn_step")
    oT_hi, hh_hi, hh_raw = sem("oT_hi"), sem("hh_hi"), sem("hh_raw")
    tab_ready, b1_sum, b1_ready = sem("tab_ready"), sem("b1_sum"), sem("b1_ready")
    hs_ready, qkv_done, sq_ready, rot_ready = mem["hs_ready"], sem("qkv_done"), sem("sq_ready"), sem("rot_ready")
    ss_ready, nrm_ready, rn_ready = sem("ss_ready"), sem("nrm_ready"), sem("rn_ready")
    added, normed, v_ready = sem("added"), sem("normed"), sem("v_ready")
    qk_turned, qkT_ready = sem("qk_turned"), sem("qkT_ready")
    waits_taken = mem["waits_taken"]
    s_done, sm_ready, probs_ready, pt_done, pt_out, pv_done = (sem(n) for n in ("s_done", "sm_ready", "probs_ready", "pt_done", "pt_out", "pv_done"))
    rinv_ready, on_ready, o_turned, oT_ready, wo_done, xmid_ready = (sem(n) for n in ("rinv_ready", "on_ready", "o_turned", "oT_ready", "wo_done", "xmid_ready"))
    mean_done, xc_ready, sqx_ready, var_done, lnv_ready, rstd_ready, xn_ready = (sem(n) for n in ("mean_done", "xc_ready", "sqx_ready", "var_done", "lnv_ready", "rstd_ready", "xn_ready"))
    g_done, a_done, g_ready, hh_ready, w2_done, x_done = (sem(n) for n in ("g_done", "a_done", "g_ready", "hh_ready", "w2_done", "x_done"))

    x1_in, x1_added, stored = sem("x1_in"), sem("x1_added"), sem("stored")

    def wait(e, s, v):
        if not isinstance(v, int) or v > 0:
            e.wait_ge(s, v)

    def x_mid(m, p, shifted=0):
        return x2[:, m, bass.ds(p * PAIR, PAIR), 1 - shifted:LX - shifted]

    pair = lambda a: a.rearrange("p (s t) -> p s t", s=PAIR)
    heads = lambda a: a.rearrange("p (h d) -> p h d", h=HEADS)
    QB = lambda m: m % 5

    def turns(e, body):
        body(0, (0, 0), None)
        for l in range(DEPTH):
            with e.Fori(1, NP_) as j:
                body(j + l * NP_, (l, j), (l, j - 1))
            body((l + 1) * NP_, (l + 1, 0) if l + 1 < DEPTH else None, (l, NP_ - 1))

    HALVES = ((0, 0), (0, 1), (1, 0))

    def split_weights(e, v, w, loaded, n_loaded, ready, l):
        parts = [(P, slice(0, w[0].shape[1]))]
        if w is w2:
            parts = [(P, slice(0, FK - 1)), (FSZ[-1], slice(FK - 1, FK))]
        e.wait_ge(loaded, n_loaded)
        for rows, c in parts:
            v.tensor_copy(w[0][0:rows, c, :], w[2][0:rows, c, :]).then_inc(ready, 1)
        e.wait_ge(ready, (2 * l + 1) * len(parts))
        for rows, c in parts:
            v.tensor_tensor(w[1][0:rows, c, :], w[2][0:rows, c, :], w[0][0:rows, c, :].bitcast(F32), ALU.subtract).then_inc(ready, 1)

    blk = ctx.enter_context(nc.Block())

    @blk.sync
    def _(sp):
        def load_wqkv(l):
            sp.dma_start(wqkv[2][:, :, :], A["L1_ffn_wqkv"][l].rearrange("(k p) n -> p k n", p=P)).then_inc(wqkv_in, 16)

        def load_wo(l):
            sp.dma_start(wo[2][:, :, :], A["L1_ffn_wo"][l].rearrange("(k p) n -> p k n", p=P)).then_inc(wo_in, 16)

        def load_w1(l):
            src = A["L1_ffn_w1"][l].rearrange("(k p) n -> p k n", p=P)
            for to, frm, size in W1_PARTS:
                sp.dma_start(w1[2][:, :, to:to + size], src[:, :, frm:frm + size]).then_inc(w1_in, 16)

        def load_w2(l):
            full = (FK - 1) * P
            sp.dma_start(w2[2][:, 0:FK - 1, :], A["L1_ffn_w2"][l][0:full].rearrange("(k p) n -> p k n", p=P)).then_inc(w2_in, 16)
            sp.dma_start(w2[2][0:FF - full, FK - 1, :], A["L1_ffn_w2"][l][full:FF]).then_inc(w2_in, 16)

        load_wqkv(0)
        load_wo(0)
        load_w1(0)
        load_w2(0)
        sp.wait_ge(qkv_done, 12 * NP_)
        load_wqkv(1)
        sp.wait_ge(wo_done, 2 * NP_)
        load_wo(1)
        sp.wait_ge(a_done, (FK - 1) * NP_)
        sp.wait_ge(g_done, FK * NP_)
        sp.wait_ge(b1_sum, 1)
        load_w1(1)
        sp.wait_ge(w2_done, 2 * NP_ + 1)
        load_w2(1)

        def load_x1(p, k):
            sp.dma_start(x1_chunk[:, :, :], mem["x1_dram"][k][:, bass.ds(p * PAIR, PAIR), :]).then_inc(x1_in, 16)

        def store(p):
            for k in range(KD):
                sp.wait_ge(x_done, 2 * (NP_ + p) + k + 2)
                sp.dma_start(A["outT"][k][:, bass.ds(p * PAIR, PAIR), :], x_mid(k, p)).then_inc(stored, 16)

        sp.wait_ge(tab_ready, DEPTH)
        load_x1(0, 0)
        sp.wait_ge(x1_added, 1)
        load_x1(0, 1)
        with sp.Fori(1, NP_) as p:
            sp.wait_ge(x1_added, 2 * p)
            load_x1(p, 0)
            store(p - 1)
            sp.wait_ge(x1_added, 2 * p + 1)
            load_x1(p, 1)
        store(NP_ - 1)
        sp.wait_ge(stored, 16 * KD * NP_)

    @blk.gpsimd
    def _(pool):
        pool.memset(mean_w[:, :], 1.0 / D).then_inc(cst_ready, 1)
        pool.memset(eps[:, :], 1e-5).then_inc(cst_ready, 1)

        def add_x1(n, p):
            pool.wait_ge(xc_ready, 2 * n)
            for k in range(KD):
                pool.wait_ge(x1_in, 16 * (2 * p + k + 1))
                nc.gpsimd.tensor_tensor(x_mid(k, p), x_mid(k, p), x1_chunk[:, :, :], ALU.add).then_inc(x1_added, 1)

        def body(n, att, ffn):
            if att is None:
                add_x1(n, ffn[1])
                return
            l, p = att
            wait(pool, qkv_done, 12 * n)
            if l and isinstance(n, int):
                split_weights(pool, nc.gpsimd, wqkv, wqkv_in, 32, wqkv_ready, 1)
            if l:
                wait(pool, x_done, 2 * (n - NP_ + 1) + 1)
            if not isinstance(n, int) or n:
                x_halves(nc.gpsimd, mem, p, hs_step, hs_ready, n)
            for m in range(2 * NQ):
                pool.wait_ge(rot_ready, 8 * n + m + 1)
                t = qk[m // 2][m % 2]
                nc.gpsimd.tensor_tensor(t, t, rs[m % 2][:, :], ALU.add).then_inc(added, 1)
            pool.wait_ge(rn_ready, n + 1)
            for m in range(2 * NQ):
                pool.wait_ge(added, 8 * n + m + 1)
                t = qk[m // 2][m % 2]
                nc.gpsimd.tensor_tensor(heads(t), heads(t), rn[:, m // 2, m % 2, :].unsqueeze(2).broadcast_to([P, HEADS, DH]), ALU.mult).then_inc(normed, 1)
            if ffn is not None and ffn[0] == DEPTH - 1:
                add_x1(n, ffn[1])
            if isinstance(n, int):
                split_weights(pool, nc.gpsimd, wo, wo_in, 16 * (l + 1), wo_ready, l)
                split_weights(pool, nc.gpsimd, w1, w1_in, 16 * len(W1_PARTS) * (l + 1), w1_ready, l)

        turns(pool, body)

    @blk.tensor
    def _(pe):
        mm, tr = nc.tensor.matmul, nc.tensor.transpose

        def qkv_products(n, ffn):
            pe.wait_ge(hs_ready, n + 1)
            for m in range(3 * NQ):
                if m == 2 and ffn is not None:
                    variance(n - 1)
                t, w = divmod(m, 3)
                if m < 5:
                    wait(pe, *[(xmid_ready, 2 * n), (xmid_ready, 2 * n), (on_ready, 4 * n), (xc_ready, 2 * n), (lnv_ready, n)][m])
                else:
                    t0, w0 = divmod(m - 5, 3)
                    if w0 == 2:
                        pe.wait_ge(v_ready, NQ * n + t0 + 1)
                    else:
                        pe.wait_ge(rot_ready, 8 * n + 2 * t0 + w0 + 1)
                s, win = divmod(t, WINS)
                for k in range(KD):
                    for a, b in HALVES:
                        tok = hs[a][:, k, s, 1 - k + win * WIN:1 - k + (win + 1) * WIN]
                        last = mm(bank[QB(m)][:, :], tok, wqkv[b][:, k, w * INNER:(w + 1) * INNER],
                                  start=(k == 0 and a + b == 0), stop=(k == KD - 1 and a == 1))
                last.then_inc(qkv_done, 1)

        def ffn_up(f, attends):
            pe.wait_ge(xn_ready, f + 1)
            for c in range(FK):
                for half in (1, 0):
                    if half:
                        if c == 0:
                            pe.wait_ge(on_ready, 4 * f + 4)
                        elif c == 1:
                            pe.wait_ge(x_done, 2 * f + 1)
                        else:
                            pe.wait_ge(g_ready, FK * f + c - 1)
                    elif c == FK - 1:
                        continue
                    else:
                        if c == 0:
                            pe.wait_ge(x_done, 2 * f + 1)
                        elif c == 1:
                            if attends:
                                pe.wait_ge(v_ready, NQ * (f + 1) + 3)
                        else:
                            pe.wait_ge(hh_raw, FK * f + c)
                    o, size = half * FULL + c * P, P
                    if c == FK - 1:
                        o, size = 2 * FULL, W1_COLS - 2 * FULL
                    out = bank[5 + c % 2 if half else A_BANKS[c % 2]][0:size, :]
                    for k in range(KD):
                        for a, b in HALVES:
                            last = mm(out, w1[a][:, k, o:o + size], xn[b][:, k, :], start=(k == 0 and a + b == 0), stop=(k == KD - 1 and a == 1))
                    last.then_inc(g_done if half else a_done, 1)

        def ffn_down(f, m, c0, c1, attends=True):
            if c0 == 0:
                pe.wait_ge(hh_ready, FK * f + FK + 1)
                if m == 1:
                    pe.wait_ge(oT_ready, 4 * f + 4 + 2) if attends else pe.wait_ge(g_ready, FK * f + FK)
            for c in range(c0, c1):
                for a, b in HALVES:
                    last = mm(bank[DOWN_BANKS[m]][:, :], w2[a][0:FSZ[c], c, m * P:(m + 1) * P], hh[b][c][0:FSZ[c], :],
                              start=(c == 0 and a + b == 0), stop=(c == FK - 1 and a == 1))
            if c1 == FK:
                last.then_inc(w2_done, 1)

        def turn_qk(n, ffn):
            pe.wait_ge(rot_ready, 8 * n + 8)
            pe.wait_ge(v_ready, NQ * n + NQ)
            for m in range(2 * NQ):
                pe.wait_ge(normed, 8 * n + m + 1)
                if m == 2 and ffn is not None:
                    pe.wait_ge(hh_raw, FK * n + 1)
                if m >= 4:
                    pe.wait_ge(qkT_ready, 8 * n + m - 3)
                for c in range(HC):
                    last = tr(bank[1 + m % 4][:, c * P:(c + 1) * P], qk[m // 2][m % 2][:, c * P:(c + 1) * P], ident[:, :])
                last.then_inc(qk_turned, 1)

        def scores(n, u):
            s, h = divmod(u, HEADS)
            if u >= 2:
                pe.wait_ge(sm_ready, UNITS * n + u - 1)
            r = slice(DH * (h % 2), DH * (h % 2) + DH)
            q, k = qkT[0][r, h // 2, :], qkT[1][r, h // 2, :]
            b = s * L
            mm(bank[u % 2][:, 0:WIN], q[:, b:b + WIN], k[:, b:b + WIN], start=True, stop=True)
            mm(bank[u % 2][:, WIN:SC], q[:, b + WIN:b + L], k[:, b:b + L], start=True, stop=True).then_inc(s_done, 1)

        def turn_probs(n, u):
            pe.wait_ge(probs_ready, UNITS * n + u + 1)
            if u >= 2:
                pe.wait_ge(pt_out, UNITS * n + u - 1)
            for c in range(3):
                last = tr(bank[3 + u % 2][:, c * P:(c + 1) * P], pr[u % 3][:, c * P:(c + 1) * P], ident[:, :])
            last.then_inc(pt_done, 1)

        def values(n, u):
            s, h = divmod(u, HEADS)
            pe.wait_ge(pt_out, UNITS * n + u + 1)
            if u == 0:
                wait(pe, g_ready, FK * n)
            if u == HEADS:
                pe.wait_ge(on_ready, 4 * n + 1)
            hd = slice(h * DH, (h + 1) * DH)
            t = pT[u % 2]
            mm(bank[O_BANKS[s][0]][:, hd], t[:, 0, :], vv[2 * s][:, hd], start=True, stop=True)
            mm(bank[O_BANKS[s][1]][:, hd], t[:, 1, :], vv[2 * s][:, hd], start=True, stop=False)
            mm(bank[O_BANKS[s][1]][:, hd], t[:, 2, :], vv[2 * s + 1][:, hd], start=False, stop=True).then_inc(pv_done, 1)

        def turn_o(n, q):
            pe.wait_ge(on_ready, 4 * n + q + 1)
            if q == 0:
                pe.wait_ge(on_ready, 4 * n + 2)
            elif q == 1:
                pe.wait_ge(oT_ready, 4 * n + 1)
            else:
                pe.wait_ge(pt_out, UNITS * n + UNITS)
            for c in range(HC):
                last = tr(bank[TURN_BANKS[q]][:, c * P:(c + 1) * P], on[:, q, c * P:(c + 1) * P], ident[:, :])
            last.then_inc(o_turned, 1)

        def project(n, s):
            pe.wait_ge(oT_ready, 4 * n + 2 * s + 2)
            pe.wait_ge(sm_ready, UNITS * n + UNITS)
            cols = slice(s * L, (s + 1) * L)
            for m in range(KD):
                for c in range(HC):
                    for a, b in HALVES:
                        last = mm(bank[m][:, cols], wo[a][:, c, m * P:(m + 1) * P], oT[b][:, c, cols],
                                  start=(c == 0 and a + b == 0), stop=(c == HC - 1 and a == 1))
                if s:
                    last.then_inc(wo_done, 1)

        def mean(n, p):
            pe.wait_ge(xmid_ready, 2 * n + 2)
            for k in range(KD):
                last = mm(pair(bank[3][:, :]), mean_w[:, :], x_mid(k, p, k), start=(k == 0), stop=(k == KD - 1))
            last.then_inc(mean_done, 1)

        def variance(n):
            pe.wait_ge(sqx_ready, n + 1)
            for k in range(KD):
                last = mm(bank[4][:, :], mean_w[:, :], sqx[:, k, :], start=(k == 0), stop=(k == KD - 1))
            last.then_inc(var_done, 1)

        FIRST = 2
        FILL = [[2, 5, 8, 11], [18]]

        def body(n, att, ffn):
            f = n - 1
            if att is not None:
                if isinstance(n, int):
                    pe.wait_ge(wqkv_ready, 2 * (att[0] + 1))
                qkv_products(n, ffn)
            else:
                variance(f)
            if ffn is not None:
                ffn_up(f, att is not None)
            if att is not None:
                turn_qk(n, ffn)
                if ffn is not None:
                    ffn_down(f, 0, 0, FIRST)
                pe.wait_ge(qkT_ready, 8 * n + 8)
                for b in range(UNITS + 3):
                    if b < UNITS:
                        scores(n, b)
                    if ffn is not None:
                        for m in range(KD):
                            if b in FILL[m]:
                                c = FILL[m].index(b) + (0 if m else FIRST)
                                ffn_down(f, m, c, c + 1)
                    if 2 <= b < UNITS + 2:
                        turn_probs(n, b - 2)
                    if b >= 3:
                        values(n, b - 3)
                    if b in TURN_BEATS:
                        turn_o(n, TURN_BEATS[b])
            elif ffn is not None:
                ffn_down(f, 0, 0, FK, False)
            if att is not None:
                if isinstance(n, int):
                    pe.wait_ge(wo_ready, 2 * (att[0] + 1))
                project(n, 0)
                turn_o(n, 2)
                turn_o(n, 3)
                if ffn is not None:
                    ffn_down(f, 1, len(FILL[1]), FK - 1)
                project(n, 1)
                if ffn is not None:
                    ffn_down(f, 1, FK - 1, FK)
                mean(n, att[1])
            else:
                ffn_down(f, 1, 0, FK, False)
            if att is not None and isinstance(n, int):
                pe.wait_ge(w1_ready, 2 * (att[0] + 1))
                if n:
                    pe.wait_ge(x_done, 2 * f + 2)
                for j in range(2 * FK - 1):
                    o = j * P
                    size = min(P, W1_COLS - o)
                    for k in range(KD):
                        for a in range(2):
                            last = mm(bank[7][0:size, j:j + 1], w1[a][:, k, o:o + size].bitcast(F32), lgb[:, att[0], 1, k:k + 1],
                                      start=(k + a == 0), stop=(k + a == KD))
                last.then_inc(b1_sum, 1)

        pe.wait_ge(cst_ready, 2)
        pe.wait_ge(cst_in, 96)
        pe.sem_inc(w2_done, 1)
        turns(pe, body)

    @blk.scalar
    def _(act):
        S = nc.scalar.activation

        def norm_values(n):
            act.wait_ge(var_done, n + 1)
            S(lnv, bank[4][:, :], ACT.Ln, bias=eps[:, :]).then_inc(lnv_ready, 1)
            act.wait_ge(lnv_ready, n + 1)
            S(rstd, lnv, ACT.Exp, scale=-0.5).then_inc(rstd_ready, 1)

        def gelus(f, c0, c1):
            for c in range(c0, c1):
                act.wait_ge(g_done, FK * f + c + 1)
                act.wait_ge(hh_raw, FK * f + max(c - 1, 0) + 1)
                g0 = G_TAIL if c == FK - 1 else 0
                rows, col = slice(g0, g0 + FSZ[c]), min(FK - 1 + c, 2 * FK - 2)
                S(gg[c % 2][0:FSZ[c], :], bank[5 + c % 2][rows, :], ACT.Gelu, bias=b1e[rows, col:col + 1]).then_inc(g_ready, 1)

        def turned_hi(n, q):
            act.wait_ge(o_turned, 4 * n + q + 1)
            S(oT[0][:, :, q * WIN:(q + 1) * WIN], bank[TURN_BANKS[q]][:, :].rearrange("p (c t) -> p c t", c=HC), ACT.Copy).then_inc(oT_hi, 1)

        def body(n, att, ffn):
            f = n - 1
            if att is not None:
                wait(act, pv_done, UNITS * n)
                for t in range(NQ):
                    for w in range(2):
                        m = 2 * t + w
                        act.wait_ge(qkv_done, 12 * n + 3 * t + w + 1)
                        wait(act, ss_ready, 8 * n + m - 1)
                        S(sq[m % 2][:, :], bank[QB(3 * t + w)][:, :], ACT.Square).then_inc(sq_ready, 1)
                    if t == 0 and ffn is not None:
                        norm_values(f)
                    act.wait_ge(qkv_done, 12 * n + 3 * t + 3)
                    S(vv[t][:, :], bank[QB(3 * t + 2)][:, :], ACT.Copy).then_inc(v_ready, 1)
            else:
                norm_values(f)
            if ffn is not None:
                act.wait_ge(b1_ready, ffn[0] + 1)
                gelus(f, 0, 2)
            if att is not None:
                act.wait_ge(ss_ready, 8 * n + 8)
                S(nrm[:, :, :, :], ss[:, :, :, :], ACT.Sqrt).then_inc(nrm_ready, 1)
            if ffn is not None:
                gelus(f, 2, FK)
            if att is None:
                return
            wait(act, s_done, UNITS * n)
            for m in range(2 * NQ):
                act.wait_ge(qk_turned, 8 * n + m + 1)
                S(qkT[m % 2][:, :, (m // 2) * WIN:(m // 2 + 1) * WIN], bank[1 + m % 4][:, :].rearrange("p (c t) -> p c t", c=HC),
                  ACT.Copy).then_inc(qkT_ready, 1)
            wait(act, on_ready, 4 * n)
            for u in range(UNITS):
                act.wait_ge(sm_ready, UNITS * n + u + 1)
                wait(act, pt_done, UNITS * n + u - 2)
                r = u % 3
                S(pr[r][:, 0:WIN], sm[r][:, 0:WIN], ACT.Exp, scale=-1.0, bias=mx[:, r, 0:1], accum_out=rsum[:, 0, u:u + 1])
                S(pr[r][:, WIN:SC], sm[r][:, WIN:SC], ACT.Exp, scale=-1.0, bias=mx[:, r, 1:2], accum_out=rsum[:, 1, u:u + 1]).then_inc(probs_ready, 1)
                if u in TURN_BEATS:
                    turned_hi(n, TURN_BEATS[u])
            for q in range(2, NQ):
                turned_hi(n, q)
            act.wait_ge(xc_ready, 2 * n + 2)
            S(sqx[:, :, :], xc, ACT.Square).then_inc(sqx_ready, 1)

        act.wait_ge(cst_ready, 2)
        turns(act, body)

    @blk.vector
    def _(dve):
        V = nc.vector

        def tables(l):
            H = DH // 2
            for w in range(2):
                ql = lambda a, b: qks[:, l, w, a:b].unsqueeze(1).broadcast_to([P, WINS, b - a])
                V.tensor_tensor(tab[:, w, 0, :, :], tabs[:, w, 0, :, :], ql(0, DH), ALU.mult)
                V.tensor_tensor(tab[:, w, 1, :, 0:H], tabs[:, w, 1, :, 0:H], ql(H, DH), ALU.mult)
                last = V.tensor_tensor(tab[:, w, 1, :, H:DH], tabs[:, w, 1, :, H:DH], ql(0, H), ALU.mult)
            last.then_inc(tab_ready, 1)
            dve.wait_ge(tab_ready, l + 1)

        def rotate(n, m):
            t, w = divmod(m, 2)
            win = t % WINS
            H = DH // 2
            src = heads(bank[QB(3 * t + w)][:, :])
            dve.wait_ge(sq_ready, 8 * n + m + 1)
            c = lambda a, b, i: tab[:, w, i, win, a:b].unsqueeze(1).broadcast_to([P, HEADS, b - a])
            V.tensor_tensor(heads(qk[t][w]), src, c(0, DH, 0), ALU.mult)
            wait(dve, added, 8 * n + m - 1)
            o = heads(rs[m % 2][:, :])
            V.tensor_tensor(o[:, :, 0:H], src[:, :, H:DH], c(0, H, 1), ALU.mult)
            V.tensor_tensor(o[:, :, H:DH], src[:, :, 0:H], c(H, DH, 1), ALU.mult).then_inc(rot_ready, 1)
            V.tensor_reduce(ss[:, t, w, :], heads(sq[m % 2][:, :]), AX.X, ALU.add).then_inc(ss_ready, 1)

        def norms(n):
            fl = lambda a: a.rearrange("p t w h -> p (t w h)")
            dve.wait_ge(nrm_ready, n + 1)
            V.tensor_scalar(nrm[:, :, :, :], nrm[:, :, :, :], 1e-12, None, ALU.max).then_inc(rn_step, 1)
            dve.wait_ge(rn_step, 2 * n + 1)
            wait(dve, normed, 8 * n)
            V.reciprocal(fl(rn[:, :, :, :]), fl(nrm[:, :, :, :])).then_inc(rn_step, 1)
            dve.wait_ge(rn_step, 2 * n + 2)
            V.tensor_scalar(rn[:, :, 0, :], rn[:, :, 0, :], QK_SCALE, None, ALU.mult).then_inc(rn_ready, 1)

        def gate(f, c):
            if c == 0:
                dve.wait_ge(w2_done, 2 * f + 1)
            dve.wait_ge(g_ready, FK * f + c + 1)
            last = c == FK - 1
            if not last:
                dve.wait_ge(a_done, (FK - 1) * f + c + 1)
            a_rows = bank[5 + c % 2 if last else A_BANKS[c % 2]][0:FSZ[c], :]
            col = 2 * FK - 2 if last else c
            hi, lo, raw = (h[c][0:FSZ[c], :] for h in hh)
            V.scalar_tensor_tensor(raw, a_rows, b1e[0:FSZ[c], col:col + 1], gg[c % 2][0:FSZ[c], :],
                                   ALU.add, ALU.mult).then_inc(hh_raw, 1)
            dve.wait_ge(hh_raw, FK * f + c + 2)
            V.tensor_copy(hi, raw).then_inc(hh_hi, 1)
            dve.wait_ge(hh_hi, FK * f + c + 1)
            V.tensor_tensor(lo, raw, hi.bitcast(F32), ALU.subtract).then_inc(hh_ready, 1)

        def mask_scores(n, u):
            dve.wait_ge(s_done, UNITS * n + u + 1)
            wait(dve, probs_ready, UNITS * n + u - 2)
            dve.sem_inc(waits_taken, 1)
            r = u % 3
            for w, (a, b) in enumerate(((0, WIN), (WIN, SC))):
                last = V.tensor_tensor_reduce(out=sm[r][:, a:b], in0=bank[u % 2][:, a:b], in1=mask[:, a:b], scale=-1.0, scalar=3e38,
                                              op0=ALU.add, op1=ALU.min, accum_out=mx[:, r, w:w + 1])
            last.then_inc(sm_ready, 1)

        def probs_out(n, u):
            dve.wait_ge(pt_done, UNITS * n + u + 1)
            wait(dve, pv_done, UNITS * n + u - 1)
            V.tensor_copy(pT[u % 2][:, :, :], bank[3 + u % 2][:, 0:SC].rearrange("p (c t) -> p c t", c=3)).then_inc(pt_out, 1)

        def normalise(n, s, w):
            us = slice(s * HEADS, (s + 1) * HEADS)
            if w == 0:
                dve.wait_ge(pv_done, UNITS * n + (s + 1) * HEADS)
                if s == 0:
                    wait(dve, o_turned, 4 * n)
                V.reciprocal(rinv[:, :, us], rsum[:, :, us]).then_inc(rinv_ready, 1)
                dve.wait_ge(rinv_ready, 2 * n + s + 1)
            V.tensor_tensor(heads(on[:, 2 * s + w, :]), heads(bank[O_BANKS[s][w]][:, :]),
                            rinv[:, w, us].unsqueeze(2).broadcast_to([P, HEADS, DH]), ALU.mult).then_inc(on_ready, 1)

        def result_lo(n, q):
            dve.wait_ge(oT_hi, 4 * n + q + 1)
            cols = slice(q * WIN, (q + 1) * WIN)
            V.tensor_tensor(oT[1][:, :, cols], bank[TURN_BANKS[q]][:, :].rearrange("p (c t) -> p c t", c=HC), oT[0][:, :, cols].bitcast(F32),
                            ALU.subtract).then_inc(oT_ready, 1)

        def residual(n, p):
            for m in range(KD):
                dve.wait_ge(wo_done, 2 * n + m + 1)
                V.tensor_tensor(x_mid(m, p), pair(bank[m][:, :]), x_mid(m, p), ALU.add).then_inc(xmid_ready, 1)

        def centre(n, p):
            dve.wait_ge(mean_done, n + 1)
            dve.wait_ge(xmid_ready, 2 * n + 2)
            for k in range(KD):
                V.tensor_tensor(pair(xc[:, k, :]), x_mid(k, p, k), pair(bank[3][:, :]), ALU.subtract).then_inc(xc_ready, 1)

        def scale(n, l):
            dve.wait_ge(rstd_ready, n + 1)
            hi, lo, raw = xn
            for k in range(KD):
                V.scalar_tensor_tensor(raw[:, k, :], xc[:, k, :], lgb[:, l, 0, k:k + 1], rstd, ALU.mult, ALU.mult).then_inc(xn_step, 1)
            dve.wait_ge(xn_step, 3 * n + 2)
            V.tensor_copy(hi[:, :, :], raw[:, :, :]).then_inc(xn_step, 1)
            dve.wait_ge(xn_step, 3 * n + 3)
            V.tensor_tensor(lo[:, :, :], raw[:, :, :], hi[:, :, :].bitcast(F32), ALU.subtract).then_inc(xn_ready, 1)

        def finish(f, l, p, m):
            dve.wait_ge(w2_done, 2 * f + m + 2)
            if l == DEPTH - 1:
                dve.wait_ge(x1_added, 2 * p + m + 1)
            V.scalar_tensor_tensor(x_mid(m, p), pair(bank[DOWN_BANKS[m]][:, :]), b2[:, l, m:m + 1], x_mid(m, p), ALU.add, ALU.add).then_inc(x_done, 1)

        def body(n, att, ffn):
            f = n - 1
            if att is not None:
                if isinstance(n, int):
                    tables(att[0])
                wait(dve, qk_turned, 8 * n)
                for m in range(2 * NQ):
                    rotate(n, m)
                    if ffn is not None and m == 3:
                        scale(f, ffn[0])
                    if ffn is not None and m == 2 * NQ - 1:
                        gate(f, 0)
                if ffn is not None:
                    gate(f, 1)
                norms(n)
            else:
                scale(f, ffn[0])
            if ffn is not None:
                for c in range(2 if att is not None else 0, FK):
                    if c == FK - 2 and att is not None:
                        dve.wait_ge(added, 8 * n + 8)
                    gate(f, c)
            if att is not None:
                for b in range(UNITS + 2):
                    if b == HEADS + 3:
                        normalise(n, 0, 0)
                    if b < UNITS:
                        mask_scores(n, b)
                    if b >= 2:
                        probs_out(n, b - 2)
                    if b == HEADS + 3:
                        normalise(n, 0, 1)
                    if b - 1 in TURN_BEATS:
                        result_lo(n, TURN_BEATS[b - 1])
                for w in range(WINS):
                    normalise(n, 1, w)
                for q in range(2, NQ):
                    result_lo(n, q)
            if ffn is not None:
                finish(f, ffn[0], ffn[1], 0)
            if att is not None:
                residual(n, att[1])
                centre(n, att[1])
            if ffn is not None:
                finish(f, ffn[0], ffn[1], 1)
            if att is not None and isinstance(n, int):
                dve.wait_ge(b1_sum, att[0] + 1)
                n_full, size = 2 * FK - 2, W1_COLS - 2 * FULL
                V.tensor_tensor(b1e[:, 0:n_full], bank[7][:, 0:n_full], b1[:, att[0], 0:n_full], ALU.add)
                V.tensor_tensor(b1e[0:size, n_full:n_full + 1], bank[7][0:size, n_full:n_full + 1], b1[0:size, att[0], n_full:n_full + 1],
                                ALU.add).then_inc(b1_ready, 1)
                dve.wait_ge(b1_ready, att[0] + 1)
                split_weights(dve, V, w2, w2_in, 32 * (att[0] + 1), w2_ready, att[0])

        dve.wait_ge(cst_in, 96)
        split_weights(dve, V, wqkv, wqkv_in, 16, wqkv_ready, 0)
        for s in (x_done, hh_ready, hh_raw):
            dve.sem_inc(s, 1)
        turns(dve, body)


def build(nc, A, out):
    A["outT"] = out
    with ExitStack() as ctx:
        mem = {}

        def keep(c, name, shape, dt=F32):
            mem[name] = c.enter_context(nc.sbuf_tensor(name, shape, dt))

        keep(ctx, "ident", [P, P])
        keep(ctx, "x2", [P, KD, B, LX])
        attention_places(nc, ctx, mem)
        mem["slots"] = nc.dram_tensor("slots", (NSLOTS, D), F32, kind="Internal").ap()
        mem["ydram"] = nc.dram_tensor("expert_rows", (NSLOTS, D), F32, kind="Internal").ap()
        mem["x1_dram"] = nc.dram_tensor("x1_kept", (KD, P, B, L), F32, kind="Internal").ap()
        mem["n_slots"] = NSLOTS
        mem["get_dram"] = nc.dram_tensor("slots_by_token", (P, B, TOP, L // P), U32, kind="Internal").ap()
        mem["cw_dram"] = nc.dram_tensor("gates_by_token", (P, B, TOP, L // P), F32, kind="Internal").ap()
        mem["zero_ready"] = ctx.enter_context(nc.semaphore("zero_ready"))
        for name in ("route_loaded", "scan_loaded", "cst_in", "hs_step", "hs_ready", "waits_taken"):
            mem[name] = ctx.enter_context(nc.semaphore(name))
        mem["zeroed"] = ctx.enter_context(nc.semaphore("slots_zeroed"))
        with ExitStack() as c0:
            keep(c0, "cw", [P, P // TT, TOP, L // P])
            keep(c0, "put", [P, TOP, NT], U32)
            keep(c0, "get", [P, P // TT, TOP, L // P], U32)
            keep(c0, "cw_seq", [P, B, TOP, L // P])
            keep(c0, "get_seq", [P, B, TOP, L // P], U32)
            with ExitStack() as c1:
                keep(c1, "rows", [P, NT, D])
                keep(c1, "wg", [P, KD, E])
                mem["p_lg"] = c1.enter_context(nc.psum_tensor("p_lg", [P, NT, E], F32))
                with ExitStack() as c2:
                    keep(c2, "xt", [P, KD, T])
                    keep(c2, "zero", [P, 8 * D])
                    gated_recurrence(nc, c2, mem, A)
                with ExitStack() as c2:
                    route(nc, c2, mem, A)
            mem["scan_loads"] = scan_constants(nc, c0, mem, A)
            with ExitStack() as c1:
                experts(nc, c1, mem, A)
            with ExitStack() as c1:
                keep(c1, "x1", [P, KD, B, LP])
                combine_and_scan(nc, c1, mem, A)
        with ExitStack() as c1:
            transformer(nc, c1, mem, A)



def shape_constants():
    f = np.float32
    half = np.arange(0, DH, 2, dtype=f)
    inv = (f(1) / f(10000) ** (half / f(DH))).astype(f)
    t = np.arange(L, dtype=f)
    fr = t[:, None] * inv[None]
    base = (half + f(0.4 * DH)) / f(1.4 * DH)
    sc = base[None] ** ((t - L // 2) / f(WIN // 2))[:, None]
    cos, sin = np.cos(fr), np.sin(fr)
    cat = lambda a, b: np.concatenate([a, b], 1)
    tabs = np.stack([np.stack([cat(cos * sc, cos * sc), cat(-sin * sc, sin * sc)]),
                     np.stack([cat(cos / sc, cos / sc), cat(-sin / sc, sin / sc)])])
    tabs = tabs.reshape(2, 2, WINS, WIN, DH).transpose(3, 0, 1, 2, 4).astype(f)
    i, j = np.arange(WIN)[:, None], np.arange(WIN)[None]
    own, before = np.where(j <= i, 0, NEVER), np.where(j >= i, 0, NEVER)
    mask = np.concatenate([own, before, own], 1).astype(f)
    bb, tt = np.arange(P) % B, np.arange(P) // B
    same = bb[:, None] == bb[None]
    routes = np.stack([bb[:, None] < bb[None], np.ones((P, P), bool), same]).astype(f)
    routes = np.concatenate([routes, ((same & (tt[:, None] < tt[None])).astype(f) - same.astype(f))[None]])
    keepcol = np.ones((E * TOP, NT), f)
    keepcol[0::TOP, 0] = 0
    keepcol[1::TOP, 0] = 0
    return {
        "rot_tabs": tabs, "mask": mask, "ident": np.eye(P, dtype=f), "route_masks": routes.transpose(1, 0, 2),
        "iota": np.broadcast_to(np.tile(np.arange(E, dtype=f), NT), (P, NT * E)),
        "keepcol": np.broadcast_to(keepcol.ravel(), (P, E * TOP * NT)),
    }


def layouts(x, cond_1024, L0_ffn_Wg, L0_ffn_b1, L1_cond_conv_b, L1_cond_bp, L1_cond_bs, L1_cond_A_log, L1_cond_dt_log, L1_cond_bo,
            L1_ffn_q_scale, L1_ffn_k_scale, L1_ffn_ln_g, L1_ffn_ln_b, L1_ffn_b1, L1_ffn_b2, **whole):
    cols = lambda a: a.reshape(KD, P).T
    b1 = np.zeros((DEPTH, (2 * FK - 1) * P), np.float32)
    for to, frm, size in W1_PARTS:
        b1[:, to:to + size] = L1_ffn_b1[:, frm:frm + size]
    return {
        "xT_tb": x.transpose(2, 1, 0).reshape(D, T), "x_rows": x.reshape(T, D), "condT": cond_1024.T,
        "WgT": L0_ffn_Wg.T, "b1T": L0_ffn_b1.reshape(E, KH, P).transpose(2, 0, 1).reshape(P, E * KH),
        "conv_bT": cols(L1_cond_conv_b), "bpT": L1_cond_bp[:, None], "bsT": L1_cond_bs[:, None], "boT": cols(L1_cond_bo),
        "A_logT": L1_cond_A_log[:, None], "dt_logT": L1_cond_dt_log[:, None],
        "qk_scales": np.stack([L1_ffn_q_scale, L1_ffn_k_scale], 1), "b1f": b1.reshape(DEPTH, 2 * FK - 1, P).transpose(2, 0, 1),
        "b2f": L1_ffn_b2.reshape(DEPTH, KD, P).transpose(2, 0, 1),
        "lgb": np.stack([L1_ffn_ln_g, L1_ffn_ln_b], 1).reshape(DEPTH, 2, KD, P).transpose(3, 0, 1, 2),
        **whole,
    }


def kernel(**inputs):
    import concourse.bacc as _bacc
    from concourse.bass_utils import run_bass_kernel_spmd as _run

    nc = _bacc.Bacc("TRN2", target_bir_lowering=False, num_devices=1)
    given = {**layouts(**{k: np.asarray(v) for k, v in inputs.items()}), **shape_constants()}
    arrays, A = {}, {}
    for name, a in given.items():
        arrays[f"in_{name}"] = np.ascontiguousarray(a)
        A[name] = nc.dram_tensor(f"in_{name}", a.shape, mybir.dt.from_np(a.dtype), kind="ExternalInput").ap()
    out = nc.dram_tensor("out_features", (KD, P, B, L), F32, kind="ExternalOutput").ap()
    build(nc, A, out)
    r = _run(nc, [arrays], core_ids=[0])
    got = r.results[0]["out_features"]
    return np.ascontiguousarray(got.reshape(D, B, L).transpose(1, 2, 0))
```
